# Optimizing a Trainium2 kernel written in Bass

```python
import numpy as np
import jax
import jax.numpy as jnp

def _softmax(x, axis=-1):
    return jax.nn.softmax(x, axis=axis)

def _gelu(x):
    return jax.nn.gelu(x, approximate=True)

def _silu(x):
    return jax.nn.silu(x)

def _sigmoid(x):
    return jax.nn.sigmoid(x)

def _layernorm(x, axis=-1, eps=1e-05):
    m = jnp.mean(x, axis=axis, keepdims=True)
    v = jnp.var(x, axis=axis, keepdims=True)
    return (x - m) / jnp.sqrt(v + eps)

def _scatter_add(tgt, idx, src, axis=0):
    return tgt.at[idx].add(src)

def _segment_sum(src, seg, n):
    return jax.ops.segment_sum(src, seg, n)
kernel_name = 'mk_decoder_preln_d2_seqx_r8_595d64'

def setup_inputs(seed: int=0):
    np.random.seed(seed)
    _w = jnp.asarray

    def _rec_inputs():
        import jax
        import jax.numpy as jnp
        _rk = jax.random.key(seed)
        x = -0.0003929 + 0.9999 * jax.random.normal(jax.random.fold_in(_rk, 1), (8, 128, 256), jnp.float32)
        _lenS = 128 - jax.random.randint(jax.random.fold_in(_rk, 7), (8,), 0, max(1, 128 // 4) + 1, jnp.int32)
        _lenS2 = 128 - jax.random.randint(jax.random.fold_in(_rk, 8), (8,), 0, max(1, 128 // 4) + 1, jnp.int32)
        _ctx_2048P = jax.random.normal(jax.random.fold_in(_rk, 11), (8, 16, 256), jnp.float32)
        _ctx_2048c = jax.random.dirichlet(jax.random.fold_in(_rk, 511), 0.3 * jnp.ones((16,), jnp.float32), (8, 128))
        _ctx_2048t = jnp.einsum('bsk,bkd->bsd', _ctx_2048c, _ctx_2048P)
        _ctx_2048t = _ctx_2048t * jax.lax.rsqrt(jnp.mean(jnp.square(_ctx_2048t)) + 1e-12) * 0.953939
        ctx_2048 = -0.000514642 + 1.00011 * (_ctx_2048t + 0.3 * jax.random.normal(jax.random.fold_in(_rk, 611), (8, 128, 256), jnp.float32))
        return (x, ctx_2048)
    x, ctx_2048 = _rec_inputs()

    def _L0_attn_setup():
        import jax, jax.numpy as jnp
        import numpy as np
        B, S, H, R, L = (4, 256, 256, 256, 256)
        W_SCALE = 0.02

        def _reference_tuple_inner(x, w_f, w_i, w_v, w_q, w_ro, w_aux, w_up, w_gate, w_down, init_state):
            b, s, _ = x.shape
            f = jnp.tanh(jnp.einsum('bsh,hr->bsr', x, w_f))
            g = jax.nn.sigmoid(jnp.einsum('bsh,hr->bsr', x, w_i)) * jax.nn.silu(jnp.einsum('bsh,hr->bsr', x, w_v))

            def step(state, fg):
                ft, gt = fg
                state = ft * state + gt
                return (state, state)
            s0 = jnp.broadcast_to(init_state, (b, init_state.shape[0]))
            _, states = jax.lax.scan(step, s0, (jnp.swapaxes(f, 0, 1), jnp.swapaxes(g, 0, 1)))
            states = jnp.swapaxes(states, 0, 1)
            q = jnp.einsum('bsh,hr->bsr', x, w_q)
            readout = jax.nn.silu(q * states)
            local = jnp.einsum('bsl,lh->bsh', jnp.einsum('bsh,hl->bsl', x, w_up) * jax.nn.silu(jnp.einsum('bsh,hl->bsl', x, w_gate)), w_down)
            out = jnp.einsum('bsr,rh->bsh', readout, w_ro) + local
            aux_pred = jnp.einsum('bsr,rh->bsh', jax.nn.silu(states[:, :-1]), w_aux)
            aux_target = jax.lax.stop_gradient(x[:, 1:])
            aux_loss = jnp.mean((aux_pred - aux_target) ** 2)
            return (out, aux_loss)
        key = jax.random.key(seed)
        ks = jax.random.split(key, 11)
        w = lambda k, shp: jax.random.normal(k, shp, jnp.float32) * W_SCALE
        return {'x': jax.random.normal(ks[0], (B, S, H), jnp.float32), 'w_f': w(ks[1], (H, R)), 'w_i': w(ks[2], (H, R)), 'w_v': w(ks[3], (H, R)), 'w_q': w(ks[4], (H, R)), 'w_ro': w(ks[5], (R, H)), 'w_aux': w(ks[6], (R, H)), 'w_up': w(ks[7], (H, L)), 'w_gate': w(ks[8], (H, L)), 'w_down': w(ks[9], (L, H)), 'init_state': jnp.zeros((R,), jnp.float32)}
    _L0_attn_all = _L0_attn_setup()
    _L0_attn_in = {k: v for k, v in _L0_attn_all.items() if k in ('w_f', 'w_i', 'w_v', 'w_q', 'w_ro', 'w_aux', 'w_up', 'w_gate', 'w_down', 'init_state')}
    del _L0_attn_all

    def _L0_xattn_setup():
        import jax, jax.numpy as jnp
        import numpy as np
        NUM_HEADS = 16

        def _qdq(x):
            s = jnp.maximum(jnp.max(jnp.abs(x), axis=-1, keepdims=True) / 127.0, 1e-08)
            return jnp.clip(jnp.round(x / s), -127.0, 127.0) * s
        key = jax.random.key(seed)
        ks = jax.random.split(key, 8)
        B, N, M, D = (2, 512, 64, 256)
        w_std = 0.02
        return {'x': jax.random.normal(ks[0], (B, N, D), jnp.float32), 'cond': jax.random.normal(ks[1], (B, M, D), jnp.float32), 'wq': jax.random.normal(ks[2], (D, D), jnp.float32) * w_std, 'bq': jax.random.normal(ks[3], (D,), jnp.float32) * w_std, 'wkv': jax.random.normal(ks[4], (2 * D, D), jnp.float32) * w_std, 'bkv': jax.random.normal(ks[5], (2 * D,), jnp.float32) * w_std, 'wp': jax.random.normal(ks[6], (D, D), jnp.float32) * w_std, 'bp': jax.random.normal(ks[7], (D,), jnp.float32) * w_std}
    _L0_xattn_all = _L0_xattn_setup()
    _L0_xattn_in = {k: v for k, v in _L0_xattn_all.items() if k in ('wq', 'bq', 'wkv', 'bkv', 'wp', 'bp')}
    del _L0_xattn_all

    def _L0_ffn_setup():
        import jax, jax.numpy as jnp
        import numpy as np
        E = 32
        G = 8
        TKG = 4
        K = 4
        D = 256
        H = 128
        HS = 512
        SCALE = 2.5
        CAP = 128

        def relu2(x):
            r = jnp.maximum(x, 0.0)
            return r * r

        def route_tokens(scores, bias_corr):
            T = scores.shape[0]
            scores_c = scores + bias_corr
            group_scores = jax.lax.top_k(scores_c.reshape(T, G, E // G), 2)[0].sum(-1)
            _, group_idx = jax.lax.top_k(group_scores, TKG)
            group_mask = jnp.zeros((T, G), scores.dtype).at[jnp.arange(T)[:, None], group_idx].set(1.0)
            score_mask = jnp.repeat(group_mask, E // G, axis=1)
            masked = jnp.where(score_mask > 0, scores_c, 0.0)
            _, topk_idx = jax.lax.top_k(masked, K)
            topk_w = jnp.take_along_axis(scores, topk_idx, axis=1)
            topk_w = topk_w / (topk_w.sum(-1, keepdims=True) + 1e-20)
            return (topk_idx, topk_w * SCALE)
        key = jax.random.key(seed)
        ks = jax.random.split(key, 6)
        B, S = (2, 256)
        return dict(hidden_states=jax.random.normal(ks[0], (B, S, D), jnp.float32), gate_w=jax.random.normal(ks[1], (E, D), jnp.float32) * 0.02, bias_corr=jnp.zeros((E,), jnp.float32), up_w=jax.random.normal(ks[2], (E, H, D), jnp.float32) * 0.02, down_w=jax.random.normal(ks[3], (E, D, H), jnp.float32) * 0.02, shared_up_w=jax.random.normal(ks[4], (HS, D), jnp.float32) * 0.02, shared_down_w=jax.random.normal(ks[5], (D, HS), jnp.float32) * 0.02)
    _L0_ffn_all = _L0_ffn_setup()
    _L0_ffn_in = {k: v for k, v in _L0_ffn_all.items() if k in ('gate_w', 'bias_corr', 'up_w', 'down_w', 'shared_up_w', 'shared_down_w')}
    del _L0_ffn_all

    def _L1_attn_setup():
        import jax, jax.numpy as jnp
        import numpy as np
        HIDDEN = 256
        N_HEADS = 16
        N_KV = 8
        HEAD_DIM = HIDDEN // N_HEADS
        GROUPS = N_HEADS // N_KV
        N_LAYERS = 28
        key = jax.random.key(seed)
        k0, k1, k2, k3, k4 = jax.random.split(key, 5)
        std = HIDDEN ** (-0.5)
        o_std = (2 * N_LAYERS) ** (-0.5)
        hidden_states = jax.random.normal(k0, (1, 256, HIDDEN), dtype=jnp.float32)
        wq = jax.random.normal(k1, (N_HEADS * HEAD_DIM, HIDDEN), dtype=jnp.float32) * std
        wk = jax.random.normal(k2, (N_KV * HEAD_DIM, HIDDEN), dtype=jnp.float32) * std
        wv = jax.random.normal(k3, (N_KV * HEAD_DIM, HIDDEN), dtype=jnp.float32) * std
        wo = jax.random.normal(k4, (HIDDEN, HIDDEN), dtype=jnp.float32) * o_std
        return {'hidden_states': hidden_states, 'wq': wq, 'wk': wk, 'wv': wv, 'wo': wo}
    _L1_attn_all = _L1_attn_setup()
    _L1_attn_in = {k: v for k, v in _L1_attn_all.items() if k in ('wq', 'wk', 'wv', 'wo')}
    del _L1_attn_all

    def _L1_xattn_setup():
        import jax, jax.numpy as jnp
        import numpy as np
        B_DIM, T_DIM, C_DIM = (16, 128, 256)

        def _wkv(w, u, k, v):
            Bn, Tn, Cn = k.shape
            NEG_INF = jnp.float32(-1e+38)

            def step(carry, kv_t):
                p, q, o = carry
                kt, vt = kv_t
                no = jnp.maximum(o, u + kt)
                A = jnp.exp(o - no)
                E = jnp.exp(u + kt - no)
                y = (A * p + E * vt) / (A * q + E)
                no2 = jnp.maximum(w + o, kt)
                A2 = jnp.exp(w + o - no2)
                E2 = jnp.exp(kt - no2)
                return ((A2 * p + E2 * vt, A2 * q + E2, no2), y)
            init = (jnp.zeros((Bn, Cn), k.dtype), jnp.zeros((Bn, Cn), k.dtype), jnp.full((Bn, Cn), NEG_INF, k.dtype))
            kT = jnp.moveaxis(k, 1, 0)
            vT = jnp.moveaxis(v, 1, 0)
            _, yT = jax.lax.scan(step, init, (kT, vT))
            return jnp.moveaxis(yT, 0, 1)
        key = jax.random.key(seed)
        k1, k2, k3, k4 = jax.random.split(key, 4)
        w = -jnp.exp(jax.random.normal(k1, (C_DIM,), jnp.float32))
        u = jax.random.normal(k2, (C_DIM,), jnp.float32)
        k = jax.random.normal(k3, (B_DIM, T_DIM, C_DIM), jnp.float32)
        v = jax.random.normal(k4, (B_DIM, T_DIM, C_DIM), jnp.float32)
        return {'B': B_DIM, 'T': T_DIM, 'C': C_DIM, 'w': w, 'u': u, 'k': k, 'v': v}
    _L1_xattn_all = _L1_xattn_setup()
    _L1_xattn_in = {k: v for k, v in _L1_xattn_all.items() if k in ('w', 'u')}
    del _L1_xattn_all

    def _L1_ffn_setup():
        import jax, jax.numpy as jnp
        import numpy as np
        EPS = 1e-07

        def per_token_quant_int8(x, eps=EPS):
            absmax = jnp.max(jnp.abs(x), axis=-1, keepdims=True)
            scale = jnp.maximum(absmax, eps) / 127.0
            q = jnp.clip(jnp.round(x / scale), -128, 127).astype(jnp.int8)
            return (q, scale)
        key = jax.random.key(seed)
        k1, k2, k3, k4 = jax.random.split(key, 4)
        B, S, IN, OUT = (4, 512, 256, 256)
        x = jax.random.normal(k1, (B, S, IN), dtype=jnp.float32)
        weight = jax.random.randint(k2, (OUT, IN), -127, 128, dtype=jnp.int32).astype(jnp.int8)
        w_scale = jax.random.uniform(k3, (OUT, 1), dtype=jnp.float32) * 0.01 + 0.0001
        bias = jax.random.normal(k4, (OUT,), dtype=jnp.float32)
        return {'x': x, 'weight': weight, 'w_scale': w_scale, 'bias': bias}
    _L1_ffn_all = _L1_ffn_setup()
    _L1_ffn_in = {k: v for k, v in _L1_ffn_all.items() if k in ('weight', 'w_scale', 'bias')}
    del _L1_ffn_all
    return {'x': x, 'ctx_2048': ctx_2048, 'L0_attn_w_f': _L0_attn_in['w_f'], 'L0_attn_w_i': _L0_attn_in['w_i'], 'L0_attn_w_v': _L0_attn_in['w_v'], 'L0_attn_w_q': _L0_attn_in['w_q'], 'L0_attn_w_ro': _L0_attn_in['w_ro'], 'L0_attn_w_aux': _L0_attn_in['w_aux'], 'L0_attn_w_up': _L0_attn_in['w_up'], 'L0_attn_w_gate': _L0_attn_in['w_gate'], 'L0_attn_w_down': _L0_attn_in['w_down'], 'L0_attn_init_state': _L0_attn_in['init_state'], 'L0_xattn_wq': _L0_xattn_in['wq'], 'L0_xattn_bq': _L0_xattn_in['bq'], 'L0_xattn_wkv': _L0_xattn_in['wkv'], 'L0_xattn_bkv': _L0_xattn_in['bkv'], 'L0_xattn_wp': _L0_xattn_in['wp'], 'L0_xattn_bp': _L0_xattn_in['bp'], 'L0_ffn_gate_w': _L0_ffn_in['gate_w'], 'L0_ffn_bias_corr': _L0_ffn_in['bias_corr'], 'L0_ffn_up_w': _L0_ffn_in['up_w'], 'L0_ffn_down_w': _L0_ffn_in['down_w'], 'L0_ffn_shared_up_w': _L0_ffn_in['shared_up_w'], 'L0_ffn_shared_down_w': _L0_ffn_in['shared_down_w'], 'L1_attn_wq': _L1_attn_in['wq'], 'L1_attn_wk': _L1_attn_in['wk'], 'L1_attn_wv': _L1_attn_in['wv'], 'L1_attn_wo': _L1_attn_in['wo'], 'L1_xattn_w': _L1_xattn_in['w'], 'L1_xattn_u': _L1_xattn_in['u'], 'L1_ffn_weight': _L1_ffn_in['weight'], 'L1_ffn_w_scale': _L1_ffn_in['w_scale'], 'L1_ffn_bias': _L1_ffn_in['bias']}

def reference(x, ctx_2048, L0_attn_w_f, L0_attn_w_i, L0_attn_w_v, L0_attn_w_q, L0_attn_w_ro, L0_attn_w_aux, L0_attn_w_up, L0_attn_w_gate, L0_attn_w_down, L0_attn_init_state, L0_xattn_wq, L0_xattn_bq, L0_xattn_wkv, L0_xattn_bkv, L0_xattn_wp, L0_xattn_bp, L0_ffn_gate_w, L0_ffn_bias_corr, L0_ffn_up_w, L0_ffn_down_w, L0_ffn_shared_up_w, L0_ffn_shared_down_w, L1_attn_wq, L1_attn_wk, L1_attn_wv, L1_attn_wo, L1_xattn_w, L1_xattn_u, L1_ffn_weight, L1_ffn_w_scale, L1_ffn_bias):
    import jax
    import jax.numpy as jnp

    def _L0_attn_ref(x, w_f, w_i, w_v, w_q, w_ro, w_aux, w_up, w_gate, w_down, init_state):
        import jax, jax.numpy as jnp
        import numpy as np
        B, S, H, R, L = (4, 256, 256, 256, 256)
        W_SCALE = 0.02

        def _reference_tuple_inner(x, w_f, w_i, w_v, w_q, w_ro, w_aux, w_up, w_gate, w_down, init_state):
            b, s, _ = x.shape
            f = jnp.tanh(jnp.einsum('bsh,hr->bsr', x, w_f))
            g = jax.nn.sigmoid(jnp.einsum('bsh,hr->bsr', x, w_i)) * jax.nn.silu(jnp.einsum('bsh,hr->bsr', x, w_v))

            def step(state, fg):
                ft, gt = fg
                state = ft * state + gt
                return (state, state)
            s0 = jnp.broadcast_to(init_state, (b, init_state.shape[0]))
            _, states = jax.lax.scan(step, s0, (jnp.swapaxes(f, 0, 1), jnp.swapaxes(g, 0, 1)))
            states = jnp.swapaxes(states, 0, 1)
            q = jnp.einsum('bsh,hr->bsr', x, w_q)
            readout = jax.nn.silu(q * states)
            local = jnp.einsum('bsl,lh->bsh', jnp.einsum('bsh,hl->bsl', x, w_up) * jax.nn.silu(jnp.einsum('bsh,hl->bsl', x, w_gate)), w_down)
            out = jnp.einsum('bsr,rh->bsh', readout, w_ro) + local
            aux_pred = jnp.einsum('bsr,rh->bsh', jax.nn.silu(states[:, :-1]), w_aux)
            aux_target = jax.lax.stop_gradient(x[:, 1:])
            aux_loss = jnp.mean((aux_pred - aux_target) ** 2)
            return (out, aux_loss)
        return _reference_tuple_inner(x, w_f, w_i, w_v, w_q, w_ro, w_aux, w_up, w_gate, w_down, init_state)[0]

    def _L0_xattn_ref(x, cond, wq, bq, wkv, bkv, wp, bp):
        import jax, jax.numpy as jnp
        import numpy as np
        NUM_HEADS = 16

        def _qdq(x):
            s = jnp.maximum(jnp.max(jnp.abs(x), axis=-1, keepdims=True) / 127.0, 1e-08)
            return jnp.clip(jnp.round(x / s), -127.0, 127.0) * s
        B, N, C = x.shape
        M = cond.shape[1]
        H = NUM_HEADS
        Dh = C // H
        q = _qdq(x) @ _qdq(wq).T + bq
        kv = cond @ wkv.T + bkv
        k, v = jnp.split(kv, 2, axis=-1)
        q = q.reshape(B, N, H, Dh)
        k = k.reshape(B, M, H, Dh)
        v = v.reshape(B, M, H, Dh)
        scale = 1.0 / np.sqrt(Dh)
        attn = jax.nn.softmax(jnp.einsum('bnhd,bmhd->bhnm', q, k) * scale, axis=-1)
        o = jnp.einsum('bhnm,bmhd->bnhd', attn, v).reshape(B, N, C)
        out = _qdq(o) @ _qdq(wp).T + bp
        return out

    def _L0_ffn_ref(hidden_states, gate_w, bias_corr, up_w, down_w, shared_up_w, shared_down_w):
        import jax, jax.numpy as jnp
        import numpy as np
        E = 32
        G = 8
        TKG = 4
        K = 4
        D = 256
        H = 128
        HS = 512
        SCALE = 2.5
        CAP = 128

        def relu2(x):
            r = jnp.maximum(x, 0.0)
            return r * r

        def route_tokens(scores, bias_corr):
            T = scores.shape[0]
            scores_c = scores + bias_corr
            group_scores = jax.lax.top_k(scores_c.reshape(T, G, E // G), 2)[0].sum(-1)
            _, group_idx = jax.lax.top_k(group_scores, TKG)
            group_mask = jnp.zeros((T, G), scores.dtype).at[jnp.arange(T)[:, None], group_idx].set(1.0)
            score_mask = jnp.repeat(group_mask, E // G, axis=1)
            masked = jnp.where(score_mask > 0, scores_c, 0.0)
            _, topk_idx = jax.lax.top_k(masked, K)
            topk_w = jnp.take_along_axis(scores, topk_idx, axis=1)
            topk_w = topk_w / (topk_w.sum(-1, keepdims=True) + 1e-20)
            return (topk_idx, topk_w * SCALE)
        B, S, _ = hidden_states.shape
        T = B * S
        flat = hidden_states.reshape(T, D)
        logits = flat @ gate_w.T
        scores = jax.nn.sigmoid(logits)
        topk_idx, topk_w = route_tokens(scores, bias_corr)
        e_flat = topk_idx.reshape(-1)
        oh = jax.nn.one_hot(e_flat, E, dtype=jnp.int32)
        pos = jnp.take_along_axis(jnp.cumsum(oh, axis=0) - 1, e_flat[:, None], axis=1)[:, 0]
        tok = jnp.repeat(jnp.arange(T), K)
        valid = pos < CAP
        xe = jnp.zeros((E, CAP, D), flat.dtype).at[e_flat, pos].set(flat[tok], mode='drop')
        h = relu2(jnp.einsum('ecd,ehd->ech', xe, up_w))
        ye = jnp.einsum('ech,edh->ecd', h, down_w)
        gathered = ye[e_flat, jnp.minimum(pos, CAP - 1)]
        gathered = jnp.where(valid[:, None], gathered, 0.0) * topk_w.reshape(-1)[:, None]
        routed = gathered.reshape(T, K, D).sum(axis=1).reshape(B, S, D)
        shared = relu2(hidden_states @ shared_up_w.T) @ shared_down_w.T
        return routed + shared

    def _L1_attn_ref(hidden_states, wq, wk, wv, wo):
        import jax, jax.numpy as jnp
        import numpy as np
        HIDDEN = 256
        N_HEADS = 16
        N_KV = 8
        HEAD_DIM = HIDDEN // N_HEADS
        GROUPS = N_HEADS // N_KV
        N_LAYERS = 28
        b, s, _ = hidden_states.shape
        q = hidden_states @ wq.T
        k = hidden_states @ wk.T
        v = hidden_states @ wv.T
        q = q.reshape(b, s, N_HEADS, HEAD_DIM).transpose(0, 2, 1, 3)
        k = k.reshape(b, s, N_KV, HEAD_DIM).transpose(0, 2, 1, 3)
        v = v.reshape(b, s, N_KV, HEAD_DIM).transpose(0, 2, 1, 3)
        k = jnp.repeat(k, GROUPS, axis=1)
        v = jnp.repeat(v, GROUPS, axis=1)
        scale = 1.0 / jnp.sqrt(jnp.float32(HEAD_DIM))
        attn = jnp.einsum('bhqd,bhkd->bhqk', q, k) * scale
        attn = jax.nn.softmax(attn.astype(jnp.float32), axis=-1).astype(q.dtype)
        out = jnp.einsum('bhqk,bhkd->bhqd', attn, v)
        out = out.transpose(0, 2, 1, 3).reshape(b, s, HIDDEN)
        return out @ wo.T

    def _L1_xattn_ref(B, T, C, w, u, k, v):
        import jax, jax.numpy as jnp
        import numpy as np
        B_DIM, T_DIM, C_DIM = (16, 128, 256)

        def _wkv(w, u, k, v):
            Bn, Tn, Cn = k.shape
            NEG_INF = jnp.float32(-1e+38)

            def step(carry, kv_t):
                p, q, o = carry
                kt, vt = kv_t
                no = jnp.maximum(o, u + kt)
                A = jnp.exp(o - no)
                E = jnp.exp(u + kt - no)
                y = (A * p + E * vt) / (A * q + E)
                no2 = jnp.maximum(w + o, kt)
                A2 = jnp.exp(w + o - no2)
                E2 = jnp.exp(kt - no2)
                return ((A2 * p + E2 * vt, A2 * q + E2, no2), y)
            init = (jnp.zeros((Bn, Cn), k.dtype), jnp.zeros((Bn, Cn), k.dtype), jnp.full((Bn, Cn), NEG_INF, k.dtype))
            kT = jnp.moveaxis(k, 1, 0)
            vT = jnp.moveaxis(v, 1, 0)
            _, yT = jax.lax.scan(step, init, (kT, vT))
            return jnp.moveaxis(yT, 0, 1)
        return _wkv(w, u, k, v)

    def _L1_ffn_ref(x, weight, w_scale, bias):
        import jax, jax.numpy as jnp
        import numpy as np
        EPS = 1e-07

        def per_token_quant_int8(x, eps=EPS):
            absmax = jnp.max(jnp.abs(x), axis=-1, keepdims=True)
            scale = jnp.maximum(absmax, eps) / 127.0
            q = jnp.clip(jnp.round(x / scale), -128, 127).astype(jnp.int8)
            return (q, scale)
        q, in_scale = per_token_quant_int8(x)
        acc = jnp.einsum('bsk,nk->bsn', q, weight, preferred_element_type=jnp.int32)
        out = acc.astype(jnp.float32) * in_scale * w_scale[:, 0] + bias
        return out.astype(jnp.float16)
    x = x + _L0_attn_ref(_layernorm(x, axis=-1), L0_attn_w_f, L0_attn_w_i, L0_attn_w_v, L0_attn_w_q, L0_attn_w_ro, L0_attn_w_aux, L0_attn_w_up, L0_attn_w_gate, L0_attn_w_down, L0_attn_init_state)
    x = x + _L0_xattn_ref(_layernorm(x, axis=-1), ctx_2048, L0_xattn_wq, L0_xattn_bq, L0_xattn_wkv, L0_xattn_bkv, L0_xattn_wp, L0_xattn_bp)
    x = x + _L0_ffn_ref(_layernorm(x, axis=-1), L0_ffn_gate_w, L0_ffn_bias_corr, L0_ffn_up_w, L0_ffn_down_w, L0_ffn_shared_up_w, L0_ffn_shared_down_w)
    x = x + _L1_attn_ref(_layernorm(x, axis=-1), L1_attn_wq, L1_attn_wk, L1_attn_wv, L1_attn_wo)
    x = x + _L1_xattn_ref(8, 128, 256, L1_xattn_w, L1_xattn_u, _layernorm(x, axis=-1), ctx_2048)
    x = x + _L1_ffn_ref(_layernorm(x, axis=-1), L1_ffn_weight, L1_ffn_w_scale, L1_ffn_bias)
    return x

_drawn_inputs = setup_inputs


def setup_inputs(seed=0):
    import zlib

    import numpy as np

    out = dict(_drawn_inputs(seed))
    spreads = {'L0_attn_init_state': (0.0, 0.8), 'L0_ffn_bias_corr': (0.0, 0.8)}
    factors = {'L0_attn_w_f': 8.0,
     'L0_attn_w_i': 8.0,
     'L0_attn_w_v': 7.224,
     'L0_attn_w_q': 7.137,
     'L0_attn_w_ro': 7.079,
     'L0_attn_w_up': 3.184,
     'L0_attn_w_gate': 3.224,
     'L0_attn_w_down': 3.142,
     'L0_xattn_wq': 64.0,
     'L0_xattn_bq': 64.0,
     'L0_xattn_bkv': 34.728,
     'L0_xattn_wkv': 5.235,
     'L0_xattn_wp': 5.081,
     'L0_xattn_bp': 8.0,
     'L0_ffn_gate_w': 8.0,
     'L0_ffn_up_w': 8.0,
     'L0_ffn_down_w': 8.0,
     'L0_ffn_shared_up_w': 5.722,
     'L0_ffn_shared_down_w': 5.338,
     'L1_attn_wq': 3.643,
     'L1_attn_wk': 3.67,
     'L1_xattn_w': 4.532,
     'L1_xattn_u': 4.627}
    for name, (base, spread) in spreads.items():
        noise = np.random.default_rng([zlib.crc32(name.encode()), seed]).standard_normal(out[name].shape)
        drawn = base * np.exp(spread * noise) if base else spread * noise
        out[name] = jnp.asarray(drawn.astype(out[name].dtype))
    for name, factor in factors.items():
        out[name] = (out[name] * factor).astype(out[name].dtype)
    return out
```

```python
from contextlib import ExitStack

import numpy as np

import concourse.bass as bass
from concourse import mybir

F32 = mybir.dt.float32
F32R = mybir.dt.float32r
BF16 = mybir.dt.bfloat16
F16 = mybir.dt.float16
U32 = mybir.dt.uint32
I8 = mybir.dt.int8
I32 = mybir.dt.int32
ALU = mybir.AluOpType
ACT = mybir.ActivationFunctionType
AX = mybir.AxisListType

P = 128
BATCH, SEQ, D = 8, 128, 256
KC = D // P
TOK = BATCH * SEQ
PAIRS = BATCH // 2
HEADS, HD = 16, 16
GROUPS = 4
CH = HEADS // GROUPS
VC = HD + 1
EXPERTS, TOPK, CAP, HID = 32, 4, 128, 128
EGROUPS, KEPT_GROUPS = 8, 4
EPG = EXPERTS // EGROUPS
SHARED = 512
SC = SHARED // P
ROUTE_SCALE = 2.5
LN_EPS = 1e-5
ROUND = 12582912.0
NEG_BIG = -1e38
SKIP = 8192.0
ATT_SCALE = HD ** -0.5

L0_MATS = ("w_f", "w_i", "w_v", "w_q", "w_gate", "w_up", "w_ro", "w_down")


def named(**parts):
    return type("Named", (), parts)


def build(nc, t):
    ctx = ExitStack()
    with ctx:
        def sb(name, shape, dt=F32):
            return ctx.enter_context(nc.sbuf_tensor(name, shape, dt))

        def sems(prefix, names):
            return named(**{n: ctx.enter_context(nc.semaphore(f"{prefix}_{n}"))
                                      for n in names.split()})

        def views(buffer):
            at = 0

            def take(shape):
                nonlocal at
                size = int(np.prod(shape[1:]))
                part = buffer[:, at:at + size]
                at += size
                names = "abcd"[:len(shape) - 1]
                if len(names) == 1:
                    return part
                return part.rearrange(f"p ({' '.join(names)}) -> p {' '.join(names)}",
                                      **{n: int(k) for n, k in zip(names, shape[1:])})
            return take

        ident = sb("ident", [P, P])
        identb = sb("identb", [P, P], BF16)
        ones = sb("ones", [P, P])
        onesb = sb("onesb", [P, P], BF16)
        before = sb("before", [P, P], BF16)
        lo_rows = sb("lo_rows", [P, 1])
        pick = sb("pick", [P, CH, P], F32R)
        half_pow = sb("half_pow", [P, BATCH])
        iota_e = sb("iota_e", [P, EXPERTS])
        lower_g = sb("lower_g", [P, EGROUPS, EGROUPS])
        scratch = sb("scratch", [P, 36 * 256])
        w0_flat = sb("w0", [P, KC * len(L0_MATS) * D])
        w0 = w0_flat[:, :].rearrange("p (k m n) -> p k m n", k=KC, m=len(L0_MATS))
        init4 = sb("init4", [P, KC])
        wk0 = sb("wk0", [P, KC, 2 * D])
        wv0 = sb("wv0", [P, KC, D])
        bk0 = sb("bk0", [P, CH])
        rows = sb("rows", [P, 5, D])
        bq, bv, bp, wscale, fbias = (rows[:, i, :] for i in range(5))
        rbias = sb("rbias", [P, EXPERTS])
        wq1 = sb("wq1", [P, KC, 2 * D])
        wk1 = sb("wk1", [P, KC, 2 * D])
        wv1 = sb("wv1", [P, KC, D])
        wo1 = sb("wo1", [P, KC, D])
        gate = sb("gate", [P, KC, EXPERTS])
        sup = sb("sup", [P, KC, SHARED])
        sdown = sb("sdown", [P, SC, D])
        decay = sb("decay", [P, KC])
        bonus = sb("bonus", [P, KC])
        wf8 = sb("wf8", [P, KC, D // 4], I32)
        wfb = sb("wfb", [P, KC, D], BF16)
        ctxT = sb("ctxT", [P, KC, TOK])
        x_sb = sb("x_sb", [P, BATCH, D])

        h3_flat = sb("h3", [P, BATCH * D])
        hT3_flat = sb("hT3", [P, KC * TOK])
        take = views(h3_flat)
        pickf, beforef = take([P, CH, P]), take([P, P])

        qw = take([P, 2, KC, D])
        qw_s = sb("qw_s", [P, 2, KC])
        qw_r = sb("qw_r", [P, 2, KC])
        take = views(hT3_flat)
        qw_i, qw_diag = take([P, 2, KC, D]), take([P, 2 * KC, P])
        qw_b = sb("qw_b", [P, 2, KC, D], BF16)
        qwT = sb("qwT", [P, 2, KC, D], BF16)
        qw_row = sb("qw_row", [P, 2, D])

        bank = [ctx.enter_context(nc.psum_tensor(f"bank{i}", [P, 512], F32)) for i in range(8)]

        ld = sems("ld", "x const w0 kv0 rows qw l1 moe")
        cst = sems("cst", "ident pick small vones wfb")
        qs = sems("qw", "scale i b T row diag evacT evacrow")

        LN = sems("ln", "stats mv ve rstd h")
        ln_st = sb("ln_st", [P, 6 * BATCH, 6])
        ln_mv = sb("ln_mv", [P, 6 * BATCH, 2])
        ln_ve, ln_rstd = sb("ln_ve", [P, 6 * BATCH]), sb("ln_rstd", [P, 6 * BATCH])

        def dve_stats(v, n, b):
            i = n * BATCH + b
            v.bn_stats(ln_st[:, i, :], x_sb[:, b, :]).then_inc(LN.stats, 1)
            v.wait_ge(LN.stats, i + 1)
            v.bn_aggr(ln_mv[:, i, :], ln_st[:, i, :]).then_inc(LN.mv, 1)

        def pool_rstd(g, n, b):
            i = n * BATCH + b
            g.wait_ge(LN.mv, i + 1)
            g.tensor_scalar(ln_ve[:, i:i + 1], ln_mv[:, i, 1:2], LN_EPS, None, ALU.add).then_inc(LN.ve, 1)
            g.wait_ge(LN.ve, i + 1)
            g.tensor_tensor(ln_rstd[:, i:i + 1], ln_ve[:, i:i + 1], half_pow[:, 0:1], ALU.pow).then_inc(LN.rstd, 1)

        def dve_norm(v, n, b, out):
            i = n * BATCH + b
            v.wait_ge(LN.rstd, i + 1)
            v.tensor_scalar(out, x_sb[:, b, :], ln_mv[:, i, 0:1], ln_rstd[:, i:i + 1],
                            ALU.subtract, ALU.mult).then_inc(LN.h, 1)

        def quant_buffers(name):
            return named(am=sb(f"{name}_am", [P, 2 * BATCH]), s=sb(f"{name}_s", [P, 2 * BATCH]),
                                   r=sb(f"{name}_r", [P, 2 * BATCH]), i=sb(f"{name}_i", [P, D]),
                                   q=sb(f"{name}_q", [P, 2, D], BF16),
                                   sem=sems(name, "step q"))

        def dve_quant(v, z, b, src, least, free_q):
            v.tensor_reduce(z.am[:, b:b + 1], src, AX.X, ALU.max, apply_absolute_value=True).then_inc(z.sem.step, 1)
            v.wait_ge(z.sem.step, 4 * b + 1)
            v.tensor_scalar(z.s[:, b:b + 1], z.am[:, b:b + 1], 1.0 / 127.0, least,
                            ALU.mult, ALU.max).then_inc(z.sem.step, 1)
            v.wait_ge(z.sem.step, 4 * b + 2)
            v.reciprocal(z.r[:, b:b + 1], z.s[:, b:b + 1]).then_inc(z.sem.step, 1)
            v.wait_ge(z.sem.step, 4 * b + 3)
            v.tensor_scalar(z.i[:, :], src, z.r[:, b:b + 1], ROUND, ALU.mult, ALU.add).then_inc(z.sem.step, 1)
            v.wait_ge(z.sem.step, 4 * b + 4)
            free_q()
            v.tensor_scalar(z.q[:, b % 2, :], z.i[:, :], -ROUND, None, ALU.add).then_inc(z.sem.q, 1)

        A = sems("a", "hT hTs F I V Q G U tf ti tv tg av b4 fix zero st z tz r gg u2 y res init4")
        take = views(scratch)
        a_h = take([P, 2, 2, D])
        a_hT = take([P, 2, KC, D])
        a_tf, a_ti, a_tv, a_tg, a_av, a_b4, a_st, a_z, a_tz, a_gg = (
            take([P, KC, D]) for _ in range(10))
        a_r = take([P, KC, D])
        a_u2 = take([P, KC, D])
        A_OUT = {"F": 1, "I": 2, "V": 3, "Q": 4, "G": 5, "U": 6}

        def psA(n):
            return bank[n][:, :].rearrange("p (c n) -> p c n", c=KC)

        def pe_a_transpose(pe, p):
            for i in range(2):
                pe.wait_ge(LN.h, 2 * p + i + 1)
            if p >= 1:
                pe.wait_ge(A.hTs, p)
            for i in range(2):
                for c in range(KC):
                    mm = pe.transpose(psA(0)[:, c, i * P:(i + 1) * P],
                                      a_h[:, p % 2, i, c * P:(c + 1) * P], ident[:, :])
            mm.then_inc(A.hT, 1)

        def pe_a_project(pe, p):
            pe.wait_ge(A.hTs, p + 1)
            for name, mat, free in (("F", 0, A.tf), ("I", 1, A.ti), ("V", 2, A.av), ("Q", 3, A.z),
                                    ("G", 4, A.gg), ("U", 5, A.u2)):
                if p >= 1:
                    pe.wait_ge(free, p)
                for c in range(KC):
                    for k in range(KC):
                        mm = pe.matmul(psA(A_OUT[name])[:, c, :], w0[:, k, mat, c * P:(c + 1) * P],
                                       a_hT[:, p % 2, k, :], start=(k == 0), stop=(k == KC - 1))
                mm.then_inc({"F": A.F, "I": A.I, "V": A.V, "Q": A.Q, "G": A.G, "U": A.U}[name], 1)

        def pe_a_down(pe, p):
            if p >= 1:
                pe.wait_ge(A.res, p)
            pe.wait_ge(A.r, p + 1)
            pe.wait_ge(A.u2, p + 1)
            for i in range(2):
                for n, (src, mat) in enumerate(((a_r, 6), (a_u2, 7))):
                    for k in range(KC):
                        mm = pe.matmul(psA(7)[:, i, :], src[:, k, i * P:(i + 1) * P], w0[:, k, mat, :],
                                       start=(n == 0 and k == 0), stop=(n == 1 and k == KC - 1))
            mm.then_inc(A.y, 1)

        def act_a(act, p):
            act.wait_ge(A.hT, p + 1)
            if p >= 2:
                act.wait_ge(A.U, p - 1)
            act.copy(a_hT[:, p % 2], psA(0)).then_inc(A.hTs, 1)
            act.wait_ge(A.F, p + 1)
            if p >= 1:
                act.wait_ge(A.st, p)
            act.activation(a_tf[:], psA(1), ACT.Tanh).then_inc(A.tf, 1)
            act.wait_ge(A.I, p + 1)
            if p >= 1:
                act.wait_ge(A.b4, p)
            act.activation(a_ti[:], psA(2), ACT.Tanh, scale=0.5).then_inc(A.ti, 1)
            act.wait_ge(A.V, p + 1)
            if p >= 1:
                act.wait_ge(A.av, p)
            act.activation(a_tv[:], psA(3), ACT.Tanh, scale=0.5).then_inc(A.tv, 1)
            act.wait_ge(A.z, p + 1)
            if p >= 1:
                act.wait_ge(A.r, p)
            act.activation(a_tz[:], a_z[:], ACT.Tanh, scale=0.5).then_inc(A.tz, 1)
            act.wait_ge(A.G, p + 1)
            if p >= 1:
                act.wait_ge(A.gg, p)
            act.activation(a_tg[:], psA(5), ACT.Tanh, scale=0.5).then_inc(A.tg, 1)

        def dve_a_norm(v, p):
            for i in range(2):
                b = 2 * p + i
                if p >= 2:
                    v.wait_ge(A.hT, p - 1)
                dve_norm(v, 0, b, a_h[:, p % 2, i, :])

        def dve_a(v, p):
            v.wait_ge(A.tv, p + 1)
            v.scalar_tensor_tensor(out=a_av[:], in0=a_tv[:], scalar=1.0, in1=psA(3),
                                   op0=ALU.add, op1=ALU.mult).then_inc(A.av, 1)
            v.wait_ge(A.av, p + 1)
            v.wait_ge(A.ti, p + 1)
            v.scalar_tensor_tensor(out=a_b4[:], in0=a_ti[:], scalar=1.0, in1=a_av[:],
                                   op0=ALU.add, op1=ALU.mult).then_inc(A.b4, 1)
            v.wait_ge(A.b4, p + 1)
            v.wait_ge(A.tf, p + 1)
            for c in range(KC):
                v.scalar_tensor_tensor(out=a_b4[:, c, ::SEQ], in0=a_tf[:, c, ::SEQ], scalar=init4[:, c:c + 1],
                                       in1=a_b4[:, c, ::SEQ], op0=ALU.mult, op1=ALU.add).then_inc(A.fix, 1)
            v.wait_ge(A.fix, KC * (p + 1))
            v.memset(a_tf[:, :, ::SEQ], 0.0).then_inc(A.zero, 1)
            v.wait_ge(A.zero, p + 1)
            v.tensor_tensor_scan(a_st[:].rearrange("p c n -> p (c n)"), a_tf[:].rearrange("p c n -> p (c n)"),
                                 a_b4[:].rearrange("p c n -> p (c n)"), 0.0, ALU.mult, ALU.add).then_inc(A.st, 1)
            v.wait_ge(A.st, p + 1)
            v.wait_ge(A.Q, p + 1)
            if p >= 1:
                v.wait_ge(A.tz, p)
            v.scalar_tensor_tensor(out=a_z[:], in0=psA(4), scalar=0.25, in1=a_st[:],
                                   op0=ALU.mult, op1=ALU.mult).then_inc(A.z, 1)
            v.wait_ge(A.tz, p + 1)
            if p >= 1:
                v.wait_ge(A.y, p)
            v.scalar_tensor_tensor(out=a_r[:], in0=a_tz[:], scalar=1.0, in1=a_z[:],
                                   op0=ALU.add, op1=ALU.mult).then_inc(A.r, 1)
            v.wait_ge(A.tg, p + 1)
            v.scalar_tensor_tensor(out=a_gg[:], in0=a_tg[:], scalar=1.0, in1=psA(5),
                                   op0=ALU.add, op1=ALU.mult).then_inc(A.gg, 1)
            v.wait_ge(A.gg, p + 1)
            v.wait_ge(A.U, p + 1)
            v.tensor_tensor(a_u2[:], a_gg[:], psA(6), ALU.mult).then_inc(A.u2, 1)

        def dve_a_residual(v, p):
            v.wait_ge(A.y, p + 1)
            v.scalar_tensor_tensor(out=x_sb[:, 2 * p:2 * p + 2, :], in0=psA(7), scalar=0.5,
                                   in1=x_sb[:, 2 * p:2 * p + 2, :], op0=ALU.mult, op1=ALU.add).then_inc(A.res, 1)

        att = named(
            qr=sb("t_qr", [P, CH, P], F32R), qd=sb("t_qd", [P, 2, CH, P], F32R),
            kf=sb("t_kf", [P, CH, P]), kr=sb("t_kr", [P, 3, CH, P], F32R), kl=sb("t_kl", [P, 3, CH, P], F32R),
            v1=sb("t_v1", [P, 3, HEADS, VC]), nm=sb("t_nm", [P, HEADS]),
            cc=sb("t_cc", [P, GROUPS, 2, HEADS], F32R), ccT=sb("t_ccT", [P, P], F32R),
            pt=sb("t_pt", [P, 2, CH, P]), rs=sb("t_rs", [P, HEADS]), o=sb("t_o", [P, 2, D]),
            hT=sb("t_hT", [P, 2, KC, P]), hTb=sb("t_hTb", [P, 2, KC, P], BF16),
            oT=sb("t_oT", [P, KC, P]), oTb=sb("t_oTb", [P, KC, P], BF16), h=sb("t_h", [P, 2, D]),
            q1=sb("t_q1", [P, D]), q2=sb("t_q2", [P, 2 * D]), y=sb("t_y", [P, D]))
        ATT_SEMS = ("hTp hT K kf kr kl Vp v1 Qp q1 q2 QT qr qd S nm chi clo ccp ccT E pt O rs o "
                    "oTp oT y yt xb res")

        def bank4(n):
            return bank[n][:, :].rearrange("p (c n) -> p c n", c=CH)

        def o_bank():
            return bank[4][:, 0:HEADS * VC].rearrange("p (h d) -> p h d", h=HEADS)

        def pe_scores(pe, T, b, j):
            g, n = slice(32 * j, 32 * j + 32), GROUPS * b + j
            if j == 0:
                pe.wait_ge(T.qd, b + 1)
                pe.wait_ge(T.kl, b + 1)
                pe.wait_ge(T.kr, b + 1)
            if n >= 2:
                pe.wait_ge(T.nm, n - 1)
            for c in range(CH):
                q = att.qd[g, b % 2, c, :]
                pe.matmul(bank4(j % 2)[:, c, :], q, att.kr[g, b % 3, c, :], start=True, stop=False)
                mm = pe.matmul(bank4(j % 2)[:, c, :], q, att.kl[g, b % 3, c, :], start=False, stop=True)
            mm.then_inc(T.S, 1)

        def pe_scores_t(pe, T, b, j):
            g, n = slice(32 * j, 32 * j + 32), GROUPS * b + j
            if j == 0:
                pe.wait_ge(T.ccT, b + 1)
            if n >= 2:
                pe.wait_ge(T.pt, n - 1)
            out = bank4(2 + j % 2)
            for c in range(CH):
                q = att.qd[g, b % 2, c, :]
                pe.matmul(out[:, c, :], att.kr[g, b % 3, c, :], q, start=True, stop=False)
                pe.matmul(out[:, c, :], att.kl[g, b % 3, c, :], q, start=False, stop=False)
                mm = pe.matmul(out[:, c, :], pick[g, c, :], att.ccT[g, :], start=False, stop=True)
            mm.then_inc(T.E, 1)

        def pe_values(pe, T, b, j):
            n = GROUPS * b + j
            pe.wait_ge(T.pt, n + 1)
            if j == 0:
                pe.wait_ge(T.v1, b + 1)
                if b >= 1:
                    pe.wait_ge(T.o, b)
            for c in range(CH):
                h = GROUPS * c + j
                mm = pe.matmul(o_bank()[:, h, :], att.pt[:, n % 2, c, :], att.v1[:, b % 3, h, :],
                               start=True, stop=True)
            mm.then_inc(T.O, 1)

        def pe_max_t(pe, T, b, bank_free):
            pe.wait_ge(T.clo, b + 1)
            bank_free()
            pe.transpose(bank[7][:, 0:P], att.cc[:].rearrange("p g s h -> p (g s h)").bitcast(F32),
                         ident[:, :]).then_inc(T.ccp, 1)

        def act_exp(act, T, b, j):
            n = GROUPS * b + j
            act.wait_ge(T.E, n + 1)
            if n >= 2:
                act.wait_ge(T.O, n - 1)
            act.activation(att.pt[:, n % 2], bank4(2 + j % 2), ACT.Exp, scale=ATT_SCALE).then_inc(T.pt, 1)

        def act_max_t(act, T, b):
            act.wait_ge(T.ccp, b + 1)
            if b >= 1:
                act.wait_ge(T.E, GROUPS * b)
            act.copy(att.ccT[:, :], bank[7][:, 0:P]).then_inc(T.ccT, 1)

        def act_qr(act, T, b):
            act.wait_ge(T.QT, b + 1)
            if b >= 1:
                act.wait_ge(T.qd, b)
            act.copy(att.qr[:], bank4(5)).then_inc(T.qr, 1)

        def dve_qd(v, T, b):
            v.wait_ge(T.qr, b + 1)
            if b >= 2:
                v.wait_ge(T.E, GROUPS * (b - 1))
            v.scalar_tensor_tensor(out=att.qd[:, b % 2], in0=att.qr[:].bitcast(F32), scalar=lo_rows[:, 0:1],
                                   in1=bank4(5), op0=ALU.mult, op1=ALU.add).then_inc(T.qd, 1)

        def dve_rowmax(v, T, b, j):
            n = GROUPS * b + j
            v.wait_ge(T.S, n + 1)
            if j == 0 and b >= 1:
                v.wait_ge(T.clo, b)
            v.tensor_reduce(att.nm[:, j::GROUPS], bank4(j % 2), AX.X, ALU.max, negate=True).then_inc(T.nm, 1)

        def dve_split_max(v, T, b):
            v.wait_ge(T.nm, GROUPS * (b + 1))
            if b >= 1:
                v.wait_ge(T.ccp, b)
            nm = att.nm[:, :].unsqueeze(1).to_broadcast([P, GROUPS, HEADS])
            v.tensor_copy(att.cc[:, :, 0, :], nm).then_inc(T.chi, 1)
            v.wait_ge(T.chi, b + 1)
            v.tensor_tensor(att.cc[:, :, 1, :], nm, att.cc[:, :, 0, :].bitcast(F32), ALU.subtract).then_inc(T.clo, 1)

        def dve_attended(v, T, b, free):
            v.wait_ge(T.O, GROUPS * (b + 1))
            v.reciprocal(att.rs[:, :], o_bank()[:, :, HD]).then_inc(T.rs, 1)
            v.wait_ge(T.rs, b + 1)
            free()
            v.tensor_tensor(att.o[:, b % 2].rearrange("p (h d) -> p h d", h=HEADS), o_bank()[:, :, 0:HD],
                            att.rs[:, :].unsqueeze(2).to_broadcast([P, HEADS, HD]), ALU.mult).then_inc(T.o, 1)

        T = sems("att", ATT_SEMS)
        zq = quant_buffers("zq")
        zo = quant_buffers("zo")

        def pe_b_step(pe, s):
            P_, S_, E_, O_ = (s if s < BATCH else None, s - 1 if 1 <= s <= BATCH else None,
                              s - 2 if 2 <= s < BATCH + 2 else None, s - 3 if s >= 3 else None)
            if P_ is not None:
                b = P_
                pe.wait_ge(zq.sem.q, b + 1)
                if b >= 1:
                    pe.wait_ge(T.v1, b)
                for k in range(KC):
                    mm = pe.transpose(bank[6][:, 0:P].bitcast(BF16).rearrange("p (k n) -> p k n", k=KC)[:, k, :],
                                      zq.q[:, b % 2, k * P:(k + 1) * P], identb[:, :])
                mm.then_inc(T.hTp, 1)
            for j in range(GROUPS):
                if S_ is not None:
                    pe_scores(pe, T, S_, j)
                if E_ is not None:
                    pe_scores_t(pe, T, E_, j)
                    if j >= 1:
                        pe_values(pe, T, E_, j - 1)
                if j == 0 and P_ is not None:
                    b = P_
                    if b >= 1:
                        pe.wait_ge(T.qd, b)
                    for c in range(CH):
                        for k in range(KC):
                            mm = pe.matmul(bank4(5)[:, c, :], wk0[:, k, c * P:(c + 1) * P],
                                           ctxT[:, k, b * P:(b + 1) * P], start=(k == 0), stop=(k == KC - 1))
                    mm.then_inc(T.K, 1)
                    pe.wait_ge(T.hT, b + 1)
                    if b >= 2:
                        pe.wait_ge(T.ccT, b - 1)
                    for k in range(KC):
                        mm = pe.matmul(bank[7][:, 0:D], att.hTb[:, b % 2, k, :], qwT[:, 0, k, :],
                                       start=(k == 0), stop=(k == KC - 1))
                    mm.then_inc(T.Qp, 1)
                if j == 1:
                    if O_ is not None:
                        b = O_
                        pe.wait_ge(zo.sem.q, b + 1)
                        if P_ is not None:
                            pe.wait_ge(T.q1, P_ + 1)
                        else:
                            pe.wait_ge(T.ccT, min(s - 1, BATCH))
                        for k in range(KC):
                            mm = pe.transpose(bank[7][:, 0:P].bitcast(BF16).rearrange("p (k n) -> p k n", k=KC)[:, k, :],
                                              zo.q[:, b % 2, k * P:(k + 1) * P], identb[:, :])
                        mm.then_inc(T.oTp, 1)
                    if P_ is not None:
                        b = P_
                        pe.wait_ge(T.hT, b + 1)
                        for k in range(KC):
                            mm = pe.matmul(bank[6][:, 0:D], ctxT[:, k, b * P:(b + 1) * P], wv0[:, k, :],
                                           start=(k == 0), stop=(k == KC - 1))
                        mm.then_inc(T.Vp, 1)
                if j == 2 and O_ is not None:
                    pe.wait_ge(T.oT, O_ + 1)
                    for k in range(KC):
                        mm = pe.matmul(bank[7][:, 0:D], att.oTb[:, k, :], qwT[:, 1, k, :],
                                       start=(k == 0), stop=(k == KC - 1))
                    mm.then_inc(T.y, 1)
            if P_ is not None:
                b = P_
                pe.wait_ge(T.q2, b + 1)
                pe.wait_ge(T.kf, b + 1)
                for c in range(CH):
                    mm = pe.transpose(bank4(5)[:, c, :], att.q2[:, c * P:(c + 1) * P], ident[:, :])
                mm.then_inc(T.QT, 1)
            if E_ is not None:
                pe_values(pe, T, E_, GROUPS - 1)
            if S_ is not None:
                def free():
                    if O_ is not None:
                        pe.wait_ge(T.yt, O_ + 1)
                    elif P_ is not None:
                        pe.wait_ge(T.q1, P_ + 1)
                pe_max_t(pe, T, S_, free)

        def act_b_step(act, s):
            if s < BATCH:
                b = s
                act.wait_ge(T.hTp, b + 1)
                if b >= 2:
                    act.wait_ge(T.Qp, b - 1)
                act.copy(att.hTb[:, b % 2], bank[6][:, 0:P].bitcast(BF16).rearrange("p (k n) -> p k n", k=KC))\
                   .then_inc(T.hT, 1)
            for j in range(GROUPS):
                if 2 <= s < BATCH + 2:
                    act_exp(act, T, s - 2, j)
                if j == 0 and s < BATCH:
                    b = s
                    act.wait_ge(T.kf, b + 1)
                    if b >= 3:
                        act.wait_ge(T.E, GROUPS * (b - 2))
                    act.copy(att.kr[:, b % 3], att.kf[:]).then_inc(T.kr, 1)
                if j == 1 and s >= 3:
                    b = s - 3
                    act.wait_ge(T.oTp, b + 1)
                    if b >= 1:
                        act.wait_ge(T.y, b)
                    act.copy(att.oTb[:], bank[7][:, 0:P].bitcast(BF16).rearrange("p (k n) -> p k n", k=KC))\
                       .then_inc(T.oT, 1)
            if s < BATCH:
                act_qr(act, T, s)
            if 1 <= s <= BATCH:
                act_max_t(act, T, s - 1)

        def dve_b_prep(v, b):
            if b % 2 == 0:
                v.wait_ge(A.res, b // 2 + 1)
            dve_stats(v, 1, b)
            dve_norm(v, 1, b, att.h[:, b % 2, :])
            v.wait_ge(LN.h, 1 * BATCH + b + 1)

            def free():
                if b >= 2:
                    v.wait_ge(T.hTp, b - 1)
            dve_quant(v, zq, b, att.h[:, b % 2, :], 1e-8, free)

        def dve_b_step(v, s):
            P_, S_, O_ = (s if s < BATCH else None, s - 1 if 1 <= s <= BATCH else None, s - 3 if s >= 3 else None)
            if O_ is not None:
                b = O_
                dve_attended(v, T, b, lambda: None)
                v.wait_ge(T.o, b + 1)

                def free():
                    if b >= 2:
                        v.wait_ge(T.oTp, b - 1)
                dve_quant(v, zo, b, att.o[:, b % 2], 1e-8, free)
            for j in range(GROUPS):
                if S_ is not None:
                    dve_rowmax(v, T, S_, j)
                if P_ is not None and j == 0:
                    b = P_
                    v.wait_ge(T.K, b + 1)
                    if b >= 1:
                        v.wait_ge(T.kl, b)
                    v.tensor_tensor(att.kf[:], bank4(5), bk0[:, :].unsqueeze(2).to_broadcast([P, CH, P]),
                                    ALU.add).then_inc(T.kf, 1)
                    v.wait_ge(T.Qp, b + 1)
                    if b >= 1:
                        v.wait_ge(T.q2, b)
                    v.scalar_tensor_tensor(out=att.q1[:], in0=bank[7][:, 0:D], scalar=zq.s[:, b:b + 1],
                                           in1=qw_row[:, 0, :], op0=ALU.mult, op1=ALU.mult).then_inc(T.q1, 1)
                if P_ is not None and j == 1:
                    b = P_
                    v.wait_ge(T.Vp, b + 1)
                    if b >= 3:
                        v.wait_ge(T.O, GROUPS * (b - 2))
                    v.tensor_tensor(att.v1[:, b % 3, :, 0:HD], bank[6][:, 0:D].rearrange("p (h d) -> p h d", h=HEADS),
                                    bv.rearrange("p (h d) -> p h d", h=HEADS), ALU.add).then_inc(T.v1, 1)
                if O_ is not None and j == 2:
                    b = O_
                    v.wait_ge(T.y, b + 1)
                    if b >= 1:
                        v.wait_ge(T.res, b)
                    v.scalar_tensor_tensor(out=att.y[:], in0=bank[7][:, 0:D], scalar=zo.s[:, b:b + 1],
                                           in1=qw_row[:, 1, :], op0=ALU.mult, op1=ALU.mult).then_inc(T.yt, 1)
                    v.wait_ge(T.yt, b + 1)
                    v.wait_ge(T.xb, b + 1)
                    v.tensor_tensor(x_sb[:, b, :], x_sb[:, b, :], att.y[:], ALU.add).then_inc(T.res, 1)
            if S_ is not None:
                dve_split_max(v, T, S_)
            if P_ is not None:
                dve_qd(v, T, P_)
            if s + 1 < BATCH:
                dve_b_prep(v, s + 1)

        def pool_b_step(g, s):
            if s < BATCH:
                b = s
                g.wait_ge(LN.h, 1 * BATCH + b + 1)
                g.tensor_tensor(x_sb[:, b, :], x_sb[:, b, :], bp, ALU.add).then_inc(T.xb, 1)
                g.wait_ge(T.kr, b + 1)
                if b >= 3:
                    g.wait_ge(T.E, GROUPS * (b - 2))
                g.tensor_tensor(att.kl[:, b % 3], att.kf[:], att.kr[:, b % 3].bitcast(F32), ALU.subtract)\
                 .then_inc(T.kl, 1)
                g.wait_ge(T.q1, b + 1)
                if b >= 1:
                    g.wait_ge(T.QT, b)
                twice = lambda a: a.rearrange("p (h d) -> p h d", h=HEADS).unsqueeze(2).to_broadcast([P, HEADS, 2, HD])
                g.tensor_tensor(att.q2[:].rearrange("p (h s d) -> p h s d", h=HEADS, s=2), twice(att.q1[:]), twice(bq),
                                ALU.add).then_inc(T.q2, 1)
            if s + 1 < BATCH:
                pool_rstd(g, 1, s + 1)

        C = sems("c", "hTp hT lg ex route top idx sel pos srow grow zeroed scat sup_ rel sq sdn shy "
                      "xT xTs up hr h2 dn ye acc "
                      "in0 in1 in2 in3 out0 out1 out2 out3 gat0 gat1")
        h3 = views(h3_flat)([P, BATCH, D])
        hT3 = views(hT3_flat)([P, KC, TOK])
        BE = [P, BATCH, EXPERTS]
        BKE = [P, BATCH * TOPK, EXPERTS]
        take = views(scratch)
        c_ex, c_sg, c_sc, c_ms, c_ms0 = (take(BE) for _ in range(5))
        c_mx, c_mn = (take([P, BATCH * EGROUPS, 2]) for _ in range(2))
        c_hi, c_lo, c_m3, c_sec, c_gs, c_rk, c_mk = (
            take([P, BATCH * EGROUPS]) for _ in range(7))
        c_gt, c_eq, c_eql, c_rk1 = (take([P, BATCH * EGROUPS, EGROUPS]) for _ in range(4))
        c_top = sb("c_top", [P, BATCH, 8])
        c_idx = sb("c_idx", [P, BATCH, 8], U32)
        c_idxf = sb("c_idxf", [P, BATCH, TOPK])
        c_oh = take(BKE)
        c_tmp, c_tmp2 = take(BKE), take(BKE)
        c_sel = sb("c_sel", BE, BF16)
        c_w4, c_p4, c_ok, c_wv, c_drop, c_row = (sb(f"c_{n}", [P, BATCH, TOPK]) for n in "w4 p4 ok wv drop row".split())
        c_pc = sb("c_pc", [P, BATCH, TOPK])
        c_ws, c_wr = sb("c_ws", [P, BATCH]), sb("c_wr", [P, BATCH])
        c_srow, c_grow = sb("c_srow", [P, BATCH, TOPK], U32), sb("c_grow", [P, BATCH, TOPK], U32)
        RING = 4
        e_xT, e_y = take([P, 2, KC, P]), take([P, RING, D])
        e_r, e_h = take([P, 2, P]), take([P, 2, P])
        e_x = sb("e_x", [P, RING, D])
        e_w = sb("e_w", [P, RING, 2 * D])
        e_in, e_out = (C.in0, C.in1, C.in2, C.in3), (C.out0, C.out1, C.out2, C.out3)
        gat = (C.gat0, C.gat1)
        zrow = sb("zrow", [P, 1024])
        take = views(w0_flat)
        c_sr, c_sT = take([P, SC, 512]), take([P, SC, 512])
        g_y = views(w0_flat)([P, 2, TOPK, D])
        xe_dram = nc.dram_tensor("xe_dram", [EXPERTS * CAP, D], F32).ap()
        ye_dram = nc.dram_tensor("ye_dram", [EXPERTS * CAP, D], F32).ap()
        bg = "p (b g) -> p b g"

        def pe_c(pe):
            for b in range(BATCH):
                pe.wait_ge(LN.h, 2 * BATCH + b + 1)
                if b >= 2:
                    pe.wait_ge(C.hT, b - 1)
                else:
                    pe.wait_ge(T.nm, GROUPS * BATCH)
                for k in range(KC):
                    mm = pe.transpose(bank[b % 2][:, k * P:(k + 1) * P], h3[:, b, k * P:(k + 1) * P], ident[:, :])
                mm.then_inc(C.hTp, 1)
            for b in range(BATCH):
                pe.wait_ge(C.hT, b + 1)
                if b == 0:
                    pe.wait_ge(T.pt, GROUPS * BATCH)
                for k in range(KC):
                    mm = pe.matmul(bank[2][:, b * EXPERTS:(b + 1) * EXPERTS], hT3[:, k, b * P:(b + 1) * P],
                                   gate[:, k, :], start=(k == 0), stop=(k == KC - 1))
            mm.then_inc(C.lg, 1)

        def pe_c_up(pe, half):
            for m in range(SC):
                n = SC * half + m
                if n < 2:
                    pe.wait_ge(C.hT, BATCH)
                else:
                    pe.wait_ge(C.rel, n - 1)
                for k in range(KC):
                    mm = pe.matmul(bank[n % 2][:, :], sup[:, k, m * P:(m + 1) * P],
                                   hT3[:, k, half * 512:(half + 1) * 512], start=(k == 0), stop=(k == KC - 1))
                mm.then_inc(C.sup_, 1)

        def pe_c_down(pe, half):
            pe.wait_ge(C.sq, SC * (half + 1))
            for i in range(4):
                b = 4 * half + i
                for m in range(SC):
                    mm = pe.matmul(bank[4 + b // 2][:, (b % 2) * D:(b % 2 + 1) * D], c_sT[:, m, i * P:(i + 1) * P], sdown[:, m, :],
                                   start=(m == 0), stop=(m == SC - 1))
                mm.then_inc(C.sdn, 1)

        def pe_c_pos(pe):
            pe.wait_ge(C.sel, 1)
            pe.wait_ge(C.ex, 1)
            out = bank[3][:, 0:BATCH * EXPERTS]
            for b in range(BATCH - 1):
                rest = BATCH - 1 - b
                pe.matmul(out[:, (b + 1) * EXPERTS:].rearrange("p (b e) -> p b e", b=rest), onesb[:, :],
                          c_sel[:, b, :].unsqueeze(1).to_broadcast([P, rest, EXPERTS]),
                          start=(b == 0), stop=False, skip_group_check=True)
            pe.matmul(out[:, EXPERTS:], before[:, :], c_sel[:, 1:, :].rearrange("p b e -> p (b e)"),
                      start=False, stop=True, skip_group_check=True)
            mm = pe.matmul(out[:, 0:EXPERTS], before[:, :], c_sel[:, 0, :], start=True, stop=True)
            mm.then_inc(C.pos, 1)

        def pe_x_transpose(pe, e):
            pe.wait_ge(e_in[e % RING], 32 * (e // RING + 1))
            if e >= 2:
                pe.wait_ge(C.xTs, e - 1)
            for k in range(KC):
                mm = pe.transpose(bank[e % 2][:, k * P:(k + 1) * P], e_x[:, e % RING, k * P:(k + 1) * P], ident[:, :])
            mm.then_inc(C.xT, 1)

        def pe_x_up(pe, e):
            pe.wait_ge(C.xTs, e + 1)
            if e >= 2:
                pe.wait_ge(C.hr, e - 1)
            for k in range(KC):
                mm = pe.matmul(bank[2 + e % 2][:, 0:P], e_w[:, e % RING, k * HID:(k + 1) * HID],
                               e_xT[:, e % 2, k, :], start=(k == 0), stop=(k == KC - 1))
            mm.then_inc(C.up, 1)

        def pe_x_down(pe, e):
            pe.wait_ge(C.h2, e + 1)
            if e < 2:
                pe.wait_ge(C.shy, e + 1)
            if e >= 2:
                pe.wait_ge(C.ye, e - 1)
            pe.matmul(bank[4 + e % 2][:, 0:D], e_h[:, e % 2, :], e_w[:, e % RING, D:2 * D],
                      start=True, stop=True).then_inc(C.dn, 1)

        def act_c(act):
            for b in range(BATCH):
                act.wait_ge(C.hTp, b + 1)
                act.copy(hT3[:, :, b * P:(b + 1) * P], bank[b % 2][:, 0:D].rearrange("p (k n) -> p k n", k=KC))\
                   .then_inc(C.hT, 1)
            act.wait_ge(C.lg, 1)
            act.activation(c_ex[:].rearrange("p b e -> p (b e)"), bank[2][:, 0:BATCH * EXPERTS], ACT.Exp, scale=-1.0)\
               .then_inc(C.ex, 1)

        def act_c_shared(act, half):
            for m in range(SC):
                n = SC * half + m
                act.wait_ge(C.sup_, n + 1)
                if half:
                    act.wait_ge(C.sq, n - SC + 1)
                act.activation(c_sr[:, m, :], bank[n % 2][:, :], ACT.Relu).then_inc(C.rel, 1)
                act.wait_ge(C.rel, n + 1)
                if half and m == 0:
                    act.wait_ge(C.sdn, 4)
                act.activation(c_sT[:, m, :], c_sr[:, m, :], ACT.Square).then_inc(C.sq, 1)

        def act_x(act, e):
            if e < EXPERTS:
                act.wait_ge(C.xT, e + 1)
                if e >= 2:
                    act.wait_ge(C.up, e - 1)
                act.copy(e_xT[:, e % 2], bank[e % 2][:, 0:D].rearrange("p (k n) -> p k n", k=KC)).then_inc(C.xTs, 1)
            if e >= 1:
                e -= 1
                act.wait_ge(C.up, e + 1)
                if e >= 2:
                    act.wait_ge(C.h2, e - 1)
                act.activation(e_r[:, e % 2, :], bank[2 + e % 2][:, 0:P], ACT.Relu).then_inc(C.hr, 1)

        def dve_x(v, e):
            if e < EXPERTS:
                v.wait_ge(C.hr, e + 1)
                if e >= 2:
                    v.wait_ge(C.dn, e - 1)
                v.tensor_tensor(e_h[:, e % 2, :], e_r[:, e % 2, :], e_r[:, e % 2, :], ALU.mult).then_inc(C.h2, 1)
            if e >= 1:
                e -= 1
                v.wait_ge(C.dn, e + 1)
                if e >= RING:
                    v.wait_ge(e_out[e % RING], 16 * (e // RING))
                v.tensor_copy(e_y[:, e % RING, :], bank[4 + e % 2][:, 0:D]).then_inc(C.ye, 1)

        POS_READ = 23

        def dve_c_route(v):
            steps = 0

            def done(ins):
                nonlocal steps
                steps += 1
                ins.then_inc(C.route, 1)
                v.wait_ge(C.route, steps)

            flat = lambda a: a[:].rearrange("p b e -> p (b e)")
            v.wait_ge(C.ex, 1)
            done(v.tensor_scalar(flat(c_sg), flat(c_ex), 1.0, None, ALU.add))
            done(v.reciprocal(flat(c_sg), flat(c_sg)))
            done(v.tensor_tensor(c_sc[:], c_sg[:], rbias[:, :].unsqueeze(1).to_broadcast(BE), ALU.add))
            four = flat(c_sc).rearrange("p (n i) -> p n i", i=EPG)
            done(v.tensor_tensor(c_mx[:], four[:, :, 0::2], four[:, :, 1::2], ALU.max))
            done(v.tensor_tensor(c_mn[:], four[:, :, 0::2], four[:, :, 1::2], ALU.min))
            done(v.tensor_tensor(c_hi[:], c_mx[:, :, 0], c_mx[:, :, 1], ALU.max))
            done(v.tensor_tensor(c_lo[:], c_mx[:, :, 0], c_mx[:, :, 1], ALU.min))
            done(v.tensor_tensor(c_m3[:], c_mn[:, :, 0], c_mn[:, :, 1], ALU.max))
            done(v.tensor_tensor(c_sec[:], c_lo[:], c_m3[:], ALU.max))
            done(v.tensor_tensor(c_gs[:], c_hi[:], c_sec[:], ALU.add))
            gs3 = c_gs[:].rearrange(bg, b=BATCH)
            gfull = [P, BATCH, EGROUPS, EGROUPS]
            other = gs3.unsqueeze(2).to_broadcast(gfull)
            own = gs3.unsqueeze(3).to_broadcast(gfull)
            g4 = lambda a: a[:].rearrange("p (b g) o -> p b g o", b=BATCH)
            done(v.tensor_tensor(g4(c_gt), other, own, ALU.is_gt))
            done(v.tensor_tensor(g4(c_eq), other, own, ALU.is_equal))
            done(v.tensor_tensor(g4(c_eql), g4(c_eq), lower_g[:].unsqueeze(1).to_broadcast(gfull), ALU.mult))
            done(v.tensor_tensor(c_rk1[:], c_gt[:], c_eql[:], ALU.add))
            done(v.tensor_reduce(c_rk[:], c_rk1[:], AX.X, ALU.add))
            done(v.tensor_scalar(c_mk[:], c_rk[:], float(KEPT_GROUPS), None, ALU.is_lt))
            done(v.tensor_tensor(flat(c_ms0).rearrange("p (n i) -> p n i", i=EPG), four,
                                 c_mk[:].unsqueeze(2).to_broadcast([P, BATCH * EGROUPS, EPG]), ALU.mult))
            done(v.tensor_scalar(flat(c_ms), flat(c_ms0), 0.0, None, ALU.add))
            for b in range(BATCH):
                v.max(c_top[:, b, :], c_ms[:, b, :]).then_inc(C.top, 1)
            v.wait_ge(C.top, BATCH)
            for b in range(BATCH):
                v.max_index(c_idx[:, b, :], c_top[:, b, :], c_ms[:, b, :]).then_inc(C.idx, 1)
            v.wait_ge(C.idx, BATCH)
            done(v.tensor_copy(c_idxf[:], c_idx[:, :, 0:TOPK]))
            done(v.tensor_tensor(c_oh[:], c_idxf[:].rearrange("p b k -> p (b k)").unsqueeze(2).to_broadcast(BKE),
                                 iota_e[:, :].unsqueeze(1).to_broadcast(BKE), ALU.is_equal))
            with nc.allow_low_precision(reason="a choice count is 0 or 1"):
                v.tensor_reduce(c_sel[:], c_oh[:].rearrange("p (b k) e -> p b e k", b=BATCH), AX.X, ALU.add)\
                 .then_inc(C.sel, 1)
            full4 = [P, BATCH, TOPK, EXPERTS]
            k4 = lambda a: a[:].rearrange("p (b k) e -> p b k e", b=BATCH)
            bk = lambda a: a[:].rearrange("p b k -> p (b k)")
            done(v.tensor_tensor(k4(c_tmp), k4(c_oh), c_sg[:].unsqueeze(2).to_broadcast(full4), ALU.mult))
            done(v.tensor_reduce(bk(c_w4), c_tmp[:], AX.X, ALU.add))
            v.wait_ge(C.pos, 1)
            done(v.tensor_tensor(k4(c_tmp2), k4(c_oh),
                                 bank[3][:, 0:BATCH * EXPERTS].rearrange("p (b e) -> p b e", b=BATCH)
                                 .unsqueeze(2).to_broadcast(full4), ALU.mult))
            pos_read = steps
            done(v.tensor_reduce(bk(c_p4), c_tmp2[:], AX.X, ALU.add))
            done(v.tensor_scalar(bk(c_drop), bk(c_p4), float(CAP), SKIP, ALU.is_ge, ALU.mult))
            done(v.scalar_tensor_tensor(out=bk(c_row), in0=bk(c_idxf), scalar=float(CAP), in1=bk(c_p4),
                                        op0=ALU.mult, op1=ALU.add))
            v.tensor_tensor(bk(c_srow), bk(c_row), bk(c_drop), ALU.add).then_inc(C.srow, 1)
            done(v.tensor_scalar(bk(c_pc), bk(c_p4), float(CAP - 1), None, ALU.min))
            v.scalar_tensor_tensor(out=bk(c_grow), in0=bk(c_idxf), scalar=float(CAP), in1=bk(c_pc),
                                   op0=ALU.mult, op1=ALU.add).then_inc(C.grow, 1)
            done(v.tensor_reduce(c_ws[:], c_w4[:], AX.X, ALU.add))
            done(v.tensor_scalar(c_ws[:], c_ws[:], 1e-20, None, ALU.add))
            done(v.reciprocal(c_wr[:], c_ws[:]))
            done(v.tensor_tensor(c_wv[:], c_w4[:], c_wr[:].unsqueeze(2).to_broadcast([P, BATCH, TOPK]), ALU.mult))
            done(v.tensor_scalar(bk(c_ok), bk(c_p4), float(CAP), ROUTE_SCALE, ALU.is_lt, ALU.mult))
            done(v.tensor_tensor(bk(c_wv), bk(c_wv), bk(c_ok), ALU.mult))
            assert pos_read == POS_READ

        def dve_c_shared(v):
            for p in range(PAIRS):
                v.wait_ge(C.sdn, 2 * p + 2)
                v.tensor_tensor(x_sb[:, 2 * p:2 * p + 2, :], x_sb[:, 2 * p:2 * p + 2, :],
                                bank[4 + p][:, :].rearrange("p (i n) -> p i n", i=2), ALU.add).then_inc(C.shy, 1)

        def dve_c_combine(v, b):
            v.wait_ge(gat[b % 2], 16 * TOPK * (b // 2 + 1))
            if b == 0:
                v.wait_ge(C.shy, PAIRS)
            for k in range(TOPK):
                v.scalar_tensor_tensor(out=x_sb[:, b, :], in0=g_y[:, b % 2, k, :], scalar=c_wv[:, b, k:k + 1],
                                       in1=x_sb[:, b, :], op0=ALU.mult, op1=ALU.add).then_inc(C.acc, 1)
                v.wait_ge(C.acc, TOPK * b + k + 1)

        def pool_c_scatter(g):
            g.wait_ge(C.srow, 1)
            g.wait_ge(C.zeroed, 16 * 4)
            for b in range(BATCH):
                for k in range(TOPK):
                    g.indirect_dma_start(xe_dram, bass.IndirectOffsetOnAxis(ap=c_srow[:, b, k:k + 1], axis=0),
                                         h3[:, b, :], None, bounds_check=EXPERTS * CAP - 1, oob_is_err=False)\
                     .then_inc(C.scat, 16)

        def pool_c_gather(g, b):
            if b == 0:
                g.wait_ge(C.grow, 1)
                g.wait_ge(C.sq, 2 * SC)
                for i in range(RING):
                    g.wait_ge(e_out[i], 16 * EXPERTS // RING)
            if b >= 2:
                g.wait_ge(C.acc, TOPK * (b - 1))
            for k in range(TOPK):
                g.indirect_dma_start(g_y[:, b % 2, k, :], None, ye_dram,
                                     bass.IndirectOffsetOnAxis(ap=c_grow[:, b, k:k + 1], axis=0),
                                     bounds_check=EXPERTS * CAP - 1, oob_is_err=False).then_inc(gat[b % 2], 16)


        def pe_d_step(pe, s):
            P_, S_, E_, O_ = (s if s < BATCH else None, s - 1 if 1 <= s <= BATCH else None,
                              s - 2 if 2 <= s < BATCH + 2 else None, s - 3 if s >= 3 else None)
            if P_ is not None:
                b = P_ + BATCH
                pe.wait_ge(LN.h, 2 * BATCH + b + 1)
                if b >= 1:
                    pe.wait_ge(T.v1, b)
                for k in range(KC):
                    mm = pe.transpose(bank[6][:, k * P:(k + 1) * P], att.h[:, b % 2, k * P:(k + 1) * P], ident[:, :])
                mm.then_inc(T.hTp, 1)
            for j in range(GROUPS):
                if S_ is not None:
                    pe_scores(pe, T, S_ + BATCH, j)
                if E_ is not None:
                    pe_scores_t(pe, T, E_ + BATCH, j)
                    if j >= 1:
                        pe_values(pe, T, E_ + BATCH, j - 1)
                if j == 0 and P_ is not None:
                    b = P_ + BATCH
                    pe.wait_ge(T.hT, b + 1)
                    if b >= 1:
                        pe.wait_ge(T.qd, b)
                    for c in range(CH):
                        for k in range(KC):
                            mm = pe.matmul(bank4(5)[:, c, :], wk1[:, k, c * P:(c + 1) * P], att.hT[:, b % 2, k, :],
                                           start=(k == 0), stop=(k == KC - 1))
                    mm.then_inc(T.K, 1)
                if j == 1:
                    if O_ is not None:
                        b = O_ + BATCH
                        pe.wait_ge(T.o, b + 1)
                        if S_ is not None or s - 2 < BATCH:
                            pe.wait_ge(T.ccT, BATCH + min(s - 1, BATCH))
                        for k in range(KC):
                            mm = pe.transpose(bank[7][:, k * P:(k + 1) * P], att.o[:, b % 2, k * P:(k + 1) * P],
                                              ident[:, :])
                        mm.then_inc(T.oTp, 1)
                    if P_ is not None:
                        b = P_ + BATCH
                        for k in range(KC):
                            mm = pe.matmul(bank[6][:, 0:D], att.hT[:, b % 2, k, :], wv1[:, k, :],
                                           start=(k == 0), stop=(k == KC - 1))
                        mm.then_inc(T.Vp, 1)
                if j == 2 and O_ is not None:
                    pe.wait_ge(T.oT, O_ + BATCH + 1)
                    for k in range(KC):
                        mm = pe.matmul(bank[7][:, 0:D], att.oT[:, k, :], wo1[:, k, :],
                                       start=(k == 0), stop=(k == KC - 1))
                    mm.then_inc(T.y, 1)
            if P_ is not None:
                b = P_ + BATCH
                pe.wait_ge(T.kl, b + 1)
                for c in range(CH):
                    for k in range(KC):
                        mm = pe.matmul(bank4(5)[:, c, :], wq1[:, k, c * P:(c + 1) * P], att.hT[:, b % 2, k, :],
                                       start=(k == 0), stop=(k == KC - 1))
                mm.then_inc(T.QT, 1)
            if E_ is not None:
                pe_values(pe, T, E_ + BATCH, GROUPS - 1)
            if S_ is not None:
                def free():
                    if O_ is not None:
                        pe.wait_ge(T.res, O_ + BATCH + 1)
                pe_max_t(pe, T, S_ + BATCH, free)

        def act_d_step(act, s):
            if s < BATCH:
                b = s + BATCH
                act.wait_ge(T.hTp, b + 1)
                if b >= 2:
                    act.wait_ge(T.QT, b - 1)
                act.copy(att.hT[:, b % 2], bank[6][:, 0:D].rearrange("p (k n) -> p k n", k=KC)).then_inc(T.hT, 1)
            for j in range(GROUPS):
                if 2 <= s < BATCH + 2:
                    act_exp(act, T, s - 2 + BATCH, j)
                if j == 0 and s < BATCH:
                    b = s + BATCH
                    act.wait_ge(T.K, b + 1)
                    if b >= 3:
                        act.wait_ge(T.E, GROUPS * (b - 2))
                    act.copy(att.kr[:, b % 3], bank4(5)).then_inc(T.kr, 1)
                if j == 1 and s >= 3:
                    b = s - 3 + BATCH
                    act.wait_ge(T.oTp, b + 1)
                    if b >= 1:
                        act.wait_ge(T.y, b)
                    act.copy(att.oT[:], bank[7][:, 0:D].rearrange("p (k n) -> p k n", k=KC)).then_inc(T.oT, 1)
            if s < BATCH:
                act_qr(act, T, s + BATCH)
            if 1 <= s <= BATCH:
                act_max_t(act, T, s - 1 + BATCH)

        def dve_d_prep(v, b):
            dve_stats(v, 3, b)
            v.wait_ge(T.hTp, BATCH + b - 1)
            dve_norm(v, 3, b, att.h[:, b % 2, :])

        def dve_d_step(v, s):
            P_, S_, O_ = (s if s < BATCH else None, s - 1 if 1 <= s <= BATCH else None, s - 3 if s >= 3 else None)
            if O_ is not None:
                b = O_ + BATCH

                def free():
                    if b >= 2:
                        v.wait_ge(T.oTp, b - 1)
                dve_attended(v, T, b, free)
            for j in range(GROUPS):
                if S_ is not None:
                    dve_rowmax(v, T, S_ + BATCH, j)
                if P_ is not None and j == 0:
                    b = P_ + BATCH
                    v.wait_ge(T.kr, b + 1)
                    if b >= 3:
                        v.wait_ge(T.E, GROUPS * (b - 2))
                    v.tensor_tensor(att.kl[:, b % 3], bank4(5), att.kr[:, b % 3].bitcast(F32), ALU.subtract)\
                     .then_inc(T.kl, 1)
                if P_ is not None and j == 1:
                    b = P_ + BATCH
                    v.wait_ge(T.Vp, b + 1)
                    if b >= 3:
                        v.wait_ge(T.O, GROUPS * (b - 2))
                    v.tensor_copy(att.v1[:, b % 3, :, 0:HD], bank[6][:, 0:D].rearrange("p (h d) -> p h d", h=HEADS))\
                     .then_inc(T.v1, 1)
                if O_ is not None and j == 2:
                    b = O_ + BATCH
                    v.wait_ge(T.y, b + 1)
                    v.tensor_tensor(x_sb[:, b - BATCH, :], x_sb[:, b - BATCH, :], bank[7][:, 0:D], ALU.add).then_inc(T.res, 1)
            if S_ is not None:
                dve_split_max(v, T, S_ + BATCH)
            if P_ is not None:
                dve_qd(v, T, P_ + BATCH)
            if s + 1 < BATCH:
                dve_c_combine(v, s + 1)
                dve_d_prep(v, s + 1)

        E = sems("e", "hTp kT e ma mb a1 e1 a2 e2 ov kv p q x2 num den rd y yTp res zero")
        take = views(scratch)
        f_h = take([P, 2, 2, D])
        W = [P, KC, 2, SEQ]
        f_kT, f_e, f_ma, f_mb, f_a1, f_e1, f_a2, f_e2, f_x1, f_x2, f_x3 = (
            take(W) for _ in range(11))
        WP = [P, KC, 2, SEQ + 1]
        f_o, f_p, f_q = (take(WP) for _ in range(3))
        f_dec = take(W)

        fl = lambda a: a[:].rearrange("p k i n -> p (k i n)")
        e_bank = lambda n: bank[n][:, :].rearrange("p (k i n) -> p k i n", k=KC, i=2)

        def pe_e_in(pe, p):
            for i in range(2):
                b = 2 * p + i
                pe.wait_ge(LN.h, 4 * BATCH + b + 1)
            if p >= 1:
                pe.wait_ge(E.kT, p)
            else:
                pe.wait_ge(T.nm, 2 * GROUPS * BATCH)
            for i in range(2):
                for k in range(KC):
                    mm = pe.transpose(e_bank(0)[:, k, i, :], f_h[:, p % 2, i, k * P:(k + 1) * P], ident[:, :])
            mm.then_inc(E.hTp, 1)

        def pe_e_out(pe, p):
            pe.wait_ge(E.y, p + 1)
            if p >= 1:
                pe.wait_ge(E.res, p)
            for i in range(2):
                for k in range(KC):
                    mm = pe.transpose(bank[1][:, i * D + k * P:i * D + (k + 1) * P], f_x3[:, k, i, :], ident[:, :])
            mm.then_inc(E.yTp, 1)

        def act_e(act, p):
            act.wait_ge(E.hTp, p + 1)
            if p >= 1:
                act.wait_ge(E.e, p)
            act.copy(f_kT[:], e_bank(0)).then_inc(E.kT, 1)
            act.wait_ge(E.ma, 4 * p + 2)
            if p >= 1:
                act.wait_ge(E.p, 4 * p)
                act.wait_ge(E.q, 4 * p)
            act.activation(f_a2[:], f_ma[:], ACT.Exp, scale=-1.0).then_inc(E.a2, 1)
            act.wait_ge(E.mb, 4 * p + 2)
            act.activation(f_e2[:], f_mb[:], ACT.Exp).then_inc(E.e2, 1)
            act.wait_ge(E.ma, 4 * p + 4)
            if p >= 1:
                act.wait_ge(E.den, p)
            act.activation(f_a1[:], f_ma[:], ACT.Exp, scale=-1.0).then_inc(E.a1, 1)
            act.wait_ge(E.mb, 4 * p + 4)
            act.activation(f_e1[:], f_mb[:], ACT.Exp).then_inc(E.e1, 1)

        def dve_e_norm(v, p):
            for i in range(2):
                b = 2 * p + i
                dve_stats(v, 4, b)
                if p >= 2:
                    v.wait_ge(E.hTp, p - 1)
                dve_norm(v, 4, b, f_h[:, p % 2, i, :])

        def dve_e(v, p):
            vT = ctxT[:, :, 2 * p * P:(2 * p + 2) * P].rearrange("p k (i n) -> p k i n", i=2)
            v.wait_ge(E.kT, p + 1)
            for k in range(KC):
                for i in range(2):
                    v.tensor_tensor_scan(f_o[:, k, i, 1:], f_dec[:, k, i, :], f_kT[:, k, i, :], NEG_BIG,
                                         ALU.add, ALU.max).then_inc(E.ov, 1)
            v.wait_ge(E.ov, 4 * (p + 1))
            v.tensor_tensor(f_e[:], f_kT[:], f_o[:, :, :, 0:SEQ], ALU.subtract).then_inc(E.e, 1)
            v.wait_ge(E.e, p + 1)
            if p >= 1:
                v.wait_ge(E.a1, p)
                v.wait_ge(E.e1, p)
            for k in range(KC):
                v.tensor_scalar(f_ma[:, k], f_e[:, k], decay[:, k:k + 1], 0.0, ALU.subtract, ALU.max)\
                 .then_inc(E.ma, 1)
                v.tensor_scalar(f_mb[:, k], f_e[:, k], decay[:, k:k + 1], 0.0, ALU.subtract, ALU.min)\
                 .then_inc(E.mb, 1)
            v.wait_ge(E.a2, p + 1)
            v.wait_ge(E.e2, p + 1)
            for k in range(KC):
                v.tensor_scalar(f_ma[:, k], f_e[:, k], bonus[:, k:k + 1], 0.0, ALU.add, ALU.max)\
                 .then_inc(E.ma, 1)
                v.tensor_scalar(f_mb[:, k], f_e[:, k], bonus[:, k:k + 1], 0.0, ALU.add, ALU.min)\
                 .then_inc(E.mb, 1)
            v.tensor_tensor(f_x1[:], f_e2[:], vT, ALU.mult).then_inc(E.kv, 1)
            v.wait_ge(E.kv, p + 1)
            for k in range(KC):
                for i in range(2):
                    v.tensor_tensor_scan(f_p[:, k, i, 1:], f_a2[:, k, i, :], f_x1[:, k, i, :], 0.0,
                                         ALU.mult, ALU.add).then_inc(E.p, 1)
                    v.tensor_tensor_scan(f_q[:, k, i, 1:], f_a2[:, k, i, :], f_e2[:, k, i, :], 0.0,
                                         ALU.mult, ALU.add).then_inc(E.q, 1)
            v.wait_ge(E.p, 4 * (p + 1))
            v.wait_ge(E.q, 4 * (p + 1))
            v.wait_ge(E.a1, p + 1)
            v.wait_ge(E.e1, p + 1)
            v.tensor_tensor(f_x1[:], f_a1[:], f_p[:, :, :, 0:SEQ], ALU.mult).then_inc(E.x2, 1)
            v.tensor_tensor(f_x2[:], f_e1[:], vT, ALU.mult).then_inc(E.x2, 1)
            if p >= 1:
                v.wait_ge(E.yTp, p)
            v.tensor_tensor(f_x3[:], f_a1[:], f_q[:, :, :, 0:SEQ], ALU.mult).then_inc(E.x2, 1)
            v.wait_ge(E.x2, 3 * (p + 1))
            v.tensor_tensor(f_x1[:], f_x1[:], f_x2[:], ALU.add).then_inc(E.num, 1)
            v.tensor_tensor(f_x3[:], f_x3[:], f_e1[:], ALU.add).then_inc(E.den, 1)
            v.wait_ge(E.num, p + 1)
            v.wait_ge(E.den, p + 1)
            v.reciprocal(f_x2[:], f_x3[:]).then_inc(E.rd, 1)
            v.wait_ge(E.rd, p + 1)
            v.tensor_tensor(f_x3[:], f_x1[:], f_x2[:], ALU.mult).then_inc(E.y, 1)

        def dve_e_residual(v, p):
            v.wait_ge(E.yTp, p + 1)
            v.tensor_tensor(x_sb[:, 2 * p:2 * p + 2, :], x_sb[:, 2 * p:2 * p + 2, :],
                            bank[1][:, :].rearrange("p (i n) -> p i n", i=2), ALU.add).then_inc(E.res, 1)

        F = sems("f", "hTp hT y t1 t2 res out")
        take = views(w0_flat)
        g_h, g_t1 = take([P, 2, D]), take([P, 2, D])
        g_hT = sb("g_hT", [P, 2, KC, P], BF16)
        g_t2 = sb("g_t2", [P, 2, D], F16)
        g_o = views(w0_flat[:, 8 * D:])([P, BATCH, D])

        def pe_f(pe, b):
            pe.wait_ge(zq.sem.q, BATCH + b + 1)
            if b >= 2:
                pe.wait_ge(F.hT, b - 1)
            for k in range(KC):
                mm = pe.transpose(bank[2 + b % 2][:, 0:P].bitcast(BF16).rearrange("p (k n) -> p k n", k=KC)[:, k, :],
                                  zq.q[:, b % 2, k * P:(k + 1) * P], identb[:, :])
            mm.then_inc(F.hTp, 1)
            pe.wait_ge(F.hT, b + 1)
            if b >= 2:
                pe.wait_ge(F.t1, b - 1)
            for k in range(KC):
                mm = pe.matmul(bank[4 + b % 2][:, 0:D], g_hT[:, b % 2, k, :], wfb[:, k, :],
                               start=(k == 0), stop=(k == KC - 1))
            mm.then_inc(F.y, 1)

        def act_f(act, b):
            act.wait_ge(F.hTp, b + 1)
            if b >= 2:
                act.wait_ge(F.y, b - 1)
            act.copy(g_hT[:, b % 2], bank[2 + b % 2][:, 0:P].bitcast(BF16).rearrange("p (k n) -> p k n", k=KC))\
               .then_inc(F.hT, 1)

        def dve_f_in(v, b):
            dve_stats(v, 5, b)
            dve_norm(v, 5, b, g_h[:, b % 2, :])
            v.wait_ge(LN.h, 5 * BATCH + b + 1)

            def free():
                if b >= 2:
                    v.wait_ge(F.hTp, b - 1)
            dve_quant(v, zq, BATCH + b, g_h[:, b % 2, :], 1e-7 / 127.0, free)

        def dve_f_out(v, b):
            v.wait_ge(F.y, b + 1)
            v.scalar_tensor_tensor(out=g_t1[:, b % 2, :], in0=bank[4 + b % 2][:, 0:D], scalar=zq.s[:, BATCH + b:BATCH + b + 1],
                                   in1=wscale, op0=ALU.mult, op1=ALU.mult).then_inc(F.t1, 1)
            v.wait_ge(F.t1, b + 1)
            v.tensor_tensor(g_t2[:, b % 2, :], g_t1[:, b % 2, :], fbias, ALU.add).then_inc(F.t2, 1)
            v.wait_ge(F.t2, b + 1)
            v.tensor_tensor(g_o[:, b, :], x_sb[:, b, :], g_t2[:, b % 2, :], ALU.add).then_inc(F.res, 1)

        block = ctx.enter_context(nc.Block())
        LAST = BATCH + 3

        @block.sync
        def _(sp):
            for b in range(0, BATCH, 2):
                sp.dma_start(x_sb[:, b:b + 2, :], t["x"][b:b + 2].rearrange("b p d -> p b d")).then_inc(ld.x, 16)
            sp.dma_start(ident[:, :], t["ident"]).then_inc(ld.const, 16)
            sp.dma_start(half_pow[:, :], t["half_pow"]).then_inc(ld.const, 16)
            sp.dma_start(init4[:, :], t["init"]).then_inc(ld.const, 16)
            sp.dma_start(w0[:], t["w0"]).then_inc(ld.w0, 16)
            sp.dma_start(qw[:], t["qw"]).then_inc(ld.qw, 16)
            for dst, name in ((ones, "ones"), (beforef, "before"), (lo_rows, "lo_rows"),
                              (iota_e, "iota_e")):
                sp.dma_start(dst[:, :], t[name]).then_inc(ld.rows, 16)
            for dst, name in ((pickf, "pick"), (lower_g, "lower_g")):
                sp.dma_start(dst[:], t[name]).then_inc(ld.rows, 16)
            for i, name in enumerate(("bq", "bv", "bp", "wscale", "fbias")):
                sp.dma_start(rows[:, i, :], t[name].to_broadcast([P, D])).then_inc(ld.rows, 16)
            sp.dma_start(rbias[:, :], t["rbias"].to_broadcast([P, EXPERTS])).then_inc(ld.rows, 16)
            sp.dma_start(ctxT[:], t["ctxT"]).then_inc(ld.kv0, 16)
            sp.dma_start(wk0[:], t["wk0"]).then_inc(ld.kv0, 16)
            sp.dma_start(wv0[:], t["wv0"]).then_inc(ld.kv0, 16)
            sp.dma_start(bk0[:, :], t["bk0"]).then_inc(ld.kv0, 16)
            for dst, name in ((gate, "gate"), (sup, "sup"), (sdown, "sdown")):
                sp.dma_start(dst[:], t[name]).then_inc(ld.moe, 16)
            for dst, name in ((wq1, "wq1"), (wk1, "wk1"), (wv1, "wv1"), (wo1, "wo1"), (wf8, "wf8")):
                sp.dma_start(dst[:], t[name]).then_inc(ld.l1, 16)
            for dst, name in ((decay, "decay"), (bonus, "bonus")):
                sp.dma_start(dst[:, :], t[name]).then_inc(ld.l1, 16)
            sp.wait_ge(cst.small, 1)
            for i in range(4):
                n = EXPERTS * CAP // 4
                sp.dma_start(xe_dram[i * n:(i + 1) * n, :].rearrange("(p r) d -> p (r d)", p=P),
                             zrow[:, :].unsqueeze(1).to_broadcast([P, n * D // P // 1024, 1024])
                             ).then_inc(C.zeroed, 16)
            for e in range(RING):
                sp.dma_start(e_w[:, e, :], t["we"][e]).then_inc(e_in[e], 16)
            sp.wait_ge(C.scat, 16 * BATCH * TOPK)
            for e in range(EXPERTS + 2):
                if e < EXPERTS:
                    if e >= RING:
                        sp.wait_ge(C.xT, e - RING + 1)
                    sp.dma_start(e_x[:, e % RING, :], xe_dram[e * CAP:(e + 1) * CAP, :]).then_inc(e_in[e % RING], 16)
                if e >= 2:
                    n = e - 2
                    sp.wait_ge(C.ye, n + 1)
                    sp.dma_start(ye_dram[n * CAP:(n + 1) * CAP, :], e_y[:, n % RING, :]).then_inc(e_out[n % RING], 16)
                    if n + RING < EXPERTS:
                        sp.dma_start(e_w[:, n % RING, :], t["we"][n + RING]).then_inc(e_in[n % RING], 16)
            for b in range(BATCH):
                sp.wait_ge(F.res, b + 1)
                sp.dma_start(t["out"][b], g_o[:, b, :]).then_inc(F.out, 16)
            sp.wait_ge(F.out, 16 * BATCH)

        @block.gpsimd
        def _(g):
            g.wait_ge(ld.const, 48)
            for b in range(BATCH):
                pool_rstd(g, 0, b)
            pool_rstd(g, 1, 0)
            g.wait_ge(ld.rows, 16 * 12)
            for s in range(BATCH):
                pool_b_step(g, s)
            for b in range(BATCH):
                pool_rstd(g, 2, b)
            pool_c_scatter(g)
            pool_c_gather(g, 0)
            for b in range(BATCH):
                if b + 1 < BATCH:
                    pool_c_gather(g, b + 1)
                pool_rstd(g, 3, b)
            for n in (4, 5):
                for b in range(BATCH):
                    pool_rstd(g, n, b)

        @block.vector
        def _(v):
            v.memset(zrow[:, :], 0.0).then_inc(cst.small, 1)
            for b in range(3):
                v.memset(att.v1[:, b, :, HD], 1.0).then_inc(cst.vones, 1)
            v.wait_ge(ld.x, 16 * PAIRS)
            for b in range(BATCH):
                dve_stats(v, 0, b)
            v.wait_ge(ld.const, 48)
            v.tensor_scalar(init4[:, :], init4[:, :], 4.0, None, ALU.mult).then_inc(A.init4, 1)
            dve_a_norm(v, 0)
            v.wait_ge(ld.qw, 16)
            qf = qw[:].rearrange("p w c n -> p (w c) n")
            v.tensor_reduce(qw_s[:].rearrange("p w c -> p (w c)"), qf, AX.X, ALU.max,
                            apply_absolute_value=True).then_inc(qs.scale, 1)
            v.wait_ge(qs.scale, 1)
            v.tensor_scalar(qw_s[:], qw_s[:], 1.0 / 127.0, 1e-8, ALU.mult, ALU.max).then_inc(qs.scale, 1)
            v.wait_ge(qs.scale, 2)
            v.reciprocal(qw_r[:], qw_s[:]).then_inc(qs.scale, 1)
            v.wait_ge(qs.scale, 3)
            v.wait_ge(ld.rows, 16 * 12)
            for n in range(2 * KC):
                v.tensor_scalar(qw_i[:].rearrange("p w c n -> p (w c) n")[:, n, :], qf[:, n, :],
                                qw_r[:].rearrange("p w c -> p (w c)")[:, n:n + 1], ROUND,
                                ALU.mult, ALU.add).then_inc(qs.i, 1)
                v.tensor_scalar(qw_diag[:, n, :], ident[:, :], qw_s[:].rearrange("p w c -> p (w c)")[:, n:n + 1],
                                None, ALU.mult).then_inc(qs.diag, 1)
            v.wait_ge(qs.i, 2 * KC)
            v.tensor_scalar(qw_b[:], qw_i[:], -ROUND, None, ALU.add).then_inc(qs.b, 1)
            v.tensor_copy(identb[:, :], ident[:, :]).then_inc(cst.ident, 1)
            v.tensor_copy(onesb[:, :], ones[:, :]).then_inc(cst.ident, 1)
            v.tensor_copy(before[:, :], beforef[:, :]).then_inc(cst.ident, 1)
            v.tensor_copy(pick[:], pickf[:]).then_inc(cst.pick, 1)
            v.wait_ge(A.init4, 1)
            for p in range(PAIRS):
                if p + 1 < PAIRS:
                    dve_a_norm(v, p + 1)
                dve_a(v, p)
                dve_a_residual(v, p)
            v.wait_ge(qs.evacrow, 1)
            v.wait_ge(ld.kv0, 64)
            v.wait_ge(cst.vones, 3)
            dve_b_prep(v, 0)
            for s in range(LAST):
                dve_b_step(v, s)
            for b in range(BATCH):
                v.wait_ge(T.res, b + 1)
                dve_stats(v, 2, b)
                dve_norm(v, 2, b, h3[:, b, :])
            dve_c_route(v)
            v.wait_ge(LN.h, 2 * BATCH + BATCH)
            dve_c_shared(v)
            for e in range(EXPERTS + 1):
                dve_x(v, e)
            v.wait_ge(ld.l1, 16 * 7)
            v.tensor_copy(wfb[:].rearrange("p k n -> p (k n)"),
                          wf8[:].rearrange("p k n -> p (k n)").bitcast(I8)).then_inc(cst.wfb, 1)
            dve_c_combine(v, 0)
            dve_d_prep(v, 0)
            for s in range(LAST):
                dve_d_step(v, s)
            for a, value in ((f_o, NEG_BIG), (f_p, 0.0), (f_q, 0.0)):
                v.memset(a[:, :, :, 0], value).then_inc(E.zero, 1)
            v.memset(f_dec[:], 0.0).then_inc(E.zero, 1)
            v.wait_ge(E.zero, 4)
            for k in range(KC):
                v.tensor_scalar(f_dec[:, k], f_dec[:, k], decay[:, k:k + 1], None, ALU.add).then_inc(E.zero, 1)
            v.wait_ge(E.zero, 4 + KC)
            v.wait_ge(T.res, 2 * BATCH)
            dve_e_norm(v, 0)
            for p in range(PAIRS):
                if p + 1 < PAIRS:
                    dve_e_norm(v, p + 1)
                dve_e(v, p)
                dve_e_residual(v, p)
            for b in range(BATCH):
                if b % 2 == 0:
                    v.wait_ge(E.res, b // 2 + 1)
                dve_f_in(v, b)
                if b >= 1:
                    dve_f_out(v, b - 1)
            dve_f_out(v, BATCH - 1)

        @block.scalar
        def _(act):
            act.wait_ge(ld.const, 48)
            act.wait_ge(qs.T, 1)
            for w in range(2):
                act.copy(qwT[:, w], bank[1 + w][:, 0:2 * P].bitcast(BF16).rearrange("p (k n) -> p k n", k=KC))\
                   .then_inc(qs.evacT, 1)
            act.wait_ge(qs.row, 1)
            act.copy(qw_row[:].rearrange("p w n -> p (w n)"), bank[3][:, :]).then_inc(qs.evacrow, 1)
            for p in range(PAIRS):
                act_a(act, p)
            for s in range(LAST):
                act_b_step(act, s)
            act_c(act)
            for half in range(2):
                act_c_shared(act, half)
            for e in range(EXPERTS + 1):
                act_x(act, e)
            for s in range(LAST):
                act_d_step(act, s)
            for p in range(PAIRS):
                act_e(act, p)
            for b in range(BATCH):
                act_f(act, b)

        @block.tensor
        def _(pe):
            pe.wait_ge(qs.b, 1)
            pe.wait_ge(cst.ident, 3)
            pe.wait_ge(ld.const, 48)
            for w in range(2):
                for o in range(KC):
                    for k in range(KC):
                        mm = pe.transpose(bank[1 + w][:, 0:2 * P].bitcast(BF16)[:, k * D + o * P:k * D + (o + 1) * P],
                                          qw_b[:, w, o, k * P:(k + 1) * P], identb[:, :])
            mm.then_inc(qs.T, 1)
            pe.wait_ge(qs.diag, 2 * KC)
            for n in range(2 * KC):
                mm = pe.matmul(bank[3][:, n * P:(n + 1) * P], ones[:, :], qw_diag[:, n, :], start=True, stop=True)
            mm.then_inc(qs.row, 1)
            pe.wait_ge(qs.evacT, 2)
            pe.wait_ge(qs.evacrow, 1)
            pe_a_transpose(pe, 0)
            pe.wait_ge(ld.w0, 16)
            for p in range(PAIRS):
                pe_a_project(pe, p)
                if p + 1 < PAIRS:
                    pe_a_transpose(pe, p + 1)
                pe_a_down(pe, p)
            pe.wait_ge(A.res, PAIRS)
            pe.wait_ge(ld.kv0, 64)
            pe.wait_ge(cst.pick, 1)
            for s in range(LAST):
                pe_b_step(pe, s)
            pe.wait_ge(ld.moe, 48)
            pe_c(pe)
            pe_c_up(pe, 0)
            pe_c_down(pe, 0)
            pe_c_up(pe, 1)
            pe_c_down(pe, 1)
            pe_c_pos(pe)
            pe.wait_ge(C.route, POS_READ)
            pe.wait_ge(C.rel, 2 * SC)
            for e in range(EXPERTS + 2):
                if e < EXPERTS:
                    pe_x_transpose(pe, e)
                if 1 <= e <= EXPERTS:
                    pe_x_up(pe, e - 1)
                if e >= 2:
                    pe_x_down(pe, e - 2)
            pe.wait_ge(C.ye, EXPERTS)
            pe.wait_ge(C.hr, EXPERTS)
            pe.wait_ge(C.xTs, EXPERTS)
            pe.wait_ge(ld.l1, 16 * 7)
            for s in range(LAST):
                pe_d_step(pe, s)
            pe.wait_ge(T.pt, 2 * GROUPS * BATCH)
            pe.wait_ge(T.o, 2 * BATCH)
            pe_e_in(pe, 0)
            for p in range(PAIRS):
                if p + 1 < PAIRS:
                    pe_e_in(pe, p + 1)
                pe_e_out(pe, p)
            pe.wait_ge(cst.wfb, 1)
            for b in range(BATCH):
                pe_f(pe, b)


def _layouts(a):
    def chunked(w):
        w = np.asarray(w)
        return np.ascontiguousarray(w.reshape(w.shape[0] // P, P, w.shape[1]).transpose(1, 0, 2))

    def column(v):
        return np.ascontiguousarray(np.asarray(v).reshape(-1, P).T)

    def per_head(w, repeat=1):
        w = np.asarray(w)
        w = w.reshape((HEADS // repeat, 1, HD) + w.shape[1:])
        w = np.repeat(np.repeat(w, repeat, axis=0), 2, axis=1)
        return w.reshape((2 * D,) + w.shape[3:])

    l0 = [np.asarray(a[f"L0_attn_{n}"]) for n in L0_MATS]
    wkv, bkv = np.asarray(a["L0_xattn_wkv"]), np.asarray(a["L0_xattn_bkv"])
    qw = np.stack([np.asarray(a["L0_xattn_wq"]), np.asarray(a["L0_xattn_wp"])])
    up = np.asarray(a["L0_ffn_up_w"]).transpose(0, 2, 1).reshape(EXPERTS, KC, P, HID).transpose(0, 2, 1, 3)
    down = np.asarray(a["L0_ffn_down_w"]).transpose(0, 2, 1)
    wv1 = np.repeat(np.asarray(a["L1_attn_wv"]).reshape(HEADS // 2, 1, HD, D), 2, axis=1).reshape(D, D)
    row = lambda n: np.asarray(a[n]).reshape(1, -1)
    r = np.arange(P)
    pick = ((r[:, None] % HEADS) == (GROUPS * np.arange(CH)[None, :] + r[:, None] // 32))
    out = {
        "x": np.asarray(a["x"]),
        "w0": chunked(np.concatenate(l0, axis=1)).reshape(P, KC, len(L0_MATS), D),
        "init": column(a["L0_attn_init_state"]),
        "qw": qw.reshape(2, KC, P, D).transpose(2, 0, 1, 3),
        "ctxT": chunked(np.asarray(a["ctx_2048"]).reshape(TOK, D).T),
        "wk0": chunked(per_head(wkv[:D]).T), "wv0": chunked(wkv[D:].T),
        "bk0": column(per_head(bkv[:D])),
        "bq": row("L0_xattn_bq"), "bv": bkv[D:].reshape(1, D), "bp": row("L0_xattn_bp"),
        "wscale": row("L1_ffn_w_scale"), "fbias": row("L1_ffn_bias"), "rbias": row("L0_ffn_bias_corr"),
        "gate": chunked(np.asarray(a["L0_ffn_gate_w"]).T),
        "sup": chunked(np.asarray(a["L0_ffn_shared_up_w"]).T),
        "sdown": chunked(np.asarray(a["L0_ffn_shared_down_w"]).T),
        "we": np.concatenate([up.reshape(EXPERTS, P, D), down], axis=2),
        "wq1": chunked(per_head(a["L1_attn_wq"]).T), "wk1": chunked(per_head(a["L1_attn_wk"], 2).T),
        "wv1": chunked(wv1.T), "wo1": chunked(np.asarray(a["L1_attn_wo"]).T),
        "wf8": chunked(np.asarray(a["L1_ffn_weight"]).T).view(np.int32),
        "decay": column(a["L1_xattn_w"]), "bonus": column(a["L1_xattn_u"]),
        "ident": np.eye(P, dtype=np.float32), "ones": np.ones((P, P), np.float32),
        "before": (r[:, None] < r[None, :]).astype(np.float32),
        "lo_rows": np.where(r % 32 >= HD, -1.0, 0.0).astype(np.float32).reshape(P, 1),
        "pick": np.repeat(pick[:, :, None], P, axis=2).astype(np.float32),
        "half_pow": np.full((P, BATCH), -0.5, np.float32),
        "iota_e": np.tile(np.arange(EXPERTS, dtype=np.float32), (P, 1)),
        "lower_g": np.tile(np.tril(np.ones((EGROUPS, EGROUPS), np.float32), -1), (P, 1, 1)),
    }
    return {k: np.ascontiguousarray(v) for k, v in out.items()}


def kernel(**inputs):
    import concourse.bacc as bacc
    from concourse.bass_utils import run_bass_kernel_spmd

    arrays = _layouts(inputs)
    nc = bacc.Bacc("TRN2", target_bir_lowering=False, num_devices=1)
    t = {n: nc.dram_tensor(f"in_{n}", a.shape, mybir.dt.from_np(a.dtype), kind="ExternalInput").ap()
         for n, a in arrays.items()}
    t["out"] = nc.dram_tensor("out", (BATCH, SEQ, D), F32, kind="ExternalOutput").ap()
    build(nc, t)
    result = run_bass_kernel_spmd(nc, [{f"in_{n}": a for n, a in arrays.items()}], core_ids=[0])
    return result.results[0]["out"]
```

```python
from contextlib import ExitStack

import numpy as np

import concourse.bass as bass
from concourse import mybir

F32 = mybir.dt.float32
F32R = mybir.dt.float32r
BF16 = mybir.dt.bfloat16
F16 = mybir.dt.float16
U32 = mybir.dt.uint32
I8 = mybir.dt.int8
I32 = mybir.dt.int32
ALU = mybir.AluOpType
ACT = mybir.ActivationFunctionType
AX = mybir.AxisListType

P = 128
BATCH, SEQ, D = 8, 128, 256
KC = D // P
TOK = BATCH * SEQ
PAIRS = BATCH // 2
HEADS, HD = 16, 16
GROUPS = 4
CH = HEADS // GROUPS
VC = HD + 1
EXPERTS, TOPK, CAP, HID = 32, 4, 128, 128
EGROUPS, KEPT_GROUPS = 8, 4
EPG = EXPERTS // EGROUPS
SHARED = 512
SC = SHARED // P
ROUTE_SCALE = 2.5
LN_EPS = 1e-5
ROUND = 12582912.0
NEG_BIG = -1e38
SKIP = 8192.0
ATT_SCALE = HD ** -0.5

L0_MATS = ("w_f", "w_i", "w_v", "w_q", "w_gate", "w_up", "w_ro", "w_down")


def named(**parts):
    return type("Named", (), parts)


def build(nc, t):
    ctx = ExitStack()
    with ctx:
        def sb(name, shape, dt=F32):
            return ctx.enter_context(nc.sbuf_tensor(name, shape, dt))

        def sems(prefix, names):
            return named(**{n: ctx.enter_context(nc.semaphore(f"{prefix}_{n}"))
                                      for n in names.split()})

        def views(buffer):
            at = 0

            def take(shape):
                nonlocal at
                size = int(np.prod(shape[1:]))
                part = buffer[:, at:at + size]
                at += size
                names = "abcd"[:len(shape) - 1]
                if len(names) == 1:
                    return part
                return part.rearrange(f"p ({' '.join(names)}) -> p {' '.join(names)}",
                                      **{n: int(k) for n, k in zip(names, shape[1:])})
            return take

        ident = sb("ident", [P, P])
        identb = sb("identb", [P, P], BF16)
        ones = sb("ones", [P, P])
        onesb = sb("onesb", [P, P], BF16)
        before = sb("before", [P, P], BF16)
        head_rows = sb("head_rows", [P, HEADS // KC])
        half_pow = sb("half_pow", [P, BATCH])
        iota_e = sb("iota_e", [P, EXPERTS])
        lower_g = sb("lower_g", [P, EGROUPS, EGROUPS])
        scratch = sb("scratch", [P, 36 * 256])
        w0_flat = sb("w0", [P, KC * len(L0_MATS) * D])
        w0 = w0_flat[:, :].rearrange("p (k m n) -> p k m n", k=KC, m=len(L0_MATS))
        init4 = sb("init4", [P, KC])
        wk0 = sb("wk0", [P, KC, D])
        wv0 = sb("wv0", [P, KC, D])
        bk0, bq0 = sb("bk0", [P, KC]), sb("bq0", [P, KC])
        rows = sb("rows", [P, 4, D])
        bv, bp, wscale, fbias = (rows[:, i, :] for i in range(4))
        rbias = sb("rbias", [P, EXPERTS])
        wq1 = sb("wq1", [P, KC, D])
        wk1 = sb("wk1", [P, KC, D])
        wv1 = sb("wv1", [P, KC, D])
        wo1 = sb("wo1", [P, KC, D])
        gate = sb("gate", [P, KC, EXPERTS])
        sup = sb("sup", [P, KC, SHARED])
        sdown = sb("sdown", [P, SC, D])
        decay = sb("decay", [P, KC])
        bonus = sb("bonus", [P, KC])
        wf8 = sb("wf8", [P, KC, D // 4], I32)
        wfb = sb("wfb", [P, KC, D], BF16)
        ctxT = sb("ctxT", [P, KC, TOK])
        x_sb = sb("x_sb", [P, BATCH, D])

        h3_flat = sb("h3", [P, BATCH * D])
        hT3_flat = sb("hT3", [P, KC * TOK])
        take = views(h3_flat)
        beforef = take([P, P])

        qw = take([P, 2, KC, D])
        qw_s = sb("qw_s", [P, 2, KC])
        qw_r = sb("qw_r", [P, 2, KC])
        take = views(hT3_flat)
        qw_i, qw_diag = take([P, 2, KC, D]), take([P, 2 * KC, P])
        qw_b = sb("qw_b", [P, 2, KC, D], BF16)
        qwT = sb("qwT", [P, 2, KC, D], BF16)
        qw_row = sb("qw_row", [P, 2, D])

        bank = [ctx.enter_context(nc.psum_tensor(f"bank{i}", [P, 512], F32)) for i in range(8)]

        ld = sems("ld", "x const w0 kv0 rows qw l1 moe")
        cst = sems("cst", "ident small vones wfb")
        qs = sems("qw", "scale i b T row diag evacT evacrow")

        LN = sems("ln", "stats mv ve rstd h")
        ln_st = sb("ln_st", [P, 6 * BATCH, 6])
        ln_mv = sb("ln_mv", [P, 6 * BATCH, 2])
        ln_ve, ln_rstd = sb("ln_ve", [P, 6 * BATCH]), sb("ln_rstd", [P, 6 * BATCH])

        def dve_stats(v, n, b):
            i = n * BATCH + b
            v.bn_stats(ln_st[:, i, :], x_sb[:, b, :]).then_inc(LN.stats, 1)
            v.wait_ge(LN.stats, i + 1)
            v.bn_aggr(ln_mv[:, i, :], ln_st[:, i, :]).then_inc(LN.mv, 1)

        def pool_rstd(g, n, b):
            i = n * BATCH + b
            g.wait_ge(LN.mv, i + 1)
            g.tensor_scalar(ln_ve[:, i:i + 1], ln_mv[:, i, 1:2], LN_EPS, None, ALU.add).then_inc(LN.ve, 1)
            g.wait_ge(LN.ve, i + 1)
            g.tensor_tensor(ln_rstd[:, i:i + 1], ln_ve[:, i:i + 1], half_pow[:, 0:1], ALU.pow).then_inc(LN.rstd, 1)

        def dve_norm(v, n, b, out):
            i = n * BATCH + b
            v.wait_ge(LN.rstd, i + 1)
            v.tensor_scalar(out, x_sb[:, b, :], ln_mv[:, i, 0:1], ln_rstd[:, i:i + 1],
                            ALU.subtract, ALU.mult).then_inc(LN.h, 1)

        def quant_buffers(name):
            return named(am=sb(f"{name}_am", [P, 2 * BATCH]), s=sb(f"{name}_s", [P, 2 * BATCH]),
                                   r=sb(f"{name}_r", [P, 2 * BATCH]), i=sb(f"{name}_i", [P, D]),
                                   q=sb(f"{name}_q", [P, 2, D], BF16),
                                   sem=sems(name, "step q"))

        def dve_quant(v, z, b, src, least, free_q):
            v.tensor_reduce(z.am[:, b:b + 1], src, AX.X, ALU.max, apply_absolute_value=True).then_inc(z.sem.step, 1)
            v.wait_ge(z.sem.step, 4 * b + 1)
            v.tensor_scalar(z.s[:, b:b + 1], z.am[:, b:b + 1], 1.0 / 127.0, least,
                            ALU.mult, ALU.max).then_inc(z.sem.step, 1)
            v.wait_ge(z.sem.step, 4 * b + 2)
            v.reciprocal(z.r[:, b:b + 1], z.s[:, b:b + 1]).then_inc(z.sem.step, 1)
            v.wait_ge(z.sem.step, 4 * b + 3)
            v.tensor_scalar(z.i[:, :], src, z.r[:, b:b + 1], ROUND, ALU.mult, ALU.add).then_inc(z.sem.step, 1)
            v.wait_ge(z.sem.step, 4 * b + 4)
            free_q()
            v.tensor_scalar(z.q[:, b % 2, :], z.i[:, :], -ROUND, None, ALU.add).then_inc(z.sem.q, 1)

        A = sems("a", "hT hTs F I V Q G U tf ti tv tg av b4 fix zero st z tz r gg u2 y res init4")
        take = views(scratch)
        a_h = take([P, 2, 2, D])
        a_hT = take([P, 2, KC, D])
        a_tf, a_ti, a_tv, a_tg, a_av, a_b4, a_st, a_z, a_tz, a_gg = (
            take([P, KC, D]) for _ in range(10))
        a_r = take([P, KC, D])
        a_u2 = take([P, KC, D])
        A_OUT = {"F": 1, "I": 2, "V": 3, "Q": 4, "G": 5, "U": 6}

        def psA(n):
            return bank[n][:, :].rearrange("p (c n) -> p c n", c=KC)

        def pe_a_transpose(pe, p):
            for i in range(2):
                pe.wait_ge(LN.h, 2 * p + i + 1)
            if p >= 1:
                pe.wait_ge(A.hTs, p)
            for i in range(2):
                for c in range(KC):
                    mm = pe.transpose(psA(0)[:, c, i * P:(i + 1) * P],
                                      a_h[:, p % 2, i, c * P:(c + 1) * P], ident[:, :])
            mm.then_inc(A.hT, 1)

        def pe_a_project(pe, p):
            pe.wait_ge(A.hTs, p + 1)
            for name, mat, free in (("F", 0, A.tf), ("I", 1, A.ti), ("V", 2, A.av), ("Q", 3, A.z),
                                    ("G", 4, A.gg), ("U", 5, A.u2)):
                if p >= 1:
                    pe.wait_ge(free, p)
                for c in range(KC):
                    for k in range(KC):
                        mm = pe.matmul(psA(A_OUT[name])[:, c, :], w0[:, k, mat, c * P:(c + 1) * P],
                                       a_hT[:, p % 2, k, :], start=(k == 0), stop=(k == KC - 1))
                mm.then_inc({"F": A.F, "I": A.I, "V": A.V, "Q": A.Q, "G": A.G, "U": A.U}[name], 1)

        def pe_a_down(pe, p):
            if p >= 1:
                pe.wait_ge(A.res, p)
            pe.wait_ge(A.r, p + 1)
            pe.wait_ge(A.u2, p + 1)
            for i in range(2):
                for n, (src, mat) in enumerate(((a_r, 6), (a_u2, 7))):
                    for k in range(KC):
                        mm = pe.matmul(psA(7)[:, i, :], src[:, k, i * P:(i + 1) * P], w0[:, k, mat, :],
                                       start=(n == 0 and k == 0), stop=(n == 1 and k == KC - 1))
            mm.then_inc(A.y, 1)

        def act_a(act, p):
            act.wait_ge(A.hT, p + 1)
            if p >= 2:
                act.wait_ge(A.U, p - 1)
            act.copy(a_hT[:, p % 2], psA(0)).then_inc(A.hTs, 1)
            act.wait_ge(A.F, p + 1)
            if p >= 1:
                act.wait_ge(A.st, p)
            act.activation(a_tf[:], psA(1), ACT.Tanh).then_inc(A.tf, 1)
            act.wait_ge(A.I, p + 1)
            if p >= 1:
                act.wait_ge(A.b4, p)
            act.activation(a_ti[:], psA(2), ACT.Tanh, scale=0.5).then_inc(A.ti, 1)
            act.wait_ge(A.V, p + 1)
            if p >= 1:
                act.wait_ge(A.av, p)
            act.activation(a_tv[:], psA(3), ACT.Tanh, scale=0.5).then_inc(A.tv, 1)
            act.wait_ge(A.z, p + 1)
            if p >= 1:
                act.wait_ge(A.r, p)
            act.activation(a_tz[:], a_z[:], ACT.Tanh, scale=0.5).then_inc(A.tz, 1)
            act.wait_ge(A.G, p + 1)
            if p >= 1:
                act.wait_ge(A.gg, p)
            act.activation(a_tg[:], psA(5), ACT.Tanh, scale=0.5).then_inc(A.tg, 1)

        def dve_a_norm(v, p):
            for i in range(2):
                b = 2 * p + i
                if p >= 2:
                    v.wait_ge(A.hT, p - 1)
                dve_norm(v, 0, b, a_h[:, p % 2, i, :])

        def dve_a(v, p):
            v.wait_ge(A.tv, p + 1)
            v.scalar_tensor_tensor(out=a_av[:], in0=a_tv[:], scalar=1.0, in1=psA(3),
                                   op0=ALU.add, op1=ALU.mult).then_inc(A.av, 1)
            v.wait_ge(A.av, p + 1)
            v.wait_ge(A.ti, p + 1)
            v.scalar_tensor_tensor(out=a_b4[:], in0=a_ti[:], scalar=1.0, in1=a_av[:],
                                   op0=ALU.add, op1=ALU.mult).then_inc(A.b4, 1)
            v.wait_ge(A.b4, p + 1)
            v.wait_ge(A.tf, p + 1)
            for c in range(KC):
                v.scalar_tensor_tensor(out=a_b4[:, c, ::SEQ], in0=a_tf[:, c, ::SEQ], scalar=init4[:, c:c + 1],
                                       in1=a_b4[:, c, ::SEQ], op0=ALU.mult, op1=ALU.add).then_inc(A.fix, 1)
            v.wait_ge(A.fix, KC * (p + 1))
            v.memset(a_tf[:, :, ::SEQ], 0.0).then_inc(A.zero, 1)
            v.wait_ge(A.zero, p + 1)
            v.tensor_tensor_scan(a_st[:].rearrange("p c n -> p (c n)"), a_tf[:].rearrange("p c n -> p (c n)"),
                                 a_b4[:].rearrange("p c n -> p (c n)"), 0.0, ALU.mult, ALU.add).then_inc(A.st, 1)
            v.wait_ge(A.st, p + 1)
            v.wait_ge(A.Q, p + 1)
            if p >= 1:
                v.wait_ge(A.tz, p)
            v.scalar_tensor_tensor(out=a_z[:], in0=psA(4), scalar=0.25, in1=a_st[:],
                                   op0=ALU.mult, op1=ALU.mult).then_inc(A.z, 1)
            v.wait_ge(A.tz, p + 1)
            if p >= 1:
                v.wait_ge(A.y, p)
            v.scalar_tensor_tensor(out=a_r[:], in0=a_tz[:], scalar=1.0, in1=a_z[:],
                                   op0=ALU.add, op1=ALU.mult).then_inc(A.r, 1)
            v.wait_ge(A.tg, p + 1)
            v.scalar_tensor_tensor(out=a_gg[:], in0=a_tg[:], scalar=1.0, in1=psA(5),
                                   op0=ALU.add, op1=ALU.mult).then_inc(A.gg, 1)
            v.wait_ge(A.gg, p + 1)
            v.wait_ge(A.U, p + 1)
            v.tensor_tensor(a_u2[:], a_gg[:], psA(6), ALU.mult).then_inc(A.u2, 1)

        def dve_a_residual(v, p):
            v.wait_ge(A.y, p + 1)
            v.scalar_tensor_tensor(out=x_sb[:, 2 * p:2 * p + 2, :], in0=psA(7), scalar=0.5,
                                   in1=x_sb[:, 2 * p:2 * p + 2, :], op0=ALU.mult, op1=ALU.add).then_inc(A.res, 1)

        att = named(
            kf=sb("t_kf", [P, KC, P]), km=sb("t_km", [P, 2, HEADS, P]), qT=sb("t_qT", [P, 2, KC, P]),
            v1=sb("t_v1", [P, 3, HEADS, VC]), nm=sb("t_nm", [P, 2, HEADS]),
            pb=sb("t_pb", [P, 2, CH, P]), pt=sb("t_pt", [P, 2, CH, P]),
            rs=sb("t_rs", [P, HEADS]), o=sb("t_o", [P, 2, D]),
            hT=sb("t_hT", [P, 2, KC, P]), hTb=sb("t_hTb", [P, 2, KC, P], BF16),
            oT=sb("t_oT", [P, KC, P]), oTb=sb("t_oTb", [P, KC, P], BF16), h=sb("t_h", [P, 2, D]),
            q1=sb("t_q1", [P, D]), y=sb("t_y", [P, D]))
        T = sems("att", "hTp hT K kf km0 km1 Vp v1 Qp q1 QT qT S nm P PTp pt O rs o oTp oT y yt xb res")
        BLOCKS = GROUPS * BATCH

        def bank4(n):
            return bank[n][:, :].rearrange("p (c n) -> p c n", c=CH)

        def kbank(n):
            return bank[n][:, 0:D].rearrange("p (c n) -> p c n", c=KC)

        def o_bank():
            return bank[4][:, 0:HEADS * VC].rearrange("p (h d) -> p h d", h=HEADS)

        def pe_scores(pe, n):
            b, j = divmod(n, GROUPS)
            if j == 0:
                pe.wait_ge(T.qT, 2 * (b + 1))
                pe.wait_ge(T.km0, b + 1)
            if j == GROUPS // 2:
                pe.wait_ge(T.km1, b + 1)
            if n >= 2:
                pe.wait_ge(T.P, CH * (n - 1))
            pe.matmul(bank4(n % 2), att.qT[:, b % 2, j // 2, :], att.km[:, b % 2, CH * j:CH * (j + 1), :],
                      start=True, stop=True).then_inc(T.S, 1)

        def pe_turn(pe, n):
            pe.wait_ge(T.P, CH * (n + 1))
            if n >= 2:
                pe.wait_ge(T.pt, n - 1)
            for i in range(CH):
                mm = pe.transpose(bank4(2 + n % 2)[:, i, :], att.pb[:, n % 2, i, :], ident[:, :])
            mm.then_inc(T.PTp, 1)

        def pe_values(pe, n):
            b, j = divmod(n, GROUPS)
            pe.wait_ge(T.pt, n + 1)
            if j == 0:
                pe.wait_ge(T.v1, b + 1)
                if b >= 1:
                    pe.wait_ge(T.o, b)
            for i in range(CH):
                mm = pe.matmul(o_bank()[:, CH * j + i, :], att.pt[:, n % 2, i, :], att.v1[:, b % 3, CH * j + i, :],
                               start=True, stop=True)
            mm.then_inc(T.O, 1)

        def pe_blocks(pe, s, phase, extra):
            for j in range(GROUPS):
                t = GROUPS * (s - 1) + j
                if 0 <= t < BLOCKS:
                    pe_scores(pe, BLOCKS * phase + t)
                extra(j)
                if 0 <= t - 1 < BLOCKS:
                    pe_turn(pe, BLOCKS * phase + t - 1)
                if 0 <= t - 2 < BLOCKS:
                    pe_values(pe, BLOCKS * phase + t - 2)

        def act_exp(act, n):
            b, j = divmod(n, GROUPS)
            act.wait_ge(T.nm, n + 1)
            if n >= 2:
                act.wait_ge(T.PTp, n - 1)
            for i in range(CH):
                h = CH * j + i
                act.activation(att.pb[:, n % 2, i, :], bank4(n % 2)[:, i, :], ACT.Exp,
                               bias=att.nm[:, b % 2, h:h + 1]).then_inc(T.P, 1)

        def act_turned(act, n):
            act.wait_ge(T.PTp, n + 1)
            if n >= 2:
                act.wait_ge(T.O, n - 1)
            act.copy(att.pt[:, n % 2], bank4(2 + n % 2)).then_inc(T.pt, 1)

        def act_blocks(act, s, phase, extra):
            for j in range(GROUPS):
                t = GROUPS * (s - 1) + j
                if 0 <= t < BLOCKS:
                    act_exp(act, BLOCKS * phase + t)
                extra(j)
                if 0 <= t - 1 < BLOCKS:
                    act_turned(act, BLOCKS * phase + t - 1)

        def dve_rowmax(v, s, phase, j):
            t = GROUPS * (s - 1) + j
            if 0 <= t < BLOCKS:
                n = BLOCKS * phase + t
                b = n // GROUPS
                v.wait_ge(T.S, n + 1)
                if j == 0 and b >= 2:
                    v.wait_ge(T.P, HEADS * (b - 1))
                v.tensor_reduce(att.nm[:, b % 2, CH * j:CH * (j + 1)], bank4(n % 2), AX.X, ALU.max,
                                negate=True).then_inc(T.nm, 1)

        def key_copies(e, b, c, done):
            full = [P, HEADS // KC, P]
            e.wait_ge(T.kf, b + 1)
            if b >= 2:
                e.wait_ge(T.S, GROUPS * (b - 1))
            e.tensor_tensor(att.km[:, b % 2, c * (HEADS // KC):(c + 1) * (HEADS // KC), :],
                            att.kf[:, c, :].unsqueeze(1).to_broadcast(full),
                            head_rows[:, :].unsqueeze(2).to_broadcast(full), ALU.mult).then_inc(done, 1)

        def dve_attended(v, b, free):
            v.wait_ge(T.O, GROUPS * (b + 1))
            v.reciprocal(att.rs[:, :], o_bank()[:, :, HD]).then_inc(T.rs, 1)
            v.wait_ge(T.rs, b + 1)
            free()
            v.tensor_tensor(att.o[:, b % 2].rearrange("p (h d) -> p h d", h=HEADS), o_bank()[:, :, 0:HD],
                            att.rs[:, :].unsqueeze(2).to_broadcast([P, HEADS, HD]), ALU.mult).then_inc(T.o, 1)

        zq = quant_buffers("zq")
        zo = quant_buffers("zo")

        def pe_b_step(pe, s):
            b, o = s, s - 3
            def extra(j):
                if j == 0 and b < BATCH:
                    pe.wait_ge(zq.sem.q, b + 1)
                    if b >= 1:
                        pe.wait_ge(T.v1, b)
                    for k in range(KC):
                        mm = pe.transpose(bank[6][:, 0:P].bitcast(BF16).rearrange("p (k n) -> p k n", k=KC)[:, k, :],
                                          zq.q[:, b % 2, k * P:(k + 1) * P], identb[:, :])
                    mm.then_inc(T.hTp, 1)
                    if b >= 1:
                        pe.wait_ge(T.qT, 2 * b)
                    for c in range(KC):
                        for k in range(KC):
                            mm = pe.matmul(kbank(5)[:, c, :], wk0[:, k, c * P:(c + 1) * P],
                                           ctxT[:, k, b * P:(b + 1) * P], start=(k == 0), stop=(k == KC - 1))
                    mm.then_inc(T.K, 1)
                    pe.wait_ge(T.hT, b + 1)
                    if o >= 1:
                        pe.wait_ge(T.yt, o)
                    for k in range(KC):
                        mm = pe.matmul(bank[7][:, 0:D], att.hTb[:, b % 2, k, :], qwT[:, 0, k, :],
                                       start=(k == 0), stop=(k == KC - 1))
                    mm.then_inc(T.Qp, 1)
                if j == 1 and o >= 0:
                    pe.wait_ge(zo.sem.q, o + 1)
                    if b < BATCH:
                        pe.wait_ge(T.q1, b + 1)
                    elif o >= 1:
                        pe.wait_ge(T.yt, o)
                    for k in range(KC):
                        mm = pe.transpose(bank[7][:, 0:P].bitcast(BF16).rearrange("p (k n) -> p k n", k=KC)[:, k, :],
                                          zo.q[:, o % 2, k * P:(k + 1) * P], identb[:, :])
                    mm.then_inc(T.oTp, 1)
                if j == 1 and b < BATCH:
                    pe.wait_ge(T.hT, b + 1)
                    for k in range(KC):
                        mm = pe.matmul(bank[6][:, 0:D], ctxT[:, k, b * P:(b + 1) * P], wv0[:, k, :],
                                       start=(k == 0), stop=(k == KC - 1))
                    mm.then_inc(T.Vp, 1)
                if j == 2 and o >= 0:
                    pe.wait_ge(T.oT, o + 1)
                    for k in range(KC):
                        mm = pe.matmul(bank[7][:, 0:D], att.oTb[:, k, :], qwT[:, 1, k, :],
                                       start=(k == 0), stop=(k == KC - 1))
                    mm.then_inc(T.y, 1)
                if j == 2 and b < BATCH:
                    pe.wait_ge(T.q1, b + 1)
                    pe.wait_ge(T.kf, b + 1)
                    for c in range(KC):
                        mm = pe.transpose(kbank(5)[:, c, :], att.q1[:, c * P:(c + 1) * P], ident[:, :])
                    mm.then_inc(T.QT, 1)

            pe_blocks(pe, s, 0, extra)

        def act_b_step(act, s):
            b, o = s, s - 3
            if b < BATCH:
                act.wait_ge(T.hTp, b + 1)
                if b >= 2:
                    act.wait_ge(T.Qp, b - 1)
                act.copy(att.hTb[:, b % 2], bank[6][:, 0:P].bitcast(BF16).rearrange("p (k n) -> p k n", k=KC))\
                   .then_inc(T.hT, 1)

            def extra(j):
                if j == 1 and o >= 0:
                    act.wait_ge(T.oTp, o + 1)
                    if o >= 1:
                        act.wait_ge(T.y, o)
                    act.copy(att.oTb[:], bank[7][:, 0:P].bitcast(BF16).rearrange("p (k n) -> p k n", k=KC))\
                       .then_inc(T.oT, 1)

            act_blocks(act, s, 0, extra)

        def dve_b_stats(v, b):
            if b % 2 == 0:
                v.wait_ge(A.res, b // 2 + 1)
            dve_stats(v, 1, b)

        def dve_b_prep(v, b):
            dve_norm(v, 1, b, att.h[:, b % 2, :])
            v.wait_ge(LN.h, 1 * BATCH + b + 1)

            def free():
                if b >= 2:
                    v.wait_ge(T.hTp, b - 1)
            dve_quant(v, zq, b, att.h[:, b % 2, :], 1e-8, free)

        def dve_b_step(v, s):
            b, a, o = s, s - 2, s - 3
            dve_rowmax(v, s, 0, 0)
            if b < BATCH:
                v.wait_ge(T.K, b + 1)
                if b >= 1:
                    v.wait_ge(T.km0, b)
                    v.wait_ge(T.km1, b)
                v.tensor_tensor(att.kf[:], kbank(5), bk0[:, :].unsqueeze(2).to_broadcast([P, KC, P]),
                                ALU.add).then_inc(T.kf, 1)
                v.wait_ge(T.Qp, b + 1)
                if b >= 1:
                    v.wait_ge(T.QT, b)
                v.scalar_tensor_tensor(out=att.q1[:], in0=bank[7][:, 0:D], scalar=zq.s[:, b:b + 1],
                                       in1=qw_row[:, 0, :], op0=ALU.mult, op1=ALU.mult).then_inc(T.q1, 1)
            dve_rowmax(v, s, 0, 1)
            if b + 1 < BATCH:
                dve_b_stats(v, b + 1)
            if b < BATCH:
                key_copies(v, b, 0, T.km0)
                v.wait_ge(T.Vp, b + 1)
                if b >= 3:
                    v.wait_ge(T.O, GROUPS * (b - 2))
                v.tensor_tensor(att.v1[:, b % 3, :, 0:HD], bank[6][:, 0:D].rearrange("p (h d) -> p h d", h=HEADS),
                                bv.rearrange("p (h d) -> p h d", h=HEADS), ALU.add).then_inc(T.v1, 1)
            if 0 <= a < BATCH:
                dve_attended(v, a, lambda: None)
            dve_rowmax(v, s, 0, 2)
            if o >= 0:
                v.wait_ge(T.y, o + 1)
                if o >= 1:
                    v.wait_ge(T.res, o)
                v.scalar_tensor_tensor(out=att.y[:], in0=bank[7][:, 0:D], scalar=zo.s[:, o:o + 1],
                                       in1=qw_row[:, 1, :], op0=ALU.mult, op1=ALU.mult).then_inc(T.yt, 1)
                v.wait_ge(T.yt, o + 1)
                v.wait_ge(T.xb, o + 1)
                v.tensor_tensor(x_sb[:, o, :], x_sb[:, o, :], att.y[:], ALU.add).then_inc(T.res, 1)
            if b < BATCH:
                v.wait_ge(T.QT, b + 1)
                if b >= 2:
                    v.wait_ge(T.S, GROUPS * (b - 1))
                for c in range(KC):
                    v.tensor_scalar(att.qT[:, b % 2, c, :], kbank(5)[:, c, :], bq0[:, c:c + 1], ATT_SCALE,
                                    ALU.add, ALU.mult).then_inc(T.qT, 1)
            if b + 1 < BATCH:
                dve_b_prep(v, b + 1)
            dve_rowmax(v, s, 0, 3)
            if 0 <= a < BATCH:
                v.wait_ge(T.o, a + 1)

                def free():
                    if a >= 2:
                        v.wait_ge(T.oTp, a - 1)
                dve_quant(v, zo, a, att.o[:, a % 2], 1e-8, free)

        def pool_b_step(g, s):
            g.wait_ge(LN.h, 1 * BATCH + s + 1)
            g.tensor_tensor(x_sb[:, s, :], x_sb[:, s, :], bp, ALU.add).then_inc(T.xb, 1)
            key_copies(g, s, 1, T.km1)
            if s + 1 < BATCH:
                pool_rstd(g, 1, s + 1)

        C = sems("c", "hTp hT lg ex route top idx sel pos srow grow zeroed scat sup_ rel sq sdn shy "
                      "xT xTs up hr h2 dn ye acc "
                      "in0 in1 in2 in3 in4 in5 in6 in7 out0 out1 out2 out3 gat0 gat1")
        h3 = views(h3_flat)([P, BATCH, D])
        hT3 = views(hT3_flat)([P, KC, TOK])
        BE = [P, BATCH, EXPERTS]
        BKE = [P, BATCH * TOPK, EXPERTS]
        take = views(scratch)
        c_ex, c_sg, c_sc, c_ms, c_ms0 = (take(BE) for _ in range(5))
        c_mx, c_mn = (take([P, BATCH * EGROUPS, 2]) for _ in range(2))
        c_hi, c_lo, c_m3, c_sec, c_gs, c_rk, c_mk = (
            take([P, BATCH * EGROUPS]) for _ in range(7))
        c_gt, c_eq, c_eql, c_rk1 = (take([P, BATCH * EGROUPS, EGROUPS]) for _ in range(4))
        c_top = sb("c_top", [P, BATCH, 8])
        c_idx = sb("c_idx", [P, BATCH, 8], U32)
        c_idxf = sb("c_idxf", [P, BATCH, TOPK])
        c_oh = take(BKE)
        c_tmp, c_tmp2 = take(BKE), take(BKE)
        c_sel = sb("c_sel", BE, BF16)
        c_w4, c_p4, c_ok, c_wv, c_drop, c_row = (sb(f"c_{n}", [P, BATCH, TOPK]) for n in "w4 p4 ok wv drop row".split())
        c_pc = sb("c_pc", [P, BATCH, TOPK])
        c_ws, c_wr = sb("c_ws", [P, BATCH]), sb("c_wr", [P, BATCH])
        c_srow, c_grow = sb("c_srow", [P, BATCH, TOPK], U32), sb("c_grow", [P, BATCH, TOPK], U32)
        RING, OUT_RING = 8, 4
        e_xT, e_y = take([P, 2, KC, P]), take([P, OUT_RING, D])
        e_r, e_h = take([P, 2, P]), take([P, 2, P])
        e_x = sb("e_x", [P, RING, D])
        e_w = sb("e_w", [P, RING, 2 * D])
        e_in = (C.in0, C.in1, C.in2, C.in3, C.in4, C.in5, C.in6, C.in7)
        e_out = (C.out0, C.out1, C.out2, C.out3)
        gat = (C.gat0, C.gat1)
        zrow = sb("zrow", [P, 1024])
        take = views(w0_flat)
        c_sr, c_sT = take([P, SC, 512]), take([P, SC, 512])
        g_y = views(w0_flat)([P, 2, TOPK, D])
        xe_dram = nc.dram_tensor("xe_dram", [EXPERTS * CAP, D], F32).ap()
        ye_dram = nc.dram_tensor("ye_dram", [EXPERTS * CAP, D], F32).ap()
        bg = "p (b g) -> p b g"

        def pe_c(pe):
            for b in range(BATCH):
                pe.wait_ge(LN.h, 2 * BATCH + b + 1)
                if b >= 2:
                    pe.wait_ge(C.hT, b - 1)
                else:
                    pe.wait_ge(T.P, HEADS * BATCH)
                for k in range(KC):
                    mm = pe.transpose(bank[b % 2][:, k * P:(k + 1) * P], h3[:, b, k * P:(k + 1) * P], ident[:, :])
                mm.then_inc(C.hTp, 1)
            for b in range(BATCH):
                pe.wait_ge(C.hT, b + 1)
                if b == 0:
                    pe.wait_ge(T.pt, BLOCKS)
                for k in range(KC):
                    mm = pe.matmul(bank[2][:, b * EXPERTS:(b + 1) * EXPERTS], hT3[:, k, b * P:(b + 1) * P],
                                   gate[:, k, :], start=(k == 0), stop=(k == KC - 1))
            mm.then_inc(C.lg, 1)

        def pe_c_up(pe, half):
            for m in range(SC):
                n = SC * half + m
                if n < 2:
                    pe.wait_ge(C.hT, BATCH)
                else:
                    pe.wait_ge(C.rel, n - 1)
                for k in range(KC):
                    mm = pe.matmul(bank[n % 2][:, :], sup[:, k, m * P:(m + 1) * P],
                                   hT3[:, k, half * 512:(half + 1) * 512], start=(k == 0), stop=(k == KC - 1))
                mm.then_inc(C.sup_, 1)

        def pe_c_down(pe, half):
            pe.wait_ge(C.sq, SC * (half + 1))
            for i in range(4):
                b = 4 * half + i
                for m in range(SC):
                    mm = pe.matmul(bank[4 + b // 2][:, (b % 2) * D:(b % 2 + 1) * D], c_sT[:, m, i * P:(i + 1) * P], sdown[:, m, :],
                                   start=(m == 0), stop=(m == SC - 1))
                mm.then_inc(C.sdn, 1)

        def pe_c_pos(pe):
            pe.wait_ge(C.sel, 1)
            pe.wait_ge(C.ex, 1)
            out = bank[3][:, 0:BATCH * EXPERTS]
            for b in range(BATCH - 1):
                rest = BATCH - 1 - b
                pe.matmul(out[:, (b + 1) * EXPERTS:].rearrange("p (b e) -> p b e", b=rest), onesb[:, :],
                          c_sel[:, b, :].unsqueeze(1).to_broadcast([P, rest, EXPERTS]),
                          start=(b == 0), stop=False, skip_group_check=True)
            pe.matmul(out[:, EXPERTS:], before[:, :], c_sel[:, 1:, :].rearrange("p b e -> p (b e)"),
                      start=False, stop=True, skip_group_check=True)
            mm = pe.matmul(out[:, 0:EXPERTS], before[:, :], c_sel[:, 0, :], start=True, stop=True)
            mm.then_inc(C.pos, 1)

        def pe_x_transpose(pe, e):
            pe.wait_ge(e_in[e % RING], 32 * (e // RING + 1))
            if e >= 2:
                pe.wait_ge(C.xTs, e - 1)
            for k in range(KC):
                mm = pe.transpose(bank[e % 2][:, k * P:(k + 1) * P], e_x[:, e % RING, k * P:(k + 1) * P], ident[:, :])
            mm.then_inc(C.xT, 1)

        def pe_x_up(pe, e):
            pe.wait_ge(C.xTs, e + 1)
            if e >= 2:
                pe.wait_ge(C.hr, e - 1)
            for k in range(KC):
                mm = pe.matmul(bank[2 + e % 2][:, 0:P], e_w[:, e % RING, k * HID:(k + 1) * HID],
                               e_xT[:, e % 2, k, :], start=(k == 0), stop=(k == KC - 1))
            mm.then_inc(C.up, 1)

        def pe_x_down(pe, e):
            pe.wait_ge(C.h2, e + 1)
            if e < 2:
                pe.wait_ge(C.shy, e + 1)
            if e >= 2:
                pe.wait_ge(C.ye, e - 1)
            pe.matmul(bank[4 + e % 2][:, 0:D], e_h[:, e % 2, :], e_w[:, e % RING, D:2 * D],
                      start=True, stop=True).then_inc(C.dn, 1)

        def act_c(act):
            for b in range(BATCH):
                act.wait_ge(C.hTp, b + 1)
                act.copy(hT3[:, :, b * P:(b + 1) * P], bank[b % 2][:, 0:D].rearrange("p (k n) -> p k n", k=KC))\
                   .then_inc(C.hT, 1)
            act.wait_ge(C.lg, 1)
            act.activation(c_ex[:].rearrange("p b e -> p (b e)"), bank[2][:, 0:BATCH * EXPERTS], ACT.Exp, scale=-1.0)\
               .then_inc(C.ex, 1)

        def act_c_shared(act, half):
            for m in range(SC):
                n = SC * half + m
                act.wait_ge(C.sup_, n + 1)
                if half:
                    act.wait_ge(C.sq, n - SC + 1)
                act.activation(c_sr[:, m, :], bank[n % 2][:, :], ACT.Relu).then_inc(C.rel, 1)
                act.wait_ge(C.rel, n + 1)
                if half and m == 0:
                    act.wait_ge(C.sdn, 4)
                act.activation(c_sT[:, m, :], c_sr[:, m, :], ACT.Square).then_inc(C.sq, 1)

        def act_x(act, e):
            if e < EXPERTS:
                act.wait_ge(C.xT, e + 1)
                if e >= 2:
                    act.wait_ge(C.up, e - 1)
                act.copy(e_xT[:, e % 2], bank[e % 2][:, 0:D].rearrange("p (k n) -> p k n", k=KC)).then_inc(C.xTs, 1)
            if e >= 1:
                e -= 1
                act.wait_ge(C.up, e + 1)
                if e >= 2:
                    act.wait_ge(C.h2, e - 1)
                act.activation(e_r[:, e % 2, :], bank[2 + e % 2][:, 0:P], ACT.Relu).then_inc(C.hr, 1)

        def dve_x(v, e):
            if e < EXPERTS:
                v.wait_ge(C.hr, e + 1)
                if e >= 2:
                    v.wait_ge(C.dn, e - 1)
                v.tensor_tensor(e_h[:, e % 2, :], e_r[:, e % 2, :], e_r[:, e % 2, :], ALU.mult).then_inc(C.h2, 1)
            if e >= 1:
                e -= 1
                v.wait_ge(C.dn, e + 1)
                if e >= OUT_RING:
                    v.wait_ge(e_out[e % OUT_RING], 16 * (e // OUT_RING))
                v.tensor_copy(e_y[:, e % OUT_RING, :], bank[4 + e % 2][:, 0:D]).then_inc(C.ye, 1)

        POS_READ = 23

        def dve_c_route(v):
            steps = 0

            def done(ins):
                nonlocal steps
                steps += 1
                ins.then_inc(C.route, 1)
                v.wait_ge(C.route, steps)

            flat = lambda a: a[:].rearrange("p b e -> p (b e)")
            v.wait_ge(C.ex, 1)
            done(v.tensor_scalar(flat(c_sg), flat(c_ex), 1.0, None, ALU.add))
            done(v.reciprocal(flat(c_sg), flat(c_sg)))
            done(v.tensor_tensor(c_sc[:], c_sg[:], rbias[:, :].unsqueeze(1).to_broadcast(BE), ALU.add))
            four = flat(c_sc).rearrange("p (n i) -> p n i", i=EPG)
            done(v.tensor_tensor(c_mx[:], four[:, :, 0::2], four[:, :, 1::2], ALU.max))
            done(v.tensor_tensor(c_mn[:], four[:, :, 0::2], four[:, :, 1::2], ALU.min))
            done(v.tensor_tensor(c_hi[:], c_mx[:, :, 0], c_mx[:, :, 1], ALU.max))
            done(v.tensor_tensor(c_lo[:], c_mx[:, :, 0], c_mx[:, :, 1], ALU.min))
            done(v.tensor_tensor(c_m3[:], c_mn[:, :, 0], c_mn[:, :, 1], ALU.max))
            done(v.tensor_tensor(c_sec[:], c_lo[:], c_m3[:], ALU.max))
            done(v.tensor_tensor(c_gs[:], c_hi[:], c_sec[:], ALU.add))
            gs3 = c_gs[:].rearrange(bg, b=BATCH)
            gfull = [P, BATCH, EGROUPS, EGROUPS]
            other = gs3.unsqueeze(2).to_broadcast(gfull)
            own = gs3.unsqueeze(3).to_broadcast(gfull)
            g4 = lambda a: a[:].rearrange("p (b g) o -> p b g o", b=BATCH)
            done(v.tensor_tensor(g4(c_gt), other, own, ALU.is_gt))
            done(v.tensor_tensor(g4(c_eq), other, own, ALU.is_equal))
            done(v.tensor_tensor(g4(c_eql), g4(c_eq), lower_g[:].unsqueeze(1).to_broadcast(gfull), ALU.mult))
            done(v.tensor_tensor(c_rk1[:], c_gt[:], c_eql[:], ALU.add))
            done(v.tensor_reduce(c_rk[:], c_rk1[:], AX.X, ALU.add))
            done(v.tensor_scalar(c_mk[:], c_rk[:], float(KEPT_GROUPS), None, ALU.is_lt))
            done(v.tensor_tensor(flat(c_ms0).rearrange("p (n i) -> p n i", i=EPG), four,
                                 c_mk[:].unsqueeze(2).to_broadcast([P, BATCH * EGROUPS, EPG]), ALU.mult))
            done(v.tensor_scalar(flat(c_ms), flat(c_ms0), 0.0, None, ALU.add))
            for b in range(BATCH):
                v.max(c_top[:, b, :], c_ms[:, b, :]).then_inc(C.top, 1)
            v.wait_ge(C.top, BATCH)
            for b in range(BATCH):
                v.max_index(c_idx[:, b, :], c_top[:, b, :], c_ms[:, b, :]).then_inc(C.idx, 1)
            v.wait_ge(C.idx, BATCH)
            done(v.tensor_copy(c_idxf[:], c_idx[:, :, 0:TOPK]))
            done(v.tensor_tensor(c_oh[:], c_idxf[:].rearrange("p b k -> p (b k)").unsqueeze(2).to_broadcast(BKE),
                                 iota_e[:, :].unsqueeze(1).to_broadcast(BKE), ALU.is_equal))
            with nc.allow_low_precision(reason="a choice count is 0 or 1"):
                v.tensor_reduce(c_sel[:], c_oh[:].rearrange("p (b k) e -> p b e k", b=BATCH), AX.X, ALU.add)\
                 .then_inc(C.sel, 1)
            full4 = [P, BATCH, TOPK, EXPERTS]
            k4 = lambda a: a[:].rearrange("p (b k) e -> p b k e", b=BATCH)
            bk = lambda a: a[:].rearrange("p b k -> p (b k)")
            done(v.tensor_tensor(k4(c_tmp), k4(c_oh), c_sg[:].unsqueeze(2).to_broadcast(full4), ALU.mult))
            done(v.tensor_reduce(bk(c_w4), c_tmp[:], AX.X, ALU.add))
            v.wait_ge(C.pos, 1)
            done(v.tensor_tensor(k4(c_tmp2), k4(c_oh),
                                 bank[3][:, 0:BATCH * EXPERTS].rearrange("p (b e) -> p b e", b=BATCH)
                                 .unsqueeze(2).to_broadcast(full4), ALU.mult))
            pos_read = steps
            done(v.tensor_reduce(bk(c_p4), c_tmp2[:], AX.X, ALU.add))
            done(v.tensor_scalar(bk(c_drop), bk(c_p4), float(CAP), SKIP, ALU.is_ge, ALU.mult))
            done(v.scalar_tensor_tensor(out=bk(c_row), in0=bk(c_idxf), scalar=float(CAP), in1=bk(c_p4),
                                        op0=ALU.mult, op1=ALU.add))
            v.tensor_tensor(bk(c_srow), bk(c_row), bk(c_drop), ALU.add).then_inc(C.srow, 1)
            done(v.tensor_scalar(bk(c_pc), bk(c_p4), float(CAP - 1), None, ALU.min))
            v.scalar_tensor_tensor(out=bk(c_grow), in0=bk(c_idxf), scalar=float(CAP), in1=bk(c_pc),
                                   op0=ALU.mult, op1=ALU.add).then_inc(C.grow, 1)
            done(v.tensor_reduce(c_ws[:], c_w4[:], AX.X, ALU.add))
            done(v.tensor_scalar(c_ws[:], c_ws[:], 1e-20, None, ALU.add))
            done(v.reciprocal(c_wr[:], c_ws[:]))
            done(v.tensor_tensor(c_wv[:], c_w4[:], c_wr[:].unsqueeze(2).to_broadcast([P, BATCH, TOPK]), ALU.mult))
            done(v.tensor_scalar(bk(c_ok), bk(c_p4), float(CAP), ROUTE_SCALE, ALU.is_lt, ALU.mult))
            done(v.tensor_tensor(bk(c_wv), bk(c_wv), bk(c_ok), ALU.mult))
            assert pos_read == POS_READ

        def dve_c_shared(v):
            for p in range(PAIRS):
                v.wait_ge(C.sdn, 2 * p + 2)
                v.tensor_tensor(x_sb[:, 2 * p:2 * p + 2, :], x_sb[:, 2 * p:2 * p + 2, :],
                                bank[4 + p][:, :].rearrange("p (i n) -> p i n", i=2), ALU.add).then_inc(C.shy, 1)

        def dve_c_combine(v, b):
            v.wait_ge(gat[b % 2], 16 * TOPK * (b // 2 + 1))
            if b == 0:
                v.wait_ge(C.shy, PAIRS)
            for k in range(TOPK):
                v.scalar_tensor_tensor(out=x_sb[:, b, :], in0=g_y[:, b % 2, k, :], scalar=c_wv[:, b, k:k + 1],
                                       in1=x_sb[:, b, :], op0=ALU.mult, op1=ALU.add).then_inc(C.acc, 1)
                v.wait_ge(C.acc, TOPK * b + k + 1)

        def pool_c_scatter(g):
            g.wait_ge(C.srow, 1)
            g.wait_ge(C.zeroed, 16 * 4)
            for b in range(BATCH):
                for k in range(TOPK):
                    g.indirect_dma_start(xe_dram, bass.IndirectOffsetOnAxis(ap=c_srow[:, b, k:k + 1], axis=0),
                                         h3[:, b, :], None, bounds_check=EXPERTS * CAP - 1, oob_is_err=False)\
                     .then_inc(C.scat, 16)

        def pool_c_gather(g, b):
            if b == 0:
                g.wait_ge(C.grow, 1)
                g.wait_ge(C.sq, 2 * SC)
                for i in range(OUT_RING):
                    g.wait_ge(e_out[i], 16 * EXPERTS // OUT_RING)
            if b >= 2:
                g.wait_ge(C.acc, TOPK * (b - 1))
            for k in range(TOPK):
                g.indirect_dma_start(g_y[:, b % 2, k, :], None, ye_dram,
                                     bass.IndirectOffsetOnAxis(ap=c_grow[:, b, k:k + 1], axis=0),
                                     bounds_check=EXPERTS * CAP - 1, oob_is_err=False).then_inc(gat[b % 2], 16)


        def pe_d_step(pe, s):
            b, o = BATCH + s, BATCH + s - 3
            def enter(b):
                pe.wait_ge(LN.h, 2 * BATCH + b + 1)
                pe.wait_ge(T.v1, b)
                for k in range(KC):
                    mm = pe.transpose(bank[6][:, k * P:(k + 1) * P], att.h[:, b % 2, k * P:(k + 1) * P], ident[:, :])
                mm.then_inc(T.hTp, 1)

            if s == 0:
                enter(b)

            def extra(j):
                if j == 3 and s + 1 < BATCH:
                    enter(b + 1)
                if j == 0 and s < BATCH:
                    pe.wait_ge(T.hT, b + 1)
                    pe.wait_ge(T.qT, 2 * b)
                    for c in range(KC):
                        for k in range(KC):
                            mm = pe.matmul(kbank(5)[:, c, :], wk1[:, k, c * P:(c + 1) * P], att.hT[:, b % 2, k, :],
                                           start=(k == 0), stop=(k == KC - 1))
                    mm.then_inc(T.K, 1)
                if j == 1 and s >= 3:
                    pe.wait_ge(T.o, o + 1)
                    if s >= 4:
                        pe.wait_ge(T.res, o)
                    for k in range(KC):
                        mm = pe.transpose(bank[7][:, k * P:(k + 1) * P], att.o[:, o % 2, k * P:(k + 1) * P],
                                          ident[:, :])
                    mm.then_inc(T.oTp, 1)
                if j == 1 and s < BATCH:
                    for k in range(KC):
                        mm = pe.matmul(bank[6][:, 0:D], att.hT[:, b % 2, k, :], wv1[:, k, :],
                                       start=(k == 0), stop=(k == KC - 1))
                    mm.then_inc(T.Vp, 1)
                if j == 2 and s >= 3:
                    pe.wait_ge(T.oT, o + 1)
                    for k in range(KC):
                        mm = pe.matmul(bank[7][:, 0:D], att.oT[:, k, :], wo1[:, k, :],
                                       start=(k == 0), stop=(k == KC - 1))
                    mm.then_inc(T.y, 1)
                if j == 2 and s < BATCH:
                    pe.wait_ge(T.kf, b + 1)
                    for c in range(KC):
                        for k in range(KC):
                            mm = pe.matmul(kbank(5)[:, c, :], wq1[:, k, c * P:(c + 1) * P], att.hT[:, b % 2, k, :],
                                           start=(k == 0), stop=(k == KC - 1))
                    mm.then_inc(T.QT, 1)

            pe_blocks(pe, s, 1, extra)

        def act_d_step(act, s):
            b, o = BATCH + s, BATCH + s - 3
            if s < BATCH:
                act.wait_ge(T.hTp, b + 1)
                act.wait_ge(T.QT, b - 1)
                act.copy(att.hT[:, b % 2], bank[6][:, 0:D].rearrange("p (k n) -> p k n", k=KC)).then_inc(T.hT, 1)

            def extra(j):
                if j == 0 and s < BATCH:
                    act.wait_ge(T.K, b + 1)
                    act.wait_ge(T.km0, b)
                    act.wait_ge(T.km1, b)
                    act.copy(att.kf[:], kbank(5)).then_inc(T.kf, 1)
                if j == 1 and s >= 3:
                    act.wait_ge(T.oTp, o + 1)
                    act.wait_ge(T.y, o)
                    act.copy(att.oT[:], bank[7][:, 0:D].rearrange("p (k n) -> p k n", k=KC)).then_inc(T.oT, 1)
                if j == 2 and s < BATCH:
                    act.wait_ge(T.QT, b + 1)
                    act.wait_ge(T.S, GROUPS * (b - 1))
                    act.activation(att.qT[:, b % 2], kbank(5), ACT.Copy, scale=ATT_SCALE).then_inc(T.qT, 2)

            act_blocks(act, s, 1, extra)

        def dve_d_prep(v, b):
            v.wait_ge(T.hTp, BATCH + b - 1)
            dve_norm(v, 3, b, att.h[:, b % 2, :])

        def dve_d_step(v, s):
            b, a, o = BATCH + s, BATCH + s - 2, BATCH + s - 3
            dve_rowmax(v, s, 1, 0)
            if s < BATCH:
                key_copies(v, b, 0, T.km0)
            dve_rowmax(v, s, 1, 1)
            if s < BATCH:
                v.wait_ge(T.Vp, b + 1)
                v.wait_ge(T.O, GROUPS * (b - 2))
                v.tensor_copy(att.v1[:, b % 3, :, 0:HD], bank[6][:, 0:D].rearrange("p (h d) -> p h d", h=HEADS))\
                 .then_inc(T.v1, 1)
            if 2 <= s < BATCH + 2:
                dve_attended(v, a, lambda: v.wait_ge(T.oTp, a - 1))
            dve_rowmax(v, s, 1, 2)
            if s >= 3:
                v.wait_ge(T.y, o + 1)
                v.tensor_tensor(x_sb[:, o - BATCH, :], x_sb[:, o - BATCH, :], bank[7][:, 0:D], ALU.add)\
                 .then_inc(T.res, 1)
            if s + 1 < BATCH:
                dve_c_combine(v, s + 1)
                dve_stats(v, 3, s + 1)
            dve_rowmax(v, s, 1, 3)
            if s + 1 < BATCH:
                dve_d_prep(v, s + 1)

        E = sems("e", "hTp kT e ma mb a1 e1 a2 e2 ov kv p q x2 num den rd y yTp res zero")
        take = views(scratch)
        f_h = take([P, 2, 2, D])
        W = [P, KC, 2, SEQ]
        f_kT, f_e, f_ma, f_mb, f_a1, f_e1, f_a2, f_e2, f_x1, f_x2, f_x3 = (
            take(W) for _ in range(11))
        WP = [P, KC, 2, SEQ + 1]
        f_o, f_p, f_q = (take(WP) for _ in range(3))
        f_dec = take(W)

        fl = lambda a: a[:].rearrange("p k i n -> p (k i n)")
        e_bank = lambda n: bank[n][:, :].rearrange("p (k i n) -> p k i n", k=KC, i=2)

        def pe_e_in(pe, p):
            for i in range(2):
                b = 2 * p + i
                pe.wait_ge(LN.h, 4 * BATCH + b + 1)
            if p >= 1:
                pe.wait_ge(E.kT, p)
            else:
                pe.wait_ge(T.P, 2 * HEADS * BATCH)
            for i in range(2):
                for k in range(KC):
                    mm = pe.transpose(e_bank(0)[:, k, i, :], f_h[:, p % 2, i, k * P:(k + 1) * P], ident[:, :])
            mm.then_inc(E.hTp, 1)

        def pe_e_out(pe, p):
            pe.wait_ge(E.y, p + 1)
            if p >= 1:
                pe.wait_ge(E.res, p)
            for i in range(2):
                for k in range(KC):
                    mm = pe.transpose(bank[1][:, i * D + k * P:i * D + (k + 1) * P], f_x3[:, k, i, :], ident[:, :])
            mm.then_inc(E.yTp, 1)

        def act_e(act, p):
            act.wait_ge(E.hTp, p + 1)
            if p >= 1:
                act.wait_ge(E.e, p)
            act.copy(f_kT[:], e_bank(0)).then_inc(E.kT, 1)
            act.wait_ge(E.ma, 4 * p + 2)
            if p >= 1:
                act.wait_ge(E.p, 4 * p)
                act.wait_ge(E.q, 4 * p)
            act.activation(f_a2[:], f_ma[:], ACT.Exp, scale=-1.0).then_inc(E.a2, 1)
            act.wait_ge(E.mb, 4 * p + 2)
            act.activation(f_e2[:], f_mb[:], ACT.Exp).then_inc(E.e2, 1)
            act.wait_ge(E.ma, 4 * p + 4)
            if p >= 1:
                act.wait_ge(E.den, p)
            act.activation(f_a1[:], f_ma[:], ACT.Exp, scale=-1.0).then_inc(E.a1, 1)
            act.wait_ge(E.mb, 4 * p + 4)
            act.activation(f_e1[:], f_mb[:], ACT.Exp).then_inc(E.e1, 1)

        def dve_e_norm(v, p):
            for i in range(2):
                b = 2 * p + i
                dve_stats(v, 4, b)
                if p >= 2:
                    v.wait_ge(E.hTp, p - 1)
                dve_norm(v, 4, b, f_h[:, p % 2, i, :])

        def dve_e(v, p):
            vT = ctxT[:, :, 2 * p * P:(2 * p + 2) * P].rearrange("p k (i n) -> p k i n", i=2)
            v.wait_ge(E.kT, p + 1)
            for k in range(KC):
                for i in range(2):
                    v.tensor_tensor_scan(f_o[:, k, i, 1:], f_dec[:, k, i, :], f_kT[:, k, i, :], NEG_BIG,
                                         ALU.add, ALU.max).then_inc(E.ov, 1)
            v.wait_ge(E.ov, 4 * (p + 1))
            v.tensor_tensor(f_e[:], f_kT[:], f_o[:, :, :, 0:SEQ], ALU.subtract).then_inc(E.e, 1)
            v.wait_ge(E.e, p + 1)
            if p >= 1:
                v.wait_ge(E.a1, p)
                v.wait_ge(E.e1, p)
            for k in range(KC):
                v.tensor_scalar(f_ma[:, k], f_e[:, k], decay[:, k:k + 1], 0.0, ALU.subtract, ALU.max)\
                 .then_inc(E.ma, 1)
                v.tensor_scalar(f_mb[:, k], f_e[:, k], decay[:, k:k + 1], 0.0, ALU.subtract, ALU.min)\
                 .then_inc(E.mb, 1)
            v.wait_ge(E.a2, p + 1)
            v.wait_ge(E.e2, p + 1)
            for k in range(KC):
                v.tensor_scalar(f_ma[:, k], f_e[:, k], bonus[:, k:k + 1], 0.0, ALU.add, ALU.max)\
                 .then_inc(E.ma, 1)
                v.tensor_scalar(f_mb[:, k], f_e[:, k], bonus[:, k:k + 1], 0.0, ALU.add, ALU.min)\
                 .then_inc(E.mb, 1)
            v.tensor_tensor(f_x1[:], f_e2[:], vT, ALU.mult).then_inc(E.kv, 1)
            v.wait_ge(E.kv, p + 1)
            for k in range(KC):
                for i in range(2):
                    v.tensor_tensor_scan(f_p[:, k, i, 1:], f_a2[:, k, i, :], f_x1[:, k, i, :], 0.0,
                                         ALU.mult, ALU.add).then_inc(E.p, 1)
                    v.tensor_tensor_scan(f_q[:, k, i, 1:], f_a2[:, k, i, :], f_e2[:, k, i, :], 0.0,
                                         ALU.mult, ALU.add).then_inc(E.q, 1)
            v.wait_ge(E.p, 4 * (p + 1))
            v.wait_ge(E.q, 4 * (p + 1))
            v.wait_ge(E.a1, p + 1)
            v.wait_ge(E.e1, p + 1)
            v.tensor_tensor(f_x1[:], f_a1[:], f_p[:, :, :, 0:SEQ], ALU.mult).then_inc(E.x2, 1)
            v.tensor_tensor(f_x2[:], f_e1[:], vT, ALU.mult).then_inc(E.x2, 1)
            if p >= 1:
                v.wait_ge(E.yTp, p)
            v.tensor_tensor(f_x3[:], f_a1[:], f_q[:, :, :, 0:SEQ], ALU.mult).then_inc(E.x2, 1)
            v.wait_ge(E.x2, 3 * (p + 1))
            v.tensor_tensor(f_x1[:], f_x1[:], f_x2[:], ALU.add).then_inc(E.num, 1)
            v.tensor_tensor(f_x3[:], f_x3[:], f_e1[:], ALU.add).then_inc(E.den, 1)
            v.wait_ge(E.num, p + 1)
            v.wait_ge(E.den, p + 1)
            v.reciprocal(f_x2[:], f_x3[:]).then_inc(E.rd, 1)
            v.wait_ge(E.rd, p + 1)
            v.tensor_tensor(f_x3[:], f_x1[:], f_x2[:], ALU.mult).then_inc(E.y, 1)

        def dve_e_residual(v, p):
            v.wait_ge(E.yTp, p + 1)
            v.tensor_tensor(x_sb[:, 2 * p:2 * p + 2, :], x_sb[:, 2 * p:2 * p + 2, :],
                            bank[1][:, :].rearrange("p (i n) -> p i n", i=2), ALU.add).then_inc(E.res, 1)

        F = sems("f", "hTp hT y t1 t2 res out")
        take = views(w0_flat)
        g_h, g_t1 = take([P, 2, D]), take([P, 2, D])
        g_hT = sb("g_hT", [P, 2, KC, P], BF16)
        g_t2 = sb("g_t2", [P, 2, D], F16)
        g_o = views(w0_flat[:, 8 * D:])([P, BATCH, D])

        def pe_f(pe, b):
            pe.wait_ge(zq.sem.q, BATCH + b + 1)
            if b >= 2:
                pe.wait_ge(F.hT, b - 1)
            for k in range(KC):
                mm = pe.transpose(bank[2 + b % 2][:, 0:P].bitcast(BF16).rearrange("p (k n) -> p k n", k=KC)[:, k, :],
                                  zq.q[:, b % 2, k * P:(k + 1) * P], identb[:, :])
            mm.then_inc(F.hTp, 1)
            pe.wait_ge(F.hT, b + 1)
            if b >= 2:
                pe.wait_ge(F.t1, b - 1)
            for k in range(KC):
                mm = pe.matmul(bank[4 + b % 2][:, 0:D], g_hT[:, b % 2, k, :], wfb[:, k, :],
                               start=(k == 0), stop=(k == KC - 1))
            mm.then_inc(F.y, 1)

        def act_f(act, b):
            act.wait_ge(F.hTp, b + 1)
            if b >= 2:
                act.wait_ge(F.y, b - 1)
            act.copy(g_hT[:, b % 2], bank[2 + b % 2][:, 0:P].bitcast(BF16).rearrange("p (k n) -> p k n", k=KC))\
               .then_inc(F.hT, 1)

        def dve_f_in(v, b):
            dve_stats(v, 5, b)
            dve_norm(v, 5, b, g_h[:, b % 2, :])
            v.wait_ge(LN.h, 5 * BATCH + b + 1)

            def free():
                if b >= 2:
                    v.wait_ge(F.hTp, b - 1)
            dve_quant(v, zq, BATCH + b, g_h[:, b % 2, :], 1e-7 / 127.0, free)

        def dve_f_out(v, b):
            v.wait_ge(F.y, b + 1)
            v.scalar_tensor_tensor(out=g_t1[:, b % 2, :], in0=bank[4 + b % 2][:, 0:D], scalar=zq.s[:, BATCH + b:BATCH + b + 1],
                                   in1=wscale, op0=ALU.mult, op1=ALU.mult).then_inc(F.t1, 1)
            v.wait_ge(F.t1, b + 1)
            v.tensor_tensor(g_t2[:, b % 2, :], g_t1[:, b % 2, :], fbias, ALU.add).then_inc(F.t2, 1)
            v.wait_ge(F.t2, b + 1)
            v.tensor_tensor(g_o[:, b, :], x_sb[:, b, :], g_t2[:, b % 2, :], ALU.add).then_inc(F.res, 1)

        block = ctx.enter_context(nc.Block())
        LAST = BATCH + 3

        @block.sync
        def _(sp):
            for b in range(0, BATCH, 2):
                sp.dma_start(x_sb[:, b:b + 2, :], t["x"][b:b + 2].rearrange("b p d -> p b d")).then_inc(ld.x, 16)
            sp.dma_start(ident[:, :], t["ident"]).then_inc(ld.const, 16)
            sp.dma_start(half_pow[:, :], t["half_pow"]).then_inc(ld.const, 16)
            sp.dma_start(init4[:, :], t["init"]).then_inc(ld.const, 16)
            sp.dma_start(w0[:], t["w0"]).then_inc(ld.w0, 16)
            sp.dma_start(qw[:], t["qw"]).then_inc(ld.qw, 16)
            for dst, name in ((ones, "ones"), (beforef, "before"), (head_rows, "head_rows"),
                              (iota_e, "iota_e")):
                sp.dma_start(dst[:, :], t[name]).then_inc(ld.rows, 16)
            sp.dma_start(lower_g[:], t["lower_g"]).then_inc(ld.rows, 16)
            for i, name in enumerate(("bv", "bp", "wscale", "fbias")):
                sp.dma_start(rows[:, i, :], t[name].to_broadcast([P, D])).then_inc(ld.rows, 16)
            sp.dma_start(rbias[:, :], t["rbias"].to_broadcast([P, EXPERTS])).then_inc(ld.rows, 16)
            sp.dma_start(ctxT[:], t["ctxT"]).then_inc(ld.kv0, 16)
            sp.dma_start(wk0[:], t["wk0"]).then_inc(ld.kv0, 16)
            sp.dma_start(wv0[:], t["wv0"]).then_inc(ld.kv0, 16)
            sp.dma_start(bk0[:, :], t["bk0"]).then_inc(ld.kv0, 16)
            sp.dma_start(bq0[:, :], t["bq0"]).then_inc(ld.kv0, 16)
            for dst, name in ((gate, "gate"), (sup, "sup"), (sdown, "sdown")):
                sp.dma_start(dst[:], t[name]).then_inc(ld.moe, 16)
            for dst, name in ((wq1, "wq1"), (wk1, "wk1"), (wv1, "wv1"), (wo1, "wo1"), (wf8, "wf8")):
                sp.dma_start(dst[:], t[name]).then_inc(ld.l1, 16)
            for dst, name in ((decay, "decay"), (bonus, "bonus")):
                sp.dma_start(dst[:, :], t[name]).then_inc(ld.l1, 16)
            sp.wait_ge(cst.small, 1)
            for i in range(4):
                n = EXPERTS * CAP // 4
                sp.dma_start(xe_dram[i * n:(i + 1) * n, :].rearrange("(p r) d -> p (r d)", p=P),
                             zrow[:, :].unsqueeze(1).to_broadcast([P, n * D // P // 1024, 1024])
                             ).then_inc(C.zeroed, 16)
            for e in range(RING):
                sp.dma_start(e_w[:, e, :], t["we"][e]).then_inc(e_in[e], 16)
            sp.wait_ge(C.scat, 16 * BATCH * TOPK)
            for e in range(EXPERTS):
                if e >= RING:
                    sp.wait_ge(C.dn, e - RING + 1)
                    sp.dma_start(e_w[:, e % RING, :], t["we"][e]).then_inc(e_in[e % RING], 16)
                sp.dma_start(e_x[:, e % RING, :], xe_dram[e * CAP:(e + 1) * CAP, :]).then_inc(e_in[e % RING], 16)
            for b in range(BATCH):
                sp.wait_ge(F.res, b + 1)
                sp.dma_start(t["out"][b], g_o[:, b, :]).then_inc(F.out, 16)
            sp.wait_ge(F.out, 16 * BATCH)

        @block.gpsimd
        def _(g):
            g.wait_ge(ld.const, 48)
            for b in range(BATCH):
                pool_rstd(g, 0, b)
            pool_rstd(g, 1, 0)
            g.wait_ge(ld.rows, 16 * 10)
            for s in range(BATCH):
                pool_b_step(g, s)
            for b in range(BATCH):
                pool_rstd(g, 2, b)
            pool_c_scatter(g)
            for e in range(EXPERTS):
                g.wait_ge(C.ye, e + 1)
                g.dma_start(ye_dram[e * CAP:(e + 1) * CAP, :], e_y[:, e % OUT_RING, :]).then_inc(e_out[e % OUT_RING], 16)
            pool_c_gather(g, 0)
            for b in range(BATCH):
                if b + 1 < BATCH:
                    pool_c_gather(g, b + 1)
                pool_rstd(g, 3, b)
                key_copies(g, BATCH + b, 1, T.km1)
            for n in (4, 5):
                for b in range(BATCH):
                    pool_rstd(g, n, b)

        @block.vector
        def _(v):
            v.memset(zrow[:, :], 0.0).then_inc(cst.small, 1)
            for b in range(3):
                v.memset(att.v1[:, b, :, HD], 1.0).then_inc(cst.vones, 1)
            v.wait_ge(ld.x, 16 * PAIRS)
            for b in range(BATCH):
                dve_stats(v, 0, b)
            v.wait_ge(ld.const, 48)
            v.tensor_scalar(init4[:, :], init4[:, :], 4.0, None, ALU.mult).then_inc(A.init4, 1)
            dve_a_norm(v, 0)
            v.wait_ge(ld.qw, 16)
            qf = qw[:].rearrange("p w c n -> p (w c) n")
            v.tensor_reduce(qw_s[:].rearrange("p w c -> p (w c)"), qf, AX.X, ALU.max,
                            apply_absolute_value=True).then_inc(qs.scale, 1)
            v.wait_ge(qs.scale, 1)
            v.tensor_scalar(qw_s[:], qw_s[:], 1.0 / 127.0, 1e-8, ALU.mult, ALU.max).then_inc(qs.scale, 1)
            v.wait_ge(qs.scale, 2)
            v.reciprocal(qw_r[:], qw_s[:]).then_inc(qs.scale, 1)
            v.wait_ge(qs.scale, 3)
            v.wait_ge(ld.rows, 16 * 10)
            for n in range(2 * KC):
                v.tensor_scalar(qw_i[:].rearrange("p w c n -> p (w c) n")[:, n, :], qf[:, n, :],
                                qw_r[:].rearrange("p w c -> p (w c)")[:, n:n + 1], ROUND,
                                ALU.mult, ALU.add).then_inc(qs.i, 1)
                v.tensor_scalar(qw_diag[:, n, :], ident[:, :], qw_s[:].rearrange("p w c -> p (w c)")[:, n:n + 1],
                                None, ALU.mult).then_inc(qs.diag, 1)
            v.wait_ge(qs.i, 2 * KC)
            v.tensor_scalar(qw_b[:], qw_i[:], -ROUND, None, ALU.add).then_inc(qs.b, 1)
            v.tensor_copy(identb[:, :], ident[:, :]).then_inc(cst.ident, 1)
            v.tensor_copy(onesb[:, :], ones[:, :]).then_inc(cst.ident, 1)
            v.tensor_copy(before[:, :], beforef[:, :]).then_inc(cst.ident, 1)
            v.wait_ge(A.init4, 1)
            for p in range(PAIRS):
                if p + 1 < PAIRS:
                    dve_a_norm(v, p + 1)
                dve_a(v, p)
                dve_a_residual(v, p)
            v.wait_ge(qs.evacrow, 1)
            v.wait_ge(ld.kv0, 80)
            v.wait_ge(cst.vones, 3)
            dve_b_stats(v, 0)
            dve_b_prep(v, 0)
            for s in range(LAST):
                dve_b_step(v, s)
            for b in range(BATCH):
                v.wait_ge(T.res, b + 1)
                dve_stats(v, 2, b)
                dve_norm(v, 2, b, h3[:, b, :])
            dve_c_route(v)
            v.wait_ge(LN.h, 2 * BATCH + BATCH)
            dve_c_shared(v)
            for e in range(EXPERTS + 1):
                dve_x(v, e)
            v.wait_ge(ld.l1, 16 * 7)
            v.tensor_copy(wfb[:].rearrange("p k n -> p (k n)"),
                          wf8[:].rearrange("p k n -> p (k n)").bitcast(I8)).then_inc(cst.wfb, 1)
            dve_c_combine(v, 0)
            dve_stats(v, 3, 0)
            dve_d_prep(v, 0)
            for s in range(LAST):
                dve_d_step(v, s)
            for a, value in ((f_o, NEG_BIG), (f_p, 0.0), (f_q, 0.0)):
                v.memset(a[:, :, :, 0], value).then_inc(E.zero, 1)
            v.memset(f_dec[:], 0.0).then_inc(E.zero, 1)
            v.wait_ge(E.zero, 4)
            for k in range(KC):
                v.tensor_scalar(f_dec[:, k], f_dec[:, k], decay[:, k:k + 1], None, ALU.add).then_inc(E.zero, 1)
            v.wait_ge(E.zero, 4 + KC)
            v.wait_ge(T.res, 2 * BATCH)
            dve_e_norm(v, 0)
            for p in range(PAIRS):
                if p + 1 < PAIRS:
                    dve_e_norm(v, p + 1)
                dve_e(v, p)
                dve_e_residual(v, p)
            for b in range(BATCH):
                if b % 2 == 0:
                    v.wait_ge(E.res, b // 2 + 1)
                dve_f_in(v, b)
                if b >= 1:
                    dve_f_out(v, b - 1)
            dve_f_out(v, BATCH - 1)

        @block.scalar
        def _(act):
            act.wait_ge(ld.const, 48)
            act.wait_ge(qs.T, 1)
            for w in range(2):
                act.copy(qwT[:, w], bank[1 + w][:, 0:2 * P].bitcast(BF16).rearrange("p (k n) -> p k n", k=KC))\
                   .then_inc(qs.evacT, 1)
            act.wait_ge(qs.row, 1)
            act.copy(qw_row[:].rearrange("p w n -> p (w n)"), bank[3][:, :]).then_inc(qs.evacrow, 1)
            for p in range(PAIRS):
                act_a(act, p)
            for s in range(LAST):
                act_b_step(act, s)
            act_c(act)
            for half in range(2):
                act_c_shared(act, half)
            for e in range(EXPERTS + 1):
                act_x(act, e)
            for s in range(LAST):
                act_d_step(act, s)
            for p in range(PAIRS):
                act_e(act, p)
            for b in range(BATCH):
                act_f(act, b)

        @block.tensor
        def _(pe):
            pe.wait_ge(qs.b, 1)
            pe.wait_ge(cst.ident, 3)
            pe.wait_ge(ld.const, 48)
            for w in range(2):
                for o in range(KC):
                    for k in range(KC):
                        mm = pe.transpose(bank[1 + w][:, 0:2 * P].bitcast(BF16)[:, k * D + o * P:k * D + (o + 1) * P],
                                          qw_b[:, w, o, k * P:(k + 1) * P], identb[:, :])
            mm.then_inc(qs.T, 1)
            pe.wait_ge(qs.diag, 2 * KC)
            for n in range(2 * KC):
                mm = pe.matmul(bank[3][:, n * P:(n + 1) * P], ones[:, :], qw_diag[:, n, :], start=True, stop=True)
            mm.then_inc(qs.row, 1)
            pe.wait_ge(qs.evacT, 2)
            pe.wait_ge(qs.evacrow, 1)
            pe_a_transpose(pe, 0)
            pe.wait_ge(ld.w0, 16)
            for p in range(PAIRS):
                pe_a_project(pe, p)
                if p + 1 < PAIRS:
                    pe_a_transpose(pe, p + 1)
                pe_a_down(pe, p)
            pe.wait_ge(A.res, PAIRS)
            pe.wait_ge(ld.kv0, 80)
            for s in range(LAST):
                pe_b_step(pe, s)
            pe.wait_ge(ld.moe, 48)
            pe_c(pe)
            pe_c_up(pe, 0)
            pe_c_down(pe, 0)
            pe_c_up(pe, 1)
            pe_c_down(pe, 1)
            pe_c_pos(pe)
            pe.wait_ge(C.route, POS_READ)
            pe.wait_ge(C.rel, 2 * SC)
            for e in range(EXPERTS + 2):
                if e < EXPERTS:
                    pe_x_transpose(pe, e)
                if 1 <= e <= EXPERTS:
                    pe_x_up(pe, e - 1)
                if e >= 2:
                    pe_x_down(pe, e - 2)
            pe.wait_ge(C.ye, EXPERTS)
            pe.wait_ge(C.hr, EXPERTS)
            pe.wait_ge(C.xTs, EXPERTS)
            pe.wait_ge(ld.l1, 16 * 7)
            for s in range(LAST):
                pe_d_step(pe, s)
            pe.wait_ge(T.pt, 2 * BLOCKS)
            pe.wait_ge(T.o, 2 * BATCH)
            pe_e_in(pe, 0)
            for p in range(PAIRS):
                if p + 1 < PAIRS:
                    pe_e_in(pe, p + 1)
                pe_e_out(pe, p)
            pe.wait_ge(cst.wfb, 1)
            for b in range(BATCH):
                pe_f(pe, b)


def _layouts(a):
    def chunked(w):
        w = np.asarray(w)
        return np.ascontiguousarray(w.reshape(w.shape[0] // P, P, w.shape[1]).transpose(1, 0, 2))

    def column(v):
        return np.ascontiguousarray(np.asarray(v).reshape(-1, P).T)

    l0 = [np.asarray(a[f"L0_attn_{n}"]) for n in L0_MATS]
    wkv, bkv = np.asarray(a["L0_xattn_wkv"]), np.asarray(a["L0_xattn_bkv"])
    qw = np.stack([np.asarray(a["L0_xattn_wq"]), np.asarray(a["L0_xattn_wp"])])
    up = np.asarray(a["L0_ffn_up_w"]).transpose(0, 2, 1).reshape(EXPERTS, KC, P, HID).transpose(0, 2, 1, 3)
    down = np.asarray(a["L0_ffn_down_w"]).transpose(0, 2, 1)
    row = lambda n: np.asarray(a[n]).reshape(1, -1)
    r = np.arange(P)
    heads_of = lambda w: np.repeat(np.asarray(w).reshape(HEADS // 2, 1, HD, D), 2, axis=1).reshape(D, D)
    out = {
        "x": np.asarray(a["x"]),
        "w0": chunked(np.concatenate(l0, axis=1)).reshape(P, KC, len(L0_MATS), D),
        "init": column(a["L0_attn_init_state"]),
        "qw": qw.reshape(2, KC, P, D).transpose(2, 0, 1, 3),
        "ctxT": chunked(np.asarray(a["ctx_2048"]).reshape(TOK, D).T),
        "wk0": chunked(wkv[:D].T), "wv0": chunked(wkv[D:].T),
        "bk0": column(bkv[:D]), "bq0": column(a["L0_xattn_bq"]),
        "bv": bkv[D:].reshape(1, D), "bp": row("L0_xattn_bp"),
        "wscale": row("L1_ffn_w_scale"), "fbias": row("L1_ffn_bias"), "rbias": row("L0_ffn_bias_corr"),
        "gate": chunked(np.asarray(a["L0_ffn_gate_w"]).T),
        "sup": chunked(np.asarray(a["L0_ffn_shared_up_w"]).T),
        "sdown": chunked(np.asarray(a["L0_ffn_shared_down_w"]).T),
        "we": np.concatenate([up.reshape(EXPERTS, P, D), down], axis=2),
        "wq1": chunked(np.asarray(a["L1_attn_wq"]).T), "wk1": chunked(heads_of(a["L1_attn_wk"]).T),
        "wv1": chunked(heads_of(a["L1_attn_wv"]).T), "wo1": chunked(np.asarray(a["L1_attn_wo"]).T),
        "wf8": chunked(np.asarray(a["L1_ffn_weight"]).T).view(np.int32),
        "decay": column(a["L1_xattn_w"]), "bonus": column(a["L1_xattn_u"]),
        "ident": np.eye(P, dtype=np.float32), "ones": np.ones((P, P), np.float32),
        "before": (r[:, None] < r[None, :]).astype(np.float32),
        "head_rows": (r[:, None] // HD == np.arange(HEADS // KC)[None, :]).astype(np.float32),
        "half_pow": np.full((P, BATCH), -0.5, np.float32),
        "iota_e": np.tile(np.arange(EXPERTS, dtype=np.float32), (P, 1)),
        "lower_g": np.tile(np.tril(np.ones((EGROUPS, EGROUPS), np.float32), -1), (P, 1, 1)),
    }
    return {k: np.ascontiguousarray(v) for k, v in out.items()}


def kernel(**inputs):
    import concourse.bacc as bacc
    from concourse.bass_utils import run_bass_kernel_spmd

    arrays = _layouts(inputs)
    nc = bacc.Bacc("TRN2", target_bir_lowering=False, num_devices=1)
    t = {n: nc.dram_tensor(f"in_{n}", a.shape, mybir.dt.from_np(a.dtype), kind="ExternalInput").ap()
         for n, a in arrays.items()}
    t["out"] = nc.dram_tensor("out", (BATCH, SEQ, D), F32, kind="ExternalOutput").ap()
    build(nc, t)
    result = run_bass_kernel_spmd(nc, [{f"in_{n}": a for n, a in arrays.items()}], core_ids=[0])
    return result.results[0]["out"]
```

```python
from contextlib import ExitStack

import numpy as np

import concourse.bass as bass
from concourse import mybir

F32 = mybir.dt.float32
BF16 = mybir.dt.bfloat16
F16 = mybir.dt.float16
U32 = mybir.dt.uint32
I8 = mybir.dt.int8
I32 = mybir.dt.int32
ALU = mybir.AluOpType
ACT = mybir.ActivationFunctionType
AX = mybir.AxisListType

P = 128
BATCH, SEQ, D = 8, 128, 256
KC = D // P
TOK = BATCH * SEQ
PAIRS = BATCH // 2
HEADS, HD = 16, 16
KV_HEADS = 8
GROUPS = 4
CH = HEADS // GROUPS
VC = HD + 1
EXPERTS, TOPK, CAP, HID = 32, 4, 128, 128
EGROUPS, KEPT_GROUPS = 8, 4
EPG = EXPERTS // EGROUPS
SHARED = 512
SC = SHARED // P
ROUTE_SCALE = 2.5
LN_EPS = 1e-5
ROUND = 12582912.0
NEG_BIG = -1e38
SKIP = 8192.0
ATT_SCALE = HD ** -0.5

L0_MATS = ("w_f", "w_i", "w_v", "w_q", "w_gate", "w_up", "w_ro", "w_down")


def named(**parts):
    return type("Named", (), parts)


def build(nc, t):
    ctx = ExitStack()
    with ctx:
        def sb(name, shape, dt=F32):
            return ctx.enter_context(nc.sbuf_tensor(name, shape, dt))

        def sems(prefix, names):
            return named(**{n: ctx.enter_context(nc.semaphore(f"{prefix}_{n}"))
                                      for n in names.split()})

        def views(buffer):
            at = 0

            def take(shape):
                nonlocal at
                size = int(np.prod(shape[1:]))
                part = buffer[:, at:at + size]
                at += size
                names = "abcd"[:len(shape) - 1]
                if len(names) == 1:
                    return part
                return part.rearrange(f"p ({' '.join(names)}) -> p {' '.join(names)}",
                                      **{n: int(k) for n, k in zip(names, shape[1:])})
            return take

        ident = sb("ident", [P, P])
        identb = sb("identb", [P, P], BF16)
        ones = sb("ones", [P, P])
        onesb = sb("onesb", [P, P], BF16)
        before = sb("before", [P, P], BF16)
        head_rows = sb("head_rows", [P, HEADS // KC])
        half_pow = sb("half_pow", [P, BATCH])
        iota_e = sb("iota_e", [P, EXPERTS])
        lower_g = sb("lower_g", [P, EGROUPS, EGROUPS])
        scratch = sb("scratch", [P, 36 * 256])
        w0_flat = sb("w0", [P, KC * len(L0_MATS) * D])
        w0 = w0_flat[:, :].rearrange("p (k m n) -> p k m n", k=KC, m=len(L0_MATS))
        init4 = sb("init4", [P, KC])
        wk0 = sb("wk0", [P, KC, D])
        wv0 = sb("wv0", [P, KC, D])
        bk0, bq0 = sb("bk0", [P, KC]), sb("bq0", [P, KC])
        rows = sb("rows", [P, 4, D])
        bv, bp, wscale, fbias = (rows[:, i, :] for i in range(4))
        rbias = sb("rbias", [P, EXPERTS])
        wq1 = sb("wq1", [P, KC, D])
        wk1 = sb("wk1", [P, KC, P])
        wv1 = sb("wv1", [P, KC, P])
        wo1 = sb("wo1", [P, KC, D])
        gate = sb("gate", [P, KC, EXPERTS])
        sup = sb("sup", [P, KC, SHARED])
        sdown = sb("sdown", [P, SC, D])
        decay = sb("decay", [P, KC])
        minus_decay = sb("minus_decay", [P, KC])
        bonus = sb("bonus", [P, KC])
        wf8 = sb("wf8", [P, KC, D // 4], I32)
        wfb = sb("wfb", [P, KC, D], BF16)
        ctxT = sb("ctxT", [P, KC, TOK])
        x_sb = sb("x_sb", [P, BATCH, D])

        h3_flat = sb("h3", [P, BATCH * D])
        hT3_flat = sb("hT3", [P, KC * TOK])
        take = views(h3_flat)
        beforef = take([P, P])

        qw = take([P, 2, KC, D])
        qw_s = sb("qw_s", [P, 2, KC])
        qw_r = sb("qw_r", [P, 2, KC])
        take = views(hT3_flat)
        qw_i, qw_diag = take([P, 2, KC, D]), take([P, 2 * KC, P])
        qw_b = sb("qw_b", [P, 2, KC, D], BF16)
        qwT = sb("qwT", [P, 2, KC, D], BF16)
        qw_row = sb("qw_row", [P, 2, D])

        bank = [ctx.enter_context(nc.psum_tensor(f"bank{i}", [P, 512], F32)) for i in range(8)]

        ld = sems("ld", "first x w0 w1 kv0 rows l1 moe")
        cst = sems("cst", "ident small vones wfb")
        qs = sems("qw", "scale i b T row diag evacT evacrow")

        LN, LN4, LN5 = (sems(n, "stats mv ve rstd h") for n in ("ln", "ln4", "ln5"))
        ln_st = sb("ln_st", [P, 6 * BATCH, 6])
        ln_mv = sb("ln_mv", [P, 6 * BATCH, 2])
        ln_ve, ln_rstd = sb("ln_ve", [P, 6 * BATCH]), sb("ln_rstd", [P, 6 * BATCH])

        def counts(n, b):
            ln, turn = ((LN, 0), (LN, 1), (LN4, 0), (LN, 2), (LN4, 1), (LN5, 0))[n]
            return ln, turn * BATCH + b

        def dve_stats(v, n, b):
            i, (ln, before) = n * BATCH + b, counts(n, b)
            v.bn_stats(ln_st[:, i, :], x_sb[:, b, :]).then_inc(ln.stats, 1)
            v.wait_ge(ln.stats, before + 1)
            v.bn_aggr(ln_mv[:, i, :], ln_st[:, i, :]).then_inc(ln.mv, 1)

        def pool_rstd(g, n, b):
            i, (ln, before) = n * BATCH + b, counts(n, b)
            g.wait_ge(ln.mv, before + 1)
            g.tensor_scalar(ln_ve[:, i:i + 1], ln_mv[:, i, 1:2], LN_EPS, None, ALU.add).then_inc(ln.ve, 1)
            g.wait_ge(ln.ve, before + 1)
            g.tensor_tensor(ln_rstd[:, i:i + 1], ln_ve[:, i:i + 1], half_pow[:, 0:1], ALU.pow).then_inc(ln.rstd, 1)

        def norm(e, n, b, out):
            i, (ln, before) = n * BATCH + b, counts(n, b)
            e.wait_ge(ln.rstd, before + 1)
            e.tensor_scalar(out, x_sb[:, b, :], ln_mv[:, i, 0:1], ln_rstd[:, i:i + 1],
                            ALU.subtract, ALU.mult).then_inc(ln.h, 1)

        def quant_buffers(name):
            return named(am=sb(f"{name}_am", [P, 2 * BATCH]), s=sb(f"{name}_s", [P, 2 * BATCH]),
                                   r=sb(f"{name}_r", [P, 2 * BATCH]), i=sb(f"{name}_i", [P, D]),
                                   q=sb(f"{name}_q", [P, 2, D], BF16),
                                   sem=sems(name, "step q"))

        def dve_quant(v, z, b, src, least, free_q):
            v.tensor_reduce(z.am[:, b:b + 1], src, AX.X, ALU.max, apply_absolute_value=True).then_inc(z.sem.step, 1)
            v.wait_ge(z.sem.step, 4 * b + 1)
            v.tensor_scalar(z.s[:, b:b + 1], z.am[:, b:b + 1], 1.0 / 127.0, least,
                            ALU.mult, ALU.max).then_inc(z.sem.step, 1)
            v.wait_ge(z.sem.step, 4 * b + 2)
            v.reciprocal(z.r[:, b:b + 1], z.s[:, b:b + 1]).then_inc(z.sem.step, 1)
            v.wait_ge(z.sem.step, 4 * b + 3)
            v.tensor_scalar(z.i[:, :], src, z.r[:, b:b + 1], ROUND, ALU.mult, ALU.add).then_inc(z.sem.step, 1)
            v.wait_ge(z.sem.step, 4 * b + 4)
            free_q()
            v.tensor_scalar(z.q[:, b % 2, :], z.i[:, :], -ROUND, None, ALU.add).then_inc(z.sem.q, 1)

        A = sems("a", "hT hTs F I V Q G U tf ti tv tg av b4 fix zero st z tz r gg u2 y res init4")
        take = views(scratch)
        a_h = take([P, 2, 2, D])
        a_hT = take([P, 2, KC, D])
        a_tf, a_ti, a_tv, a_tg, a_av, a_b4, a_st, a_z, a_tz, a_gg = (
            take([P, KC, D]) for _ in range(10))
        a_r = take([P, KC, D])
        a_u2 = take([P, KC, D])
        A_OUT = {"F": 1, "I": 2, "V": 3, "Q": 4, "G": 5, "U": 6}

        def psA(n):
            return bank[n][:, :].rearrange("p (c n) -> p c n", c=KC)

        def pe_a_transpose(pe, p):
            for i in range(2):
                pe.wait_ge(LN.h, 2 * p + i + 1)
            if p >= 1:
                pe.wait_ge(A.hTs, p)
            for i in range(2):
                for c in range(KC):
                    mm = pe.transpose(psA(0)[:, c, i * P:(i + 1) * P],
                                      a_h[:, p % 2, i, c * P:(c + 1) * P], ident[:, :])
            mm.then_inc(A.hT, 1)

        def pe_a_project(pe, p):
            pe.wait_ge(A.hTs, p + 1)
            for name, mat, free in (("F", 0, A.tf), ("I", 1, A.ti), ("V", 2, A.av), ("Q", 3, A.z),
                                    ("G", 4, A.gg), ("U", 5, A.u2)):
                if p >= 1:
                    pe.wait_ge(free, p)
                if name == "Q" and p == 0:
                    pe.wait_ge(ld.w1, 16)
                for c in range(KC):
                    for k in range(KC):
                        mm = pe.matmul(psA(A_OUT[name])[:, c, :], w0[:, k, mat, c * P:(c + 1) * P],
                                       a_hT[:, p % 2, k, :], start=(k == 0), stop=(k == KC - 1))
                mm.then_inc({"F": A.F, "I": A.I, "V": A.V, "Q": A.Q, "G": A.G, "U": A.U}[name], 1)

        def pe_a_down(pe, p):
            if p >= 1:
                pe.wait_ge(A.res, p)
            pe.wait_ge(A.r, p + 1)
            pe.wait_ge(A.u2, p + 1)
            for i in range(2):
                for n, (src, mat) in enumerate(((a_r, 6), (a_u2, 7))):
                    for k in range(KC):
                        mm = pe.matmul(psA(7)[:, i, :], src[:, k, i * P:(i + 1) * P], w0[:, k, mat, :],
                                       start=(n == 0 and k == 0), stop=(n == 1 and k == KC - 1))
            mm.then_inc(A.y, 1)

        def act_a(act, p):
            act.wait_ge(A.hT, p + 1)
            if p >= 2:
                act.wait_ge(A.U, p - 1)
            act.copy(a_hT[:, p % 2], psA(0)).then_inc(A.hTs, 1)
            act.wait_ge(A.F, p + 1)
            if p >= 1:
                act.wait_ge(A.st, p)
            act.activation(a_tf[:], psA(1), ACT.Tanh).then_inc(A.tf, 1)
            act.wait_ge(A.I, p + 1)
            if p >= 1:
                act.wait_ge(A.b4, p)
            act.activation(a_ti[:], psA(2), ACT.Tanh, scale=0.5).then_inc(A.ti, 1)
            act.wait_ge(A.V, p + 1)
            if p >= 1:
                act.wait_ge(A.av, p)
            act.activation(a_tv[:], psA(3), ACT.Tanh, scale=0.5).then_inc(A.tv, 1)
            act.wait_ge(A.z, p + 1)
            if p >= 1:
                act.wait_ge(A.r, p)
            act.activation(a_tz[:], a_z[:], ACT.Tanh, scale=0.5).then_inc(A.tz, 1)
            act.wait_ge(A.G, p + 1)
            if p >= 1:
                act.wait_ge(A.gg, p)
            act.activation(a_tg[:], psA(5), ACT.Tanh, scale=0.5).then_inc(A.tg, 1)

        def dve_a_norm(v, p):
            for i in range(2):
                b = 2 * p + i
                if p >= 2:
                    v.wait_ge(A.hT, p - 1)
                norm(v, 0, b, a_h[:, p % 2, i, :])

        def dve_a(v, p):
            v.wait_ge(A.tv, p + 1)
            v.scalar_tensor_tensor(out=a_av[:], in0=a_tv[:], scalar=1.0, in1=psA(3),
                                   op0=ALU.add, op1=ALU.mult).then_inc(A.av, 1)
            v.wait_ge(A.av, p + 1)
            v.wait_ge(A.ti, p + 1)
            v.scalar_tensor_tensor(out=a_b4[:], in0=a_ti[:], scalar=1.0, in1=a_av[:],
                                   op0=ALU.add, op1=ALU.mult).then_inc(A.b4, 1)
            v.wait_ge(A.b4, p + 1)
            v.wait_ge(A.tf, p + 1)
            for c in range(KC):
                v.scalar_tensor_tensor(out=a_b4[:, c, ::SEQ], in0=a_tf[:, c, ::SEQ], scalar=init4[:, c:c + 1],
                                       in1=a_b4[:, c, ::SEQ], op0=ALU.mult, op1=ALU.add).then_inc(A.fix, 1)
            v.wait_ge(A.fix, KC * (p + 1))
            v.memset(a_tf[:, :, ::SEQ], 0.0).then_inc(A.zero, 1)
            v.wait_ge(A.zero, p + 1)
            v.tensor_tensor_scan(a_st[:].rearrange("p c n -> p (c n)"), a_tf[:].rearrange("p c n -> p (c n)"),
                                 a_b4[:].rearrange("p c n -> p (c n)"), 0.0, ALU.mult, ALU.add).then_inc(A.st, 1)
            v.wait_ge(A.st, p + 1)
            v.wait_ge(A.Q, p + 1)
            if p >= 1:
                v.wait_ge(A.tz, p)
            v.scalar_tensor_tensor(out=a_z[:], in0=psA(4), scalar=0.25, in1=a_st[:],
                                   op0=ALU.mult, op1=ALU.mult).then_inc(A.z, 1)
            v.wait_ge(A.tz, p + 1)
            if p >= 1:
                v.wait_ge(A.y, p)
            v.scalar_tensor_tensor(out=a_r[:], in0=a_tz[:], scalar=1.0, in1=a_z[:],
                                   op0=ALU.add, op1=ALU.mult).then_inc(A.r, 1)
            v.wait_ge(A.tg, p + 1)
            v.scalar_tensor_tensor(out=a_gg[:], in0=a_tg[:], scalar=1.0, in1=psA(5),
                                   op0=ALU.add, op1=ALU.mult).then_inc(A.gg, 1)
            v.wait_ge(A.gg, p + 1)
            v.wait_ge(A.U, p + 1)
            v.tensor_tensor(a_u2[:], a_gg[:], psA(6), ALU.mult).then_inc(A.u2, 1)

        def dve_a_residual(v, p):
            v.wait_ge(A.y, p + 1)
            v.scalar_tensor_tensor(out=x_sb[:, 2 * p:2 * p + 2, :], in0=psA(7), scalar=0.5,
                                   in1=x_sb[:, 2 * p:2 * p + 2, :], op0=ALU.mult, op1=ALU.add).then_inc(A.res, 1)

        km_flat = sb("t_km", [P, 2 * HEADS * P])
        att = named(
            kf=sb("t_kf", [P, KC, P]), km=views(km_flat)([P, 2, HEADS, P]), qT=sb("t_qT", [P, 2, KC, P]),
            v1=sb("t_v1", [P, 3, HEADS, VC]), nm=sb("t_nm", [P, 2, HEADS]),
            pb=sb("t_pb", [P, 2, CH, P]), pt=sb("t_pt", [P, 2, CH, P]),
            rs=sb("t_rs", [P, HEADS]), o=sb("t_o", [P, 2, D]),
            hT=sb("t_hT", [P, 2, KC, P]), hTb=sb("t_hTb", [P, 2, KC, P], BF16),
            oT=sb("t_oT", [P, KC, P]), oTb=sb("t_oTb", [P, KC, P], BF16), h=sb("t_h", [P, 2, D]),
            q1=sb("t_q1", [P, D]), y=sb("t_y", [P, D]))
        T = sems("att", "hTp hT K kf km0 km1 Vp v1 Qp q1 QT qT S nm P PTp pt O rs o oTp oT y yt xb res")
        BLOCKS = GROUPS * BATCH

        def bank4(n):
            return bank[n][:, :].rearrange("p (c n) -> p c n", c=CH)

        def kbank(n):
            return bank[n][:, 0:D].rearrange("p (c n) -> p c n", c=KC)

        def o_bank():
            return bank[4][:, 0:HEADS * VC].rearrange("p (h d) -> p h d", h=HEADS)

        def keys_at(b, j):
            return CH * j if b < BATCH else CH * j % KV_HEADS

        def pe_scores(pe, n):
            b, j = divmod(n, GROUPS)
            if j == 0:
                pe.wait_ge(T.qT, 2 * (b + 1))
                pe.wait_ge(T.km0, b + 1)
            if j == GROUPS // 2:
                pe.wait_ge(T.km1, min(b + 1, BATCH))
            if n >= 2:
                pe.wait_ge(T.P, CH * (n - 1))
            at = keys_at(b, j)
            pe.matmul(bank4(n % 2), att.qT[:, b % 2, j // 2, :], att.km[:, b % 2, at:at + CH, :],
                      start=True, stop=True).then_inc(T.S, 1)

        def pe_turn(pe, n):
            pe.wait_ge(T.P, CH * (n + 1))
            if n >= 2:
                pe.wait_ge(T.pt, n - 1)
            for i in range(CH):
                mm = pe.transpose(bank4(2 + n % 2)[:, i, :], att.pb[:, n % 2, i, :], ident[:, :])
            mm.then_inc(T.PTp, 1)

        def pe_values(pe, n):
            b, j = divmod(n, GROUPS)
            pe.wait_ge(T.pt, n + 1)
            if j == 0:
                pe.wait_ge(T.v1, b + 1)
                if b >= 1:
                    pe.wait_ge(T.o, b)
            for i in range(CH):
                mm = pe.matmul(o_bank()[:, CH * j + i, :], att.pt[:, n % 2, i, :],
                               att.v1[:, b % 3, keys_at(b, j) + i, :],
                               start=True, stop=True)
            mm.then_inc(T.O, 1)

        def pe_blocks(pe, s, phase, extra):
            for j in range(GROUPS):
                t = GROUPS * (s - 1) + j
                if 0 <= t < BLOCKS:
                    pe_scores(pe, BLOCKS * phase + t)
                extra(j)
                if 0 <= t - 1 < BLOCKS:
                    pe_turn(pe, BLOCKS * phase + t - 1)
                if 0 <= t - 2 < BLOCKS:
                    pe_values(pe, BLOCKS * phase + t - 2)
            extra(GROUPS)

        def act_exp(act, n):
            b, j = divmod(n, GROUPS)
            act.wait_ge(T.nm, n + 1)
            if n >= 2:
                act.wait_ge(T.PTp, n - 1)
            for i in range(CH):
                h = CH * j + i
                act.activation(att.pb[:, n % 2, i, :], bank4(n % 2)[:, i, :], ACT.Exp,
                               bias=att.nm[:, b % 2, h:h + 1]).then_inc(T.P, 1)

        def act_turned(act, n):
            act.wait_ge(T.PTp, n + 1)
            if n >= 2:
                act.wait_ge(T.O, n - 1)
            act.copy(att.pt[:, n % 2], bank4(2 + n % 2)).then_inc(T.pt, 1)

        def act_blocks(act, s, phase, extra):
            for j in range(GROUPS):
                t = GROUPS * (s - 1) + j
                if 0 <= t < BLOCKS:
                    act_exp(act, BLOCKS * phase + t)
                extra(j)
                if 0 <= t - 1 < BLOCKS:
                    act_turned(act, BLOCKS * phase + t - 1)
            extra(GROUPS)

        def dve_rowmax(v, s, phase, j):
            t = GROUPS * (s - 1) + j
            if 0 <= t < BLOCKS:
                n = BLOCKS * phase + t
                b = n // GROUPS
                v.wait_ge(T.S, n + 1)
                if j == 0 and b >= 2:
                    v.wait_ge(T.P, HEADS * (b - 1))
                v.tensor_reduce(att.nm[:, b % 2, CH * j:CH * (j + 1)], bank4(n % 2), AX.X, ALU.max,
                                negate=True).then_inc(T.nm, 1)

        def key_copies(e, b, c, done):
            full = [P, HEADS // KC, P]
            e.wait_ge(T.kf, b + 1)
            if b >= 2:
                e.wait_ge(T.S, GROUPS * (b - 1))
            e.tensor_tensor(att.km[:, b % 2, c * (HEADS // KC):(c + 1) * (HEADS // KC), :],
                            att.kf[:, c, :].unsqueeze(1).to_broadcast(full),
                            head_rows[:, :].unsqueeze(2).to_broadcast(full), ALU.mult).then_inc(done, 1)

        def dve_attended(v, b, free):
            v.wait_ge(T.O, GROUPS * (b + 1))
            v.reciprocal(att.rs[:, :], o_bank()[:, :, HD]).then_inc(T.rs, 1)
            v.wait_ge(T.rs, b + 1)
            free()
            v.tensor_tensor(att.o[:, b % 2].rearrange("p (h d) -> p h d", h=HEADS), o_bank()[:, :, 0:HD],
                            att.rs[:, :].unsqueeze(2).to_broadcast([P, HEADS, HD]), ALU.mult).then_inc(T.o, 1)

        zq = quant_buffers("zq")
        zo = quant_buffers("zo")

        def pe_b_step(pe, s):
            b, o = s, s - 3
            def extra(j):
                if j == 0 and b < BATCH:
                    pe.wait_ge(zq.sem.q, b + 1)
                    if b >= 1:
                        pe.wait_ge(T.v1, b)
                    if s >= 5:
                        pe.wait_ge(C.ex, s - 4)
                    for k in range(KC):
                        mm = pe.transpose(bank[6][:, 0:P].bitcast(BF16).rearrange("p (k n) -> p k n", k=KC)[:, k, :],
                                          zq.q[:, b % 2, k * P:(k + 1) * P], identb[:, :])
                    mm.then_inc(T.hTp, 1)
                    if b >= 1:
                        pe.wait_ge(T.qT, 2 * b)
                    for c in range(KC):
                        for k in range(KC):
                            mm = pe.matmul(kbank(5)[:, c, :], wk0[:, k, c * P:(c + 1) * P],
                                           ctxT[:, k, b * P:(b + 1) * P], start=(k == 0), stop=(k == KC - 1))
                    mm.then_inc(T.K, 1)
                    pe.wait_ge(T.hT, b + 1)
                    if o >= 1:
                        pe.wait_ge(T.yt, o)
                    for k in range(KC):
                        mm = pe.matmul(bank[7][:, 0:D], att.hTb[:, b % 2, k, :], qwT[:, 0, k, :],
                                       start=(k == 0), stop=(k == KC - 1))
                    mm.then_inc(T.Qp, 1)
                if j == 1 and 0 <= o < BATCH:
                    pe.wait_ge(zo.sem.q, o + 1)
                    if b < BATCH:
                        pe.wait_ge(T.q1, b + 1)
                    elif o >= 1:
                        pe.wait_ge(T.yt, o)
                    for k in range(KC):
                        mm = pe.transpose(bank[7][:, 0:P].bitcast(BF16).rearrange("p (k n) -> p k n", k=KC)[:, k, :],
                                          zo.q[:, o % 2, k * P:(k + 1) * P], identb[:, :])
                    mm.then_inc(T.oTp, 1)
                if j == 1 and b < BATCH:
                    pe.wait_ge(T.hT, b + 1)
                    for k in range(KC):
                        mm = pe.matmul(bank[6][:, 0:D], ctxT[:, k, b * P:(b + 1) * P], wv0[:, k, :],
                                       start=(k == 0), stop=(k == KC - 1))
                    mm.then_inc(T.Vp, 1)
                if j == 2 and 0 <= o < BATCH:
                    pe.wait_ge(T.oT, o + 1)
                    for k in range(KC):
                        mm = pe.matmul(bank[7][:, 0:D], att.oTb[:, k, :], qwT[:, 1, k, :],
                                       start=(k == 0), stop=(k == KC - 1))
                    mm.then_inc(T.y, 1)
                if j == 2 and b < BATCH:
                    pe.wait_ge(T.q1, b + 1)
                    pe.wait_ge(T.kf, b + 1)
                    for c in range(KC):
                        mm = pe.transpose(kbank(5)[:, c, :], att.q1[:, c * P:(c + 1) * P], ident[:, :])
                    mm.then_inc(T.QT, 1)
                if s == BATCH + 2 and j == GROUPS:
                    pe_c_pos(pe, 0)
                if 0 <= s - 4 < BATCH:
                    pe_c_gate(pe, s - 4, j)

            pe_blocks(pe, s, 0, extra)

        def act_b_step(act, s):
            b, o = s, s - 3
            if b < BATCH:
                act.wait_ge(T.hTp, b + 1)
                if b >= 2:
                    act.wait_ge(T.Qp, b - 1)
                act.copy(att.hTb[:, b % 2], bank[6][:, 0:P].bitcast(BF16).rearrange("p (k n) -> p k n", k=KC))\
                   .then_inc(T.hT, 1)

            def extra(j):
                if j == 1 and 0 <= o < BATCH:
                    act.wait_ge(T.oTp, o + 1)
                    if o >= 1:
                        act.wait_ge(T.y, o)
                    act.copy(att.oTb[:], bank[7][:, 0:P].bitcast(BF16).rearrange("p (k n) -> p k n", k=KC))\
                       .then_inc(T.oT, 1)
                if 0 <= s - 4 < BATCH:
                    act_c_gate(act, s - 4, j)

            act_blocks(act, s, 0, extra)

        def dve_b_stats(v, b):
            if b % 2 == 0:
                v.wait_ge(A.res, b // 2 + 1)
            dve_stats(v, 1, b)

        def dve_b_prep(v, b):
            v.wait_ge(LN.h, 1 * BATCH + b + 1)

            def free():
                if b >= 2:
                    v.wait_ge(T.hTp, b - 1)
            dve_quant(v, zq, b, att.h[:, b % 2, :], 1e-8, free)

        def dve_b_step(v, s):
            b, a, o = s, s - 2, s - 3
            dve_rowmax(v, s, 0, 0)
            if s == BATCH:
                dve_c_scores(v, 0)
            if b < BATCH:
                v.wait_ge(T.K, b + 1)
                if b >= 1:
                    v.wait_ge(T.km0, b)
                    v.wait_ge(T.km1, b)
                v.tensor_tensor(att.kf[:], kbank(5), bk0[:, :].unsqueeze(2).to_broadcast([P, KC, P]),
                                ALU.add).then_inc(T.kf, 1)
                v.wait_ge(T.Qp, b + 1)
                if b >= 1:
                    v.wait_ge(T.QT, b)
                v.scalar_tensor_tensor(out=att.q1[:], in0=bank[7][:, 0:D], scalar=zq.s[:, b:b + 1],
                                       in1=qw_row[:, 0, :], op0=ALU.mult, op1=ALU.mult).then_inc(T.q1, 1)
            dve_rowmax(v, s, 0, 1)
            if b + 1 < BATCH:
                dve_b_stats(v, b + 1)
            if b < BATCH:
                v.wait_ge(T.Vp, b + 1)
                if b >= 3:
                    v.wait_ge(T.O, GROUPS * (b - 2))
                v.tensor_tensor(att.v1[:, b % 3, :, 0:HD], bank[6][:, 0:D].rearrange("p (h d) -> p h d", h=HEADS),
                                bv.rearrange("p (h d) -> p h d", h=HEADS), ALU.add).then_inc(T.v1, 1)
            if 0 <= a < BATCH:
                dve_attended(v, a, lambda: None)
            dve_rowmax(v, s, 0, 2)
            if 0 <= o < BATCH:
                v.wait_ge(T.y, o + 1)
                if o >= 1:
                    v.wait_ge(T.res, o)
                v.scalar_tensor_tensor(out=att.y[:], in0=bank[7][:, 0:D], scalar=zo.s[:, o:o + 1],
                                       in1=qw_row[:, 1, :], op0=ALU.mult, op1=ALU.mult).then_inc(T.yt, 1)
                v.wait_ge(T.yt, o + 1)
                v.wait_ge(T.xb, o + 1)
                v.tensor_tensor(x_sb[:, o, :], x_sb[:, o, :], att.y[:], ALU.add).then_inc(T.res, 1)
                v.wait_ge(T.res, o + 1)
                dve_stats(v, 2, o)
            if b < BATCH:
                v.wait_ge(T.QT, b + 1)
                if b >= 2:
                    v.wait_ge(T.S, GROUPS * (b - 1))
                for c in range(KC):
                    v.tensor_scalar(att.qT[:, b % 2, c, :], kbank(5)[:, c, :], bq0[:, c:c + 1], ATT_SCALE,
                                    ALU.add, ALU.mult).then_inc(T.qT, 1)
            dve_rowmax(v, s, 0, 3)
            if b + 1 < BATCH:
                dve_b_prep(v, b + 1)
            if 0 <= a < BATCH:
                v.wait_ge(T.o, a + 1)

                def free():
                    if a >= 2:
                        v.wait_ge(T.oTp, a - 1)
                dve_quant(v, zo, a, att.o[:, a % 2], 1e-8, free)
            if s == BATCH:
                dve_c_groups(v, 0)
            if s == BATCH + 1:
                dve_c_choose(v, 0)
            if s == BATCH + 2:
                dve_c_place(v, 0)

        def pool_b_norm(g, b):
            pool_rstd(g, 1, b)
            if b >= 2:
                g.wait_ge(zq.sem.step, 4 * (b - 1))
            norm(g, 1, b, att.h[:, b % 2, :])

        def pool_b_step(g, s):
            if s < BATCH:
                key_copies(g, s, 0, T.km0)
                g.wait_ge(LN.h, BATCH + s + 1)
                g.tensor_tensor(x_sb[:, s, :], x_sb[:, s, :], bp, ALU.add).then_inc(T.xb, 1)
                if s + 1 < BATCH:
                    pool_b_norm(g, s + 1)
                key_copies(g, s, 1, T.km1)
            if 3 <= s < BATCH + 3:
                pool_rstd(g, 2, s - 3)
                norm(g, 2, s - 3, h3[:, s - 3, :])
            if s == BATCH + 2:
                pool_c_scatter(g, range(HALF))

        C = sems("c", "hTp hT lg ex route placed sel pos srow grow zeroed scat sup_ rel sq sdn shy "
                      "xT xTs up hr h2 dn ye acc "
                      "x0 x1 x2 x3 w0 w1 w2 w3 out0 out1 out2 out3 gat0 gat1")
        h3 = views(h3_flat)([P, BATCH, D])
        hT3 = views(hT3_flat)([P, KC, TOK])
        HALF = BATCH // 2
        BE = [P, BATCH, EXPERTS]
        HE = [P, HALF, EXPERTS]
        BKE = [P, HALF * TOPK, EXPERTS]
        take = views(scratch)
        c_ex = take(BE)
        c_sg, c_sc, c_ms, c_ms0 = (take(HE) for _ in range(4))
        c_mx, c_mn = (take([P, HALF * EGROUPS, 2]) for _ in range(2))
        c_hi, c_lo, c_m3, c_sec, c_gs, c_rk, c_mk = (
            take([P, HALF * EGROUPS]) for _ in range(7))
        c_gt, c_eq, c_eql, c_rk1 = (take([P, HALF * EGROUPS, EGROUPS]) for _ in range(4))
        c_top = sb("c_top", [P, HALF, 8])
        c_idx = sb("c_idx", [P, HALF, 8], U32)
        c_idxf = sb("c_idxf", [P, HALF, TOPK])
        c_oh = take(BKE)
        c_tmp, c_tmp2 = take(BKE), take(BKE)
        c_sel = sb("c_sel", BE, BF16)
        c_w4, c_p4, c_ok, c_drop, c_row, c_pc = (
            sb(f"c_{n}", [P, HALF, TOPK]) for n in ("w4", "p4", "ok", "drop", "row", "pc"))
        c_wv = sb("c_wv", [P, BATCH, TOPK])
        c_ws, c_wr = sb("c_ws", [P, HALF]), sb("c_wr", [P, HALF])
        c_srow, c_grow = sb("c_srow", [P, BATCH, TOPK], U32), sb("c_grow", [P, BATCH, TOPK], U32)
        RING = 8
        GROUP = 8
        EW = [P, GROUP, 2 * D]
        take = views(scratch[:, GROUP * 2 * D:])
        e_xT, e_r, e_h = take([P, 2, KC, P]), take([P, 2, P]), take([P, 2, P])
        e_w = (sb("e_w", EW)[:], take(EW), views(km_flat)(EW), views(scratch)(EW))
        e_x = sb("e_x", [P, RING, D])
        e_y = views(w0_flat)([P, RING, D])
        x_in = (C.x0, C.x1, C.x2, C.x3)
        w_in = (C.w0, C.w1, C.w2, C.w3)
        e_out = (C.out0, C.out1, C.out2, C.out3)
        gat = (C.gat0, C.gat1)
        zrow = sb("zrow", [P, 1024])
        take = views(w0_flat)
        c_sr, c_sT = take([P, SC, 512]), take([P, SC, 512])
        g_y = views(w0_flat)([P, 2, TOPK, D])
        xe_dram = nc.dram_tensor("xe_dram", [EXPERTS * CAP, D], F32).ap()
        ye_dram = nc.dram_tensor("ye_dram", [EXPERTS * CAP, D], F32).ap()
        bg = "p (b g) -> p b g"

        def pe_c_gate(pe, b, j):
            if j == 2:
                pe.wait_ge(LN4.h, b + 1)
                pe.wait_ge(T.v1, min(b + 5, BATCH))
                if b >= 1:
                    pe.wait_ge(C.ex, b)
                for k in range(KC):
                    mm = pe.transpose(bank[6][:, k * P:(k + 1) * P], h3[:, b, k * P:(k + 1) * P], ident[:, :])
                mm.then_inc(C.hTp, 1)
            if j == 3:
                pe.wait_ge(C.hT, b + 1)
                if b == 0:
                    pe.wait_ge(ld.moe, 48)
                for k in range(KC):
                    mm = pe.matmul(bank[6][:, 0:EXPERTS], hT3[:, k, b * P:(b + 1) * P], gate[:, k, :],
                                   start=(k == 0), stop=(k == KC - 1))
                mm.then_inc(C.lg, 1)

        def act_c_gate(act, b, j):
            if j == 2:
                act.wait_ge(C.hTp, b + 1)
                act.copy(hT3[:, :, b * P:(b + 1) * P], bank[6][:, 0:D].rearrange("p (k n) -> p k n", k=KC))\
                   .then_inc(C.hT, 1)
            if j == 3:
                act.wait_ge(C.lg, b + 1)
                act.activation(c_ex[:, b, :], bank[6][:, 0:EXPERTS], ACT.Exp, scale=-1.0).then_inc(C.ex, 1)

        def pe_c_up(pe, half):
            pe.wait_ge(C.hT, HALF * (half + 1))
            for m in range(SC):
                n = SC * half + m
                if n < 2:
                    pe.wait_ge(T.P, HEADS * BATCH)
                else:
                    pe.wait_ge(C.rel, n - 1)
                for k in range(KC):
                    mm = pe.matmul(bank[n % 2][:, :], sup[:, k, m * P:(m + 1) * P],
                                   hT3[:, k, half * 512:(half + 1) * 512], start=(k == 0), stop=(k == KC - 1))
                mm.then_inc(C.sup_, 1)

        def pe_c_down(pe, tiles):
            pe.wait_ge(C.sq, SC * (tiles[0] // HALF + 1))
            for b in tiles:
                i = b % HALF
                for m in range(SC):
                    mm = pe.matmul(bank[4 + b // 2][:, (b % 2) * D:(b % 2 + 1) * D],
                                   c_sT[:, m, i * P:(i + 1) * P], sdown[:, m, :],
                                   start=(m == 0), stop=(m == SC - 1))
                mm.then_inc(C.sdn, 1)

        def pe_c_pos(pe, half):
            first = HALF * half
            pe.wait_ge(C.sel, half + 1)
            if half:
                pe.wait_ge(C.placed, 1)
            else:
                pe.wait_ge(T.qT, 2 * BATCH)
            out = bank[5][:, 0:HALF * EXPERTS].rearrange("p (b e) -> p b e", b=HALF)
            for b in range(first + HALF - 1):
                at = max(b + 1 - first, 0)
                pe.matmul(out[:, at:, :], onesb[:, :],
                          c_sel[:, b, :].unsqueeze(1).to_broadcast([P, HALF - at, EXPERTS]),
                          start=(b == 0), stop=False, skip_group_check=True)
            at = 0 if half else 1
            mm = pe.matmul(out[:, at:, :], before[:, :], c_sel[:, first + at:first + HALF, :],
                           start=False, stop=True, skip_group_check=True)
            if not half:
                mm = pe.matmul(out[:, 0, :], before[:, :], c_sel[:, 0, :], start=True, stop=True)
            mm.then_inc(C.pos, 1)

        def pe_x_transpose(pe, e):
            if e % 2 == 0:
                pe.wait_ge(x_in[e // 2 % 4], 16 * (e // RING + 1))
            if e >= 2:
                pe.wait_ge(C.xTs, e - 1)
            for k in range(KC):
                mm = pe.transpose(bank[e % 2][:, k * P:(k + 1) * P], e_x[:, e % RING, k * P:(k + 1) * P], ident[:, :])
            mm.then_inc(C.xT, 1)

        def pe_x_up(pe, e):
            pe.wait_ge(C.xTs, e + 1)
            if e % GROUP == 0:
                pe.wait_ge(w_in[e // GROUP], 16)
            if e >= 2:
                pe.wait_ge(C.hr, e - 1)
            for k in range(KC):
                mm = pe.matmul(bank[2 + e % 2][:, 0:P], e_w[e // GROUP][:, e % GROUP, k * HID:(k + 1) * HID],
                               e_xT[:, e % 2, k, :], start=(k == 0), stop=(k == KC - 1))
            mm.then_inc(C.up, 1)

        def pe_x_down(pe, e):
            pe.wait_ge(C.h2, e + 1)
            if e < 2:
                pe.wait_ge(C.shy, e + 1)
            if e >= 2:
                pe.wait_ge(C.ye, e - 1)
            pe.matmul(bank[4 + e % 2][:, 0:D], e_h[:, e % 2, :], e_w[e // GROUP][:, e % GROUP, D:2 * D],
                      start=True, stop=True).then_inc(C.dn, 1)

        def act_c_shared(act, half):
            for m in range(SC):
                n = SC * half + m
                act.wait_ge(C.sup_, n + 1)
                if half:
                    act.wait_ge(C.sq, n - SC + 1)
                act.activation(c_sr[:, m, :], bank[n % 2][:, :], ACT.Relu).then_inc(C.rel, 1)
                act.wait_ge(C.rel, n + 1)
                if half and m == 0:
                    act.wait_ge(C.sdn, 4)
                act.activation(c_sT[:, m, :], c_sr[:, m, :], ACT.Square).then_inc(C.sq, 1)

        def act_x(act, e):
            if e < EXPERTS:
                act.wait_ge(C.xT, e + 1)
                if e >= 2:
                    act.wait_ge(C.up, e - 1)
                act.copy(e_xT[:, e % 2], bank[e % 2][:, 0:D].rearrange("p (k n) -> p k n", k=KC)).then_inc(C.xTs, 1)
            if e >= 1:
                e -= 1
                act.wait_ge(C.up, e + 1)
                if e >= 2:
                    act.wait_ge(C.h2, e - 1)
                act.activation(e_r[:, e % 2, :], bank[2 + e % 2][:, 0:P], ACT.Relu).then_inc(C.hr, 1)

        def dve_x(v, e):
            if e < EXPERTS:
                v.wait_ge(C.hr, e + 1)
                if e >= 2:
                    v.wait_ge(C.dn, e - 1)
                v.tensor_tensor(e_h[:, e % 2, :], e_r[:, e % 2, :], e_r[:, e % 2, :], ALU.mult).then_inc(C.h2, 1)
            if e >= 1:
                e -= 1
                if e == 0:
                    v.wait_ge(C.sq, 2 * SC)
                v.wait_ge(C.dn, e + 1)
                if e >= RING and e % 2 == 0:
                    v.wait_ge(e_out[e // 2 % 4], 16 * (e // RING))
                v.tensor_copy(e_y[:, e % RING, :], bank[4 + e % 2][:, 0:D]).then_inc(C.ye, 1)

        route_steps = [0]

        def done(v, *steps):
            for ins in steps:
                ins.then_inc(C.route, 1)
            route_steps[0] += len(steps)
            v.wait_ge(C.route, route_steps[0])

        def flat_e(a):
            return a.rearrange("p b e -> p (b e)")

        quad = flat_e(c_sc).rearrange("p (n i) -> p n i", i=EPG)

        def dve_c_scores(v, half):
            tiles = slice(HALF * half, HALF * (half + 1))
            v.wait_ge(C.ex, HALF * (half + 1))
            done(v, v.tensor_scalar(flat_e(c_sg), flat_e(c_ex[:, tiles, :]), 1.0, None, ALU.add))
            done(v, v.reciprocal(flat_e(c_sg), flat_e(c_sg)))
            done(v, v.tensor_tensor(c_sc, c_sg, rbias[:, :].unsqueeze(1).to_broadcast(HE), ALU.add))
            done(v, v.tensor_tensor(c_mx, quad[:, :, 0::2], quad[:, :, 1::2], ALU.max),
                 v.tensor_tensor(c_mn, quad[:, :, 0::2], quad[:, :, 1::2], ALU.min))
            done(v, v.tensor_tensor(c_hi, c_mx[:, :, 0], c_mx[:, :, 1], ALU.max),
                 v.tensor_tensor(c_lo, c_mx[:, :, 0], c_mx[:, :, 1], ALU.min),
                 v.tensor_tensor(c_m3, c_mn[:, :, 0], c_mn[:, :, 1], ALU.max))
            done(v, v.tensor_tensor(c_sec, c_lo, c_m3, ALU.max))
            done(v, v.tensor_tensor(c_gs, c_hi, c_sec, ALU.add))

        def dve_c_groups(v, half):
            gs3 = c_gs.rearrange("p (b g) -> p b g", b=HALF)
            gfull = [P, HALF, EGROUPS, EGROUPS]
            other = gs3.unsqueeze(2).to_broadcast(gfull)
            own = gs3.unsqueeze(3).to_broadcast(gfull)
            g4 = lambda a: a.rearrange("p (b g) o -> p b g o", b=HALF)
            done(v, v.tensor_tensor(g4(c_gt), other, own, ALU.is_gt),
                 v.tensor_tensor(g4(c_eq), other, own, ALU.is_equal))
            done(v, v.tensor_tensor(g4(c_eql), g4(c_eq), lower_g[:].unsqueeze(1).to_broadcast(gfull), ALU.mult))
            done(v, v.tensor_tensor(c_rk1, c_gt, c_eql, ALU.add))
            done(v, v.tensor_reduce(c_rk, c_rk1, AX.X, ALU.add))
            done(v, v.tensor_scalar(c_mk, c_rk, float(KEPT_GROUPS), None, ALU.is_lt))
            done(v, v.tensor_tensor(flat_e(c_ms0).rearrange("p (n i) -> p n i", i=EPG), quad,
                                    c_mk.unsqueeze(2).to_broadcast([P, HALF * EGROUPS, EPG]), ALU.mult))
            done(v, v.tensor_scalar(flat_e(c_ms), flat_e(c_ms0), 0.0, None, ALU.add))

        def dve_c_choose(v, half):
            tiles = slice(HALF * half, HALF * (half + 1))
            done(v, *[v.max(c_top[:, b, :], c_ms[:, b, :]) for b in range(HALF)])
            done(v, *[v.max_index(c_idx[:, b, :], c_top[:, b, :], c_ms[:, b, :]) for b in range(HALF)])
            done(v, v.tensor_copy(c_idxf[:], c_idx[:, :, 0:TOPK]))
            done(v, v.tensor_tensor(c_oh, c_idxf[:].rearrange("p b k -> p (b k)").unsqueeze(2).to_broadcast(BKE),
                                    iota_e[:, :].unsqueeze(1).to_broadcast(BKE), ALU.is_equal))
            with nc.allow_low_precision(reason="a choice count is 0 or 1"):
                v.tensor_reduce(c_sel[:, tiles, :], c_oh.rearrange("p (b k) e -> p b e k", b=HALF), AX.X, ALU.add)\
                 .then_inc(C.sel, 1)
            done(v, v.tensor_tensor(k4(c_tmp), k4(c_oh), c_sg.unsqueeze(2).to_broadcast(full4), ALU.mult))
            done(v, v.tensor_reduce(bk(c_w4[:]), c_tmp, AX.X, ALU.add))

        full4 = [P, HALF, TOPK, EXPERTS]

        def k4(a):
            return a.rearrange("p (b k) e -> p b k e", b=HALF)

        def bk(a):
            return a.rearrange("p b k -> p (b k)")

        def dve_c_place(v, half):
            tiles = slice(HALF * half, HALF * (half + 1))
            v.wait_ge(C.pos, half + 1)
            v.tensor_tensor(k4(c_tmp2), k4(c_oh), bank[5][:, 0:HALF * EXPERTS].rearrange("p (b e) -> p b e", b=HALF)
                            .unsqueeze(2).to_broadcast(full4), ALU.mult).then_inc(C.placed, 1)
            v.wait_ge(C.placed, half + 1)
            done(v, v.tensor_reduce(bk(c_p4[:]), c_tmp2, AX.X, ALU.add))
            done(v, v.tensor_scalar(bk(c_drop[:]), bk(c_p4[:]), float(CAP), SKIP, ALU.is_ge, ALU.mult),
                 v.scalar_tensor_tensor(out=bk(c_row[:]), in0=bk(c_idxf[:]), scalar=float(CAP), in1=bk(c_p4[:]),
                                        op0=ALU.mult, op1=ALU.add),
                 v.tensor_scalar(bk(c_pc[:]), bk(c_p4[:]), float(CAP - 1), None, ALU.min))
            v.tensor_tensor(bk(c_srow[:, tiles, :]), bk(c_row[:]), bk(c_drop[:]), ALU.add).then_inc(C.srow, 1)
            v.scalar_tensor_tensor(out=bk(c_grow[:, tiles, :]), in0=bk(c_idxf[:]), scalar=float(CAP), in1=bk(c_pc[:]),
                                   op0=ALU.mult, op1=ALU.add).then_inc(C.grow, 1)
            wv = c_wv[:, tiles, :]
            done(v, v.tensor_reduce(c_ws[:], c_w4[:], AX.X, ALU.add),
                 v.tensor_scalar(bk(c_ok[:]), bk(c_p4[:]), float(CAP), ROUTE_SCALE, ALU.is_lt, ALU.mult))
            done(v, v.tensor_scalar(c_ws[:], c_ws[:], 1e-20, None, ALU.add))
            done(v, v.reciprocal(c_wr[:], c_ws[:]))
            done(v, v.tensor_tensor(wv, c_w4[:], c_wr[:].unsqueeze(2).to_broadcast([P, HALF, TOPK]), ALU.mult))
            done(v, v.tensor_tensor(bk(wv), bk(wv), bk(c_ok[:]), ALU.mult))

        def dve_c_shared(v):
            for p in range(PAIRS):
                v.wait_ge(C.sdn, 2 * p + 2)
                v.tensor_tensor(x_sb[:, 2 * p:2 * p + 2, :], x_sb[:, 2 * p:2 * p + 2, :],
                                bank[4 + p][:, :].rearrange("p (i n) -> p i n", i=2), ALU.add).then_inc(C.shy, 1)

        def dve_c_combine(v, b):
            v.wait_ge(gat[b % 2], 16 * TOPK * (b // 2 + 1))
            if b == 0:
                v.wait_ge(C.shy, PAIRS)
            for k in range(TOPK):
                v.scalar_tensor_tensor(out=x_sb[:, b, :], in0=g_y[:, b % 2, k, :], scalar=c_wv[:, b, k:k + 1],
                                       in1=x_sb[:, b, :], op0=ALU.mult, op1=ALU.add).then_inc(C.acc, 1)
                v.wait_ge(C.acc, TOPK * b + k + 1)

        def pool_c_scatter(g, tiles):
            g.wait_ge(C.srow, tiles[-1] // HALF + 1)
            if tiles[0] == 0:
                g.wait_ge(C.zeroed, 16 * 4)
            for b in tiles:
                for k in range(TOPK):
                    g.indirect_dma_start(xe_dram, bass.IndirectOffsetOnAxis(ap=c_srow[:, b, k:k + 1], axis=0),
                                         h3[:, b, :], None, bounds_check=EXPERTS * CAP - 1, oob_is_err=False)\
                     .then_inc(C.scat, 16)

        def pool_c_gather(g, b):
            if b == 0:
                g.wait_ge(C.grow, 2)
                g.wait_ge(C.sq, 2 * SC)
                for i in range(4):
                    g.wait_ge(e_out[i], 16 * EXPERTS // RING)
            if b >= 2:
                g.wait_ge(C.acc, TOPK * (b - 1))
            for k in range(TOPK):
                g.indirect_dma_start(g_y[:, b % 2, k, :], None, ye_dram,
                                     bass.IndirectOffsetOnAxis(ap=c_grow[:, b, k:k + 1], axis=0),
                                     bounds_check=EXPERTS * CAP - 1, oob_is_err=False).then_inc(gat[b % 2], 16)


        def leave_bank(o):
            return 7 if o < 2 * BATCH - 2 else 6

        def pe_leave_turn(pe, o):
            for k in range(KC):
                mm = pe.transpose(bank[leave_bank(o)][:, k * P:(k + 1) * P], att.o[:, o % 2, k * P:(k + 1) * P],
                                  ident[:, :])
            mm.then_inc(T.oTp, 1)

        def pe_leave_out(pe, o):
            pe.wait_ge(T.oT, o + 1)
            for k in range(KC):
                mm = pe.matmul(bank[leave_bank(o)][:, 0:D], att.oT[:, k, :], wo1[:, k, :],
                               start=(k == 0), stop=(k == KC - 1))
            mm.then_inc(T.y, 1)

        def act_leave(act, o):
            act.wait_ge(T.oTp, o + 1)
            act.wait_ge(T.y, o)
            act.copy(att.oT[:], bank[leave_bank(o)][:, 0:D].rearrange("p (k n) -> p k n", k=KC)).then_inc(T.oT, 1)

        def dve_leave(v, o):
            v.wait_ge(T.y, o + 1)
            v.tensor_tensor(x_sb[:, o - BATCH, :], x_sb[:, o - BATCH, :], bank[leave_bank(o)][:, 0:D], ALU.add)\
             .then_inc(T.res, 1)
            v.wait_ge(T.res, o + 1)
            dve_stats(v, 4, o - BATCH)

        def pe_d_step(pe, s):
            b, o = BATCH + s, BATCH + s - 3
            def enter(b):
                pe.wait_ge(LN.h, BATCH + b + 1)
                pe.wait_ge(T.v1, b)
                for k in range(KC):
                    mm = pe.transpose(bank[6][:, k * P:(k + 1) * P], att.h[:, b % 2, k * P:(k + 1) * P], ident[:, :])
                mm.then_inc(T.hTp, 1)

            if s == 0:
                enter(b)

            def extra(j):
                pe_e(pe, s, j)
                pe_f(pe, s, j)
                if j == 3 and s + 1 < BATCH:
                    enter(b + 1)
                if j == 0 and s < BATCH:
                    pe.wait_ge(T.hT, b + 1)
                    pe.wait_ge(T.qT, 2 * b)
                    for k in range(KC):
                        mm = pe.matmul(bank[5][:, 0:P], wk1[:, k, :], att.hT[:, b % 2, k, :],
                                       start=(k == 0), stop=(k == KC - 1))
                    mm.then_inc(T.K, 1)
                if j == 1 and s >= 3:
                    pe.wait_ge(T.o, o + 1)
                    if s >= 4:
                        pe.wait_ge(T.res, o)
                    if e_pair(s, 5) is not None:
                        pe.wait_ge(E.kT, e_pair(s, 5) + 1)
                    if e_pair(s, 8) is not None:
                        pe.wait_ge(F.t1, 2 * e_pair(s, 8) + 1)
                    pe_leave_turn(pe, o)
                if j == 1 and s < BATCH:
                    for k in range(KC):
                        mm = pe.matmul(bank[6][:, 0:P], att.hT[:, b % 2, k, :], wv1[:, k, :],
                                       start=(k == 0), stop=(k == KC - 1))
                    mm.then_inc(T.Vp, 1)
                if j == 2 and s >= 3:
                    pe_leave_out(pe, o)
                if j == 2 and s < BATCH:
                    pe.wait_ge(T.kf, b + 1)
                    for c in range(KC):
                        for k in range(KC):
                            mm = pe.matmul(kbank(5)[:, c, :], wq1[:, k, c * P:(c + 1) * P], att.hT[:, b % 2, k, :],
                                           start=(k == 0), stop=(k == KC - 1))
                    mm.then_inc(T.QT, 1)

            pe_blocks(pe, s, 1, extra)

        def act_d_step(act, s):
            b, o = BATCH + s, BATCH + s - 3
            if s < BATCH:
                act.wait_ge(T.hTp, b + 1)
                act.wait_ge(T.QT, b - 1)
                act.copy(att.hT[:, b % 2], bank[6][:, 0:D].rearrange("p (k n) -> p k n", k=KC)).then_inc(T.hT, 1)

            def extra(j):
                if j == 0 and s < BATCH:
                    act.wait_ge(T.K, b + 1)
                    act.wait_ge(T.km0, b)
                    act.wait_ge(T.km1, BATCH)
                    act.copy(att.kf[:, 0, :], bank[5][:, 0:P]).then_inc(T.kf, 1)
                act_e(act, s, j)
                if s == BATCH - 1 and j == GROUPS:
                    act_f(act, 0)
                if j == 1 and s >= 3:
                    act_leave(act, o)
                if j == 2 and s < BATCH:
                    act.wait_ge(T.QT, b + 1)
                    act.wait_ge(T.S, GROUPS * (b - 1))
                    act.activation(att.qT[:, b % 2], kbank(5), ACT.Copy, scale=ATT_SCALE).then_inc(T.qT, 2)

            act_blocks(act, s, 1, extra)

        def dve_d_prep(v, b):
            v.wait_ge(T.hTp, BATCH + b - 1)
            norm(v, 3, b, att.h[:, b % 2, :])

        def dve_d_step(v, s):
            b, a, o = BATCH + s, BATCH + s - 2, BATCH + s - 3
            if e_pair(s, 7) is not None:
                dve_e_residual(v, e_pair(s, 7))
            dve_rowmax(v, s, 1, 0)
            if e_pair(s, 8) is not None:
                dve_f_out(v, 2 * e_pair(s, 8))
            if e_pair(s, 6) is not None:
                dve_e_states(v, e_pair(s, 6))
            dve_rowmax(v, s, 1, 1)
            if s + 1 < BATCH:
                dve_c_combine(v, s + 1)
                dve_stats(v, 3, s + 1)
            if s < BATCH:
                v.wait_ge(T.Vp, b + 1)
                v.wait_ge(T.O, GROUPS * (b - 2))
                v.tensor_copy(att.v1[:, b % 3, 0:KV_HEADS, 0:HD],
                              bank[6][:, 0:P].rearrange("p (h d) -> p h d", h=KV_HEADS))\
                 .then_inc(T.v1, 1)
            if s >= 2:
                dve_attended(v, a, lambda: v.wait_ge(T.oTp, a - 1))
            if e_pair(s, 5) is not None:
                dve_e_maxima(v, e_pair(s, 5))
            if e_pair(s, 6) is not None:
                dve_e_reciprocal(v, e_pair(s, 6), 0)
            dve_rowmax(v, s, 1, 2)
            if s >= 3:
                dve_leave(v, o)
            if e_pair(s, 5) is not None:
                dve_e_clamp(v, e_pair(s, 5))
            if e_pair(s, 6) is not None:
                dve_e_reciprocal(v, e_pair(s, 6), 1)
            if s + 1 < BATCH:
                dve_d_prep(v, s + 1)
            dve_rowmax(v, s, 1, 3)
            if s >= 3:
                dve_e_norm(v, o - BATCH)
            if e_pair(s, 6) is not None:
                dve_e_quotient(v, e_pair(s, 6))
            if s >= 7:
                dve_f_in(v, s - 7)

        E = sems("e", "hTp kT ov e rel a2 e2 z r kv rv p q num den rd y yTp res zero")
        take = views(scratch)
        f_h = take([P, 2, 2, D])
        SEQS = 2 * KC
        WS = [P, SEQS, SEQ + 1]
        f_dec, f_kT, f_o, f_a2, f_e2, f_kv, f_p, f_q = (take(WS) for _ in range(8))
        W = [P, SEQS, SEQ]
        f_e, f_z, f_r, f_rv, f_num, f_den = (take(W) for _ in range(6))
        take = views(hT3_flat)
        f_up, f_down = take(W), take(W)
        f_rd = f_z
        E_CLAMP = 60.0

        def flat(a):
            return a.rearrange("p s n -> p (s n)")

        def chunk(a, k):
            return a[:, 2 * k:2 * k + 2, :]

        def e_pair(s, first):
            p, rest = divmod(s - first, 2)
            return p if rest == 0 and 0 <= p < PAIRS else None

        def seqs(n):
            return bank[n][:, :].rearrange("p (s n) -> p s n", s=SEQS)

        def pe_e_in(pe, p):
            for i in range(2):
                pe.wait_ge(LN4.h, BATCH + 2 * p + i + 1)
            for i in range(2):
                for k in range(KC):
                    mm = pe.transpose(seqs(7)[:, 2 * k + i, :], f_h[:, p % 2, i, k * P:(k + 1) * P], ident[:, :])
            mm.then_inc(E.hTp, 1)

        def pe_e_out(pe, p):
            pe.wait_ge(E.y, p + 1)
            for i in range(2):
                for k in range(KC):
                    mm = pe.transpose(bank[7][:, i * D + k * P:i * D + (k + 1) * P], f_num[:, 2 * k + i, :],
                                      ident[:, :])
            mm.then_inc(E.yTp, 1)

        def pe_e(pe, s, j):
            p = e_pair(s, 5)
            if p is not None and j == 0:
                pe.wait_ge(T.res, BATCH + s - 3)
                if p >= 1:
                    pe.wait_ge(E.res, p)
                pe_e_in(pe, p)
            p = e_pair(s, 6)
            if p is not None and j == GROUPS and s < BATCH:
                pe.wait_ge(T.res, BATCH + s - 2)
                pe_e_out(pe, p)

        def act_e_keys(act, p):
            act.wait_ge(E.hTp, p + 1)
            if p >= 1:
                act.wait_ge(E.e, p)
            else:
                act.wait_ge(E.zero, 8)
            act.copy(f_kT[:, :, 1:], seqs(7)).then_inc(E.kT, 1)

        def act_e_states(act, p):
            act.wait_ge(E.e, p + 1)
            for k in range(KC):
                act.activation(chunk(f_up, k), chunk(f_e, k), ACT.Relu, bias=minus_decay[:, k:k + 1]).then_inc(E.rel, 1)
                act.activation(chunk(f_down, k), chunk(f_e, k), ACT.Relu, bias=decay[:, k:k + 1], scale=-1.0)\
                   .then_inc(E.rel, 1)
            act.wait_ge(E.rel, 2 * KC * (p + 1))
            if p >= 1:
                act.wait_ge(E.q, p)
                act.wait_ge(E.p, p)
            act.activation(f_a2[:, :, 1:], f_up, ACT.Exp, scale=-1.0).then_inc(E.a2, 1)
            act.activation(f_e2[:, :, 1:], f_down, ACT.Exp, scale=-1.0).then_inc(E.e2, 1)

        def act_e_ratio(act, p):
            act.wait_ge(E.z, KC * (p + 1))
            act.activation(f_r, f_z, ACT.Exp).then_inc(E.r, 1)

        def act_e(act, s, j):
            p = e_pair(s, 5)
            if p is not None and j == 0:
                act_e_keys(act, p)
            if p is not None and j == 2:
                act_e_states(act, p)
            if p is not None and j == 3:
                act_e_ratio(act, p)

        def values_of(p):
            return ctxT[:, :, 2 * p * P:(2 * p + 2) * P].rearrange("p k (i n) -> p k i n", i=2)

        def four(a):
            return a.rearrange("p (k i) n -> p k i n", k=KC)

        def pool_e_kv(g, p):
            g.wait_ge(E.e2, p + 1)
            if p >= 1:
                g.wait_ge(E.p, p)
            g.tensor_tensor(four(f_kv[:, :, 1:]), four(f_e2[:, :, 1:]), values_of(p), ALU.mult).then_inc(E.kv, 1)

        def pool_e_rv(g, p):
            g.wait_ge(E.r, p + 1)
            if p >= 1:
                g.wait_ge(E.num, p)
            g.tensor_tensor(four(f_rv), four(f_r), values_of(p), ALU.mult).then_inc(E.rv, 1)

        def dve_e_setup(v):
            for a, value in ((f_dec, NEG_BIG), (f_kT, NEG_BIG), (f_a2, 0.0), (f_e2, 0.0), (f_kv, 0.0)):
                v.memset(a[:, :, 0], value).then_inc(E.zero, 1)
            for k in range(KC):
                v.tensor_copy(chunk(f_dec, k)[:, :, 1:], decay[:, k:k + 1].unsqueeze(2).to_broadcast([P, 2, SEQ]))\
                 .then_inc(E.zero, 1)
            v.tensor_scalar(minus_decay[:, :], decay[:, :], -1.0, None, ALU.mult).then_inc(E.zero, 1)
            v.wait_ge(E.zero, 8)

        def dve_e_norm(v, b):
            if b >= 4:
                v.wait_ge(E.hTp, b // 2 - 1)
            norm(v, 4, b, f_h[:, b // 2 % 2, b % 2, :])

        def dve_e_maxima(v, p):
            v.wait_ge(E.kT, p + 1)
            v.tensor_tensor_scan(flat(f_o), flat(f_dec), flat(f_kT), 0.0, ALU.add, ALU.max).then_inc(E.ov, 1)
            v.wait_ge(E.ov, p + 1)
            if p >= 1:
                v.wait_ge(E.rel, 2 * KC * p)
                v.wait_ge(E.z, KC * p)
            v.tensor_tensor(f_e, f_kT[:, :, 1:], f_o[:, :, 0:SEQ], ALU.subtract).then_inc(E.e, 1)

        def dve_e_clamp(v, p):
            v.wait_ge(E.e, p + 1)
            if p >= 1:
                v.wait_ge(E.y, p)
            for k in range(KC):
                v.tensor_scalar(chunk(f_z, k), chunk(f_e, k), bonus[:, k:k + 1], E_CLAMP, ALU.add, ALU.min)\
                 .then_inc(E.z, 1)

        def dve_e_states(v, p):
            v.wait_ge(E.a2, p + 1)
            v.wait_ge(E.e2, p + 1)
            v.tensor_tensor_scan(flat(f_q), flat(f_a2), flat(f_e2), 0.0, ALU.mult, ALU.add).then_inc(E.q, 1)
            v.wait_ge(E.kv, p + 1)
            v.tensor_tensor_scan(flat(f_p), flat(f_a2), flat(f_kv), 0.0, ALU.mult, ALU.add).then_inc(E.p, 1)

        def dve_e_reciprocal(v, p, part):
            if part == 0:
                v.wait_ge(E.r, p + 1)
                v.wait_ge(E.q, p + 1)
                v.tensor_tensor(f_den, f_q[:, :, 0:SEQ], f_r, ALU.add).then_inc(E.den, 1)
                v.wait_ge(E.den, p + 1)
            v.reciprocal(chunk(f_rd, part), chunk(f_den, part)).then_inc(E.rd, 1)

        def dve_e_quotient(v, p):
            v.wait_ge(E.rv, p + 1)
            v.wait_ge(E.p, p + 1)
            if p >= 1:
                v.wait_ge(E.yTp, p)
            v.tensor_tensor(f_num, f_p[:, :, 0:SEQ], f_rv, ALU.add).then_inc(E.num, 1)
            v.wait_ge(E.num, p + 1)
            v.wait_ge(E.rd, 2 * (p + 1))
            v.tensor_tensor(f_num, f_num, f_rd, ALU.mult).then_inc(E.y, 1)

        def dve_e_residual(v, p):
            v.wait_ge(E.yTp, p + 1)
            v.tensor_tensor(x_sb[:, 2 * p:2 * p + 2, :], x_sb[:, 2 * p:2 * p + 2, :],
                            bank[7][:, :].rearrange("p (i n) -> p i n", i=2), ALU.add).then_inc(E.res, 1)
            v.wait_ge(E.res, p + 1)
            for i in range(2):
                dve_stats(v, 5, 2 * p + i)

        F = sems("f", "hTp hT y t1 t2 res out")
        take = views(w0_flat)
        g_h, g_t1 = take([P, 2, D]), take([P, 2, D])
        g_hT = sb("g_hT", [P, 2, KC, P], BF16)
        g_t2 = sb("g_t2", [P, 2, D], F16)
        g_o = views(w0_flat[:, 8 * D:])([P, BATCH, D])

        def f_bank(b):
            return 7 if b == 0 else 6

        def pe_f_product(pe, b):
            pe.wait_ge(F.hT, b + 1)
            for k in range(KC):
                mm = pe.matmul(bank[f_bank(b)][:, 0:D], g_hT[:, b % 2, k, :], wfb[:, k, :],
                               start=(k == 0), stop=(k == KC - 1))
            mm.then_inc(F.y, 1)

        def pe_f_turn(pe, b):
            pe.wait_ge(zq.sem.q, BATCH + b + 1)
            if b == 0:
                pe.wait_ge(T.qT, 4 * BATCH)
            else:
                pe.wait_ge(F.hT, b)
            for k in range(KC):
                mm = pe.transpose(bank[5][:, 0:P].bitcast(BF16).rearrange("p (k n) -> p k n", k=KC)[:, k, :],
                                  zq.q[:, b % 2, k * P:(k + 1) * P], identb[:, :])
            mm.then_inc(F.hTp, 1)

        def pe_f(pe, s, j):
            if s == BATCH - 1 and j == GROUPS:
                pe_f_turn(pe, 0)
            if s == BATCH and j == 0:
                pe.wait_ge(cst.wfb, 1)
                pe.wait_ge(T.res, BATCH + s - 3)
                pe.wait_ge(E.kT, 2)
                pe.wait_ge(E.res, 1)
                pe_f_product(pe, 0)

        def act_f(act, b):
            act.wait_ge(F.hTp, b + 1)
            if b >= 2:
                act.wait_ge(F.y, b - 1)
            act.copy(g_hT[:, b % 2], bank[5][:, 0:P].bitcast(BF16).rearrange("p (k n) -> p k n", k=KC))\
               .then_inc(F.hT, 1)

        def pool_f_norm(g, b):
            pool_rstd(g, 5, b)
            if b >= 2:
                g.wait_ge(zq.sem.step, 4 * (BATCH + b - 1))
            norm(g, 5, b, g_h[:, b % 2, :])

        def dve_f_in(v, b):
            v.wait_ge(LN5.h, b + 1)

            def free():
                if b >= 2:
                    v.wait_ge(F.hTp, b - 1)
            dve_quant(v, zq, BATCH + b, g_h[:, b % 2, :], 1e-7 / 127.0, free)

        def dve_f_out(v, b):
            v.wait_ge(F.y, b + 1)
            if b >= 2:
                v.wait_ge(F.t2, b - 1)
            v.scalar_tensor_tensor(out=g_t1[:, b % 2, :], in0=bank[f_bank(b)][:, 0:D],
                                   scalar=zq.s[:, BATCH + b:BATCH + b + 1],
                                   in1=wscale, op0=ALU.mult, op1=ALU.mult).then_inc(F.t1, 1)

        def f_residual(e, b):
            e.wait_ge(F.t1, b + 1)
            e.tensor_tensor(g_t2[:, b % 2, :], g_t1[:, b % 2, :], fbias, ALU.add).then_inc(F.t2, 1)
            e.wait_ge(F.t2, b + 1)
            e.tensor_tensor(g_o[:, b, :], x_sb[:, b, :], g_t2[:, b % 2, :], ALU.add).then_inc(F.res, 1)

        block = ctx.enter_context(nc.Block())
        LAST = BATCH + 4
        LAST_D = BATCH + 1

        def pe_tail(pe):
            pe.wait_ge(T.o, 2 * BATCH - 1)
            pe.wait_ge(T.v1, 2 * BATCH)
            pe_leave_turn(pe, 2 * BATCH - 2)
            pe_turn(pe, 2 * BLOCKS - 1)
            pe_values(pe, 2 * BLOCKS - 2)
            pe_values(pe, 2 * BLOCKS - 1)
            pe_leave_out(pe, 2 * BATCH - 2)
            pe.wait_ge(T.res, 2 * BATCH - 2)
            pe.wait_ge(F.t1, 1)
            pe_e_out(pe, 1)
            pe.wait_ge(T.o, 2 * BATCH)
            pe.wait_ge(T.res, 2 * BATCH - 1)
            pe_leave_turn(pe, 2 * BATCH - 1)
            pe.wait_ge(E.res, 2)
            pe_e_in(pe, 2)
            pe_leave_out(pe, 2 * BATCH - 1)
            pe_f_turn(pe, 1)
            pe.wait_ge(T.res, 2 * BATCH)
            pe_f_product(pe, 1)
            pe.wait_ge(E.kT, 3)
            pe_e_in(pe, 3)
            pe.wait_ge(E.kT, 4)
            pe_e_out(pe, 2)
            for b in range(2, 4):
                pe_f_turn(pe, b)
                pe.wait_ge(F.t1, b)
                pe_f_product(pe, b)
            pe_f_turn(pe, 4)
            pe.wait_ge(F.t1, 4)
            pe_f_product(pe, 4)
            pe.wait_ge(E.res, 3)
            pe_e_out(pe, 3)
            for b in range(5, BATCH):
                pe_f_turn(pe, b)
                pe.wait_ge(F.t1, b)
                pe_f_product(pe, b)

        def act_tail(act):
            act_leave(act, 2 * BATCH - 2)
            act_turned(act, 2 * BLOCKS - 1)
            act_leave(act, 2 * BATCH - 1)
            act_e_keys(act, 2)
            act_f(act, 1)
            act_e_states(act, 2)
            act_e_ratio(act, 2)
            act_e_keys(act, 3)
            act_e_states(act, 3)
            act_e_ratio(act, 3)
            for b in range(2, BATCH):
                act_f(act, b)

        def dve_tail(v):
            dve_attended(v, 2 * BATCH - 1, lambda: v.wait_ge(T.oTp, 2 * BATCH - 2))
            dve_leave(v, 2 * BATCH - 2)
            dve_e_residual(v, 1)
            dve_leave(v, 2 * BATCH - 1)
            dve_e_maxima(v, 2)
            dve_e_norm(v, BATCH - 2)
            dve_e_clamp(v, 2)
            dve_e_norm(v, BATCH - 1)
            dve_f_out(v, 1)
            dve_e_states(v, 2)
            dve_e_reciprocal(v, 2, 0)
            dve_e_maxima(v, 3)
            dve_e_reciprocal(v, 2, 1)
            dve_e_quotient(v, 2)
            dve_e_clamp(v, 3)
            dve_f_in(v, 2)
            dve_e_residual(v, 2)
            dve_e_states(v, 3)
            dve_f_in(v, 3)
            dve_f_out(v, 2)
            dve_e_reciprocal(v, 3, 0)
            dve_f_out(v, 3)
            dve_f_in(v, 4)
            dve_e_reciprocal(v, 3, 1)
            dve_e_quotient(v, 3)
            dve_f_in(v, 5)
            dve_f_out(v, 4)
            dve_e_residual(v, 3)
            dve_f_out(v, 5)
            for b in range(6, BATCH):
                v.wait_ge(zq.sem.step, 4 * (BATCH + b - 1))
                norm(v, 5, b, g_h[:, b % 2, :])
                dve_f_in(v, b)
            for b in range(6, BATCH):
                dve_f_out(v, b)
                v.wait_ge(F.res, b)
                f_residual(v, b)

        def pool_tail(g):
            pool_rstd(g, 4, BATCH - 2)
            pool_rstd(g, 4, BATCH - 1)
            pool_f_norm(g, 2)
            pool_e_kv(g, 2)
            pool_f_norm(g, 3)
            pool_e_rv(g, 2)
            f_residual(g, 1)
            pool_e_kv(g, 3)
            pool_e_rv(g, 3)
            pool_f_norm(g, 4)
            pool_f_norm(g, 5)
            f_residual(g, 2)
            f_residual(g, 3)
            f_residual(g, 4)
            for b in range(6, BATCH):
                pool_rstd(g, 5, b)
            f_residual(g, 5)


        @block.sync
        def _(sp):
            sp.dma_start(x_sb[:, 0:2, :], t["x"][0:2].rearrange("b p d -> p b d")).then_inc(ld.first, 16)
            sp.dma_start(ident[:, :], t["ident"]).then_inc(ld.first, 16)
            sp.dma_start(half_pow[:, :], t["half_pow"]).then_inc(ld.first, 16)
            sp.dma_start(init4[:, :], t["init"]).then_inc(ld.first, 16)
            sp.dma_start(w0[:, :, 0:3, :], t["w0"][:, :, 0:3, :]).then_inc(ld.w0, 16)
            for b in range(2, BATCH, 2):
                sp.dma_start(x_sb[:, b:b + 2, :], t["x"][b:b + 2].rearrange("b p d -> p b d")).then_inc(ld.x, 16)
            sp.dma_start(w0[:, :, 3:, :], t["w0"][:, :, 3:, :]).then_inc(ld.w1, 16)
            sp.dma_start(qw[:], t["qw"]).then_inc(ld.rows, 16)
            for dst, name in ((ones, "ones"), (beforef, "before"), (head_rows, "head_rows"),
                              (iota_e, "iota_e")):
                sp.dma_start(dst[:, :], t[name]).then_inc(ld.rows, 16)
            sp.dma_start(lower_g[:], t["lower_g"]).then_inc(ld.rows, 16)
            for i, name in enumerate(("bv", "bp", "wscale", "fbias")):
                sp.dma_start(rows[:, i, :], t[name].to_broadcast([P, D])).then_inc(ld.rows, 16)
            sp.dma_start(rbias[:, :], t["rbias"].to_broadcast([P, EXPERTS])).then_inc(ld.rows, 16)
            sp.dma_start(ctxT[:], t["ctxT"]).then_inc(ld.kv0, 16)
            sp.dma_start(wk0[:], t["wk0"]).then_inc(ld.kv0, 16)
            sp.dma_start(wv0[:], t["wv0"]).then_inc(ld.kv0, 16)
            sp.dma_start(bk0[:, :], t["bk0"]).then_inc(ld.kv0, 16)
            sp.dma_start(bq0[:, :], t["bq0"]).then_inc(ld.kv0, 16)
            for dst, name in ((gate, "gate"), (sup, "sup"), (sdown, "sdown")):
                sp.dma_start(dst[:], t[name]).then_inc(ld.moe, 16)
            for dst, name in ((wq1, "wq1"), (wk1, "wk1"), (wv1, "wv1"), (wo1, "wo1"), (wf8, "wf8")):
                sp.dma_start(dst[:], t[name]).then_inc(ld.l1, 16)
            for dst, name in ((decay, "decay"), (bonus, "bonus")):
                sp.dma_start(dst[:, :], t[name]).then_inc(ld.l1, 16)
            sp.wait_ge(cst.small, 1)
            for i in range(4):
                n = EXPERTS * CAP // 4
                sp.dma_start(xe_dram[i * n:(i + 1) * n, :].rearrange("(p r) d -> p (r d)", p=P),
                             zrow[:, :].unsqueeze(1).to_broadcast([P, n * D // P // 1024, 1024])
                             ).then_inc(C.zeroed, 16)
            for n in range(EXPERTS // GROUP):
                if n == 1:
                    sp.wait_ge(A.y, PAIRS)
                if n == 2:
                    sp.wait_ge(T.S, GROUPS * BATCH)
                if n == 3:
                    sp.wait_ge(C.grow, 2)
                sp.dma_start(e_w[n], t["we"][n * GROUP:(n + 1) * GROUP].rearrange("e p n -> p e n"))\
                  .then_inc(w_in[n], 16)
            sp.wait_ge(C.scat, 16 * BATCH * TOPK)
            for q in range(EXPERTS // 2):
                at = 2 * q % RING
                if q >= 4:
                    sp.wait_ge(C.xT, 2 * (q - 3))
                sp.dma_start(e_x[:, at:at + 2, :], xe_dram[2 * q * CAP:2 * (q + 1) * CAP, :]
                             .rearrange("(i p) d -> p i d", p=P)).then_inc(x_in[q % 4], 16)
            for b in range(BATCH):
                sp.wait_ge(F.res, b + 1)
                sp.dma_start(t["out"][b], g_o[:, b, :]).then_inc(F.out, 16)
            sp.wait_ge(F.out, 16 * BATCH)

        @block.gpsimd
        def _(g):
            g.wait_ge(ld.first, 64)
            for b in range(BATCH):
                pool_rstd(g, 0, b)
            pool_b_norm(g, 0)
            g.wait_ge(ld.rows, 16 * 11)
            for s in range(LAST):
                pool_b_step(g, s)
            pool_c_scatter(g, range(HALF, BATCH))
            for q in range(EXPERTS // 2):
                g.wait_ge(C.ye, 2 * (q + 1))
                at = 2 * q % RING
                g.dma_start(ye_dram[2 * q * CAP:2 * (q + 1) * CAP, :].rearrange("(i p) d -> p i d", p=P),
                            e_y[:, at:at + 2, :]).then_inc(e_out[q % 4], 16)
            pool_c_gather(g, 0)
            pool_c_gather(g, 1)
            pool_rstd(g, 3, 0)
            for s in range(LAST_D):
                if e_pair(s, 7) is not None:
                    for i in range(2):
                        pool_f_norm(g, 2 * e_pair(s, 7) + i)
                if s < BATCH:
                    key_copies(g, BATCH + s, 0, T.km0)
                if s + 1 < BATCH:
                    pool_rstd(g, 3, s + 1)
                if s + 2 < BATCH:
                    pool_c_gather(g, s + 2)
                if s >= 3:
                    pool_rstd(g, 4, s - 3)
                if e_pair(s, 5) is not None:
                    pool_e_kv(g, e_pair(s, 5))
                if e_pair(s, 5) is not None:
                    pool_e_rv(g, e_pair(s, 5))
                if e_pair(s, 8) is not None:
                    f_residual(g, 2 * e_pair(s, 8))
            pool_tail(g)

        @block.vector
        def _(v):
            v.memset(zrow[:, :], 0.0).then_inc(cst.small, 1)
            for b in range(3):
                v.memset(att.v1[:, b, :, HD], 1.0).then_inc(cst.vones, 1)
            v.wait_ge(ld.first, 64)
            for b in range(2):
                dve_stats(v, 0, b)
            v.tensor_scalar(init4[:, :], init4[:, :], 4.0, None, ALU.mult).then_inc(A.init4, 1)
            dve_a_norm(v, 0)
            v.wait_ge(ld.x, 16 * (PAIRS - 1))
            for b in range(2, BATCH):
                dve_stats(v, 0, b)
            dve_a_norm(v, 1)
            v.wait_ge(ld.rows, 16 * 11)
            qf = qw[:].rearrange("p w c n -> p (w c) n")
            v.tensor_reduce(qw_s[:].rearrange("p w c -> p (w c)"), qf, AX.X, ALU.max,
                            apply_absolute_value=True).then_inc(qs.scale, 1)
            v.wait_ge(qs.scale, 1)
            v.tensor_scalar(qw_s[:], qw_s[:], 1.0 / 127.0, 1e-8, ALU.mult, ALU.max).then_inc(qs.scale, 1)
            v.wait_ge(qs.scale, 2)
            v.reciprocal(qw_r[:], qw_s[:]).then_inc(qs.scale, 1)
            v.wait_ge(qs.scale, 3)
            for n in range(2 * KC):
                v.tensor_scalar(qw_i[:].rearrange("p w c n -> p (w c) n")[:, n, :], qf[:, n, :],
                                qw_r[:].rearrange("p w c -> p (w c)")[:, n:n + 1], ROUND,
                                ALU.mult, ALU.add).then_inc(qs.i, 1)
                v.tensor_scalar(qw_diag[:, n, :], ident[:, :], qw_s[:].rearrange("p w c -> p (w c)")[:, n:n + 1],
                                None, ALU.mult).then_inc(qs.diag, 1)
            v.wait_ge(qs.i, 2 * KC)
            v.tensor_scalar(qw_b[:], qw_i[:], -ROUND, None, ALU.add).then_inc(qs.b, 1)
            v.tensor_copy(identb[:, :], ident[:, :]).then_inc(cst.ident, 1)
            v.tensor_copy(onesb[:, :], ones[:, :]).then_inc(cst.ident, 1)
            v.tensor_copy(before[:, :], beforef[:, :]).then_inc(cst.ident, 1)
            v.wait_ge(A.init4, 1)
            for p in range(PAIRS):
                dve_a(v, p)
                if p + 2 < PAIRS:
                    dve_a_norm(v, p + 2)
                if p >= 1:
                    dve_a_residual(v, p - 1)
            dve_b_stats(v, 0)
            dve_b_prep(v, 0)
            dve_a_residual(v, PAIRS - 1)
            v.wait_ge(qs.evacrow, 1)
            v.wait_ge(ld.kv0, 80)
            v.wait_ge(cst.vones, 3)
            for s in range(LAST):
                dve_b_step(v, s)
            dve_c_scores(v, 1)
            dve_c_groups(v, 1)
            dve_c_choose(v, 1)
            dve_c_place(v, 1)
            dve_c_shared(v)
            for e in range(EXPERTS + 1):
                dve_x(v, e)
            v.wait_ge(ld.l1, 16 * 7)
            v.tensor_copy(wfb[:].rearrange("p k n -> p (k n)"),
                          wf8[:].rearrange("p k n -> p (k n)").bitcast(I8)).then_inc(cst.wfb, 1)
            dve_c_combine(v, 0)
            dve_stats(v, 3, 0)
            dve_d_prep(v, 0)
            dve_e_setup(v)
            for s in range(LAST_D):
                dve_d_step(v, s)
            dve_tail(v)

        @block.scalar
        def _(act):
            act.wait_ge(ld.first, 64)
            for p in range(PAIRS):
                act_a(act, p)
            act.wait_ge(qs.T, 1)
            act.copy(qwT[:].rearrange("p w k n -> p (w k n)"), bank[0][:, :].bitcast(BF16)).then_inc(qs.evacT, 1)
            act.wait_ge(qs.row, 1)
            act.copy(qw_row[:].rearrange("p w n -> p (w n)"), bank[1][:, :]).then_inc(qs.evacrow, 1)
            for s in range(LAST):
                act_b_step(act, s)
            for half in range(2):
                act_c_shared(act, half)
            for e in range(EXPERTS + 1):
                act_x(act, e)
            for s in range(LAST_D):
                act_d_step(act, s)
            act_tail(act)

        @block.tensor
        def _(pe):
            pe.wait_ge(ld.first, 64)
            pe_a_transpose(pe, 0)
            pe.wait_ge(ld.w0, 16)
            for p in range(PAIRS):
                pe_a_project(pe, p)
                if p + 1 < PAIRS:
                    pe_a_transpose(pe, p + 1)
                if p >= 1:
                    pe_a_down(pe, p - 1)
            pe.wait_ge(qs.b, 1)
            pe.wait_ge(cst.ident, 3)
            pe.wait_ge(A.hTs, PAIRS)
            for w in range(2):
                for o in range(KC):
                    for k in range(KC):
                        at = w * KC * D + k * D + o * P
                        mm = pe.transpose(bank[0][:, :].bitcast(BF16)[:, at:at + P],
                                          qw_b[:, w, o, k * P:(k + 1) * P], identb[:, :])
            mm.then_inc(qs.T, 1)
            pe.wait_ge(qs.diag, 2 * KC)
            pe.wait_ge(A.tf, PAIRS)
            for n in range(2 * KC):
                mm = pe.matmul(bank[1][:, n * P:(n + 1) * P], ones[:, :], qw_diag[:, n, :], start=True, stop=True)
            mm.then_inc(qs.row, 1)
            pe_a_down(pe, PAIRS - 1)
            pe.wait_ge(qs.evacT, 1)
            pe.wait_ge(qs.evacrow, 1)
            pe.wait_ge(A.res, PAIRS)
            pe.wait_ge(ld.kv0, 80)
            for s in range(LAST):
                pe_b_step(pe, s)
            pe_c_up(pe, 0)
            pe_c_pos(pe, 1)
            pe.wait_ge(C.placed, 2)
            pe_c_down(pe, range(HALF))
            pe_c_up(pe, 1)
            pe_c_down(pe, range(HALF, BATCH))
            pe.wait_ge(C.rel, 2 * SC)
            for e in range(EXPERTS + 2):
                if e < EXPERTS:
                    pe_x_transpose(pe, e)
                if 1 <= e <= EXPERTS:
                    pe_x_up(pe, e - 1)
                if e >= 2:
                    pe_x_down(pe, e - 2)
            pe.wait_ge(C.shy, PAIRS)
            pe.wait_ge(C.ye, EXPERTS)
            pe.wait_ge(C.hr, EXPERTS)
            pe.wait_ge(C.xTs, EXPERTS)
            pe.wait_ge(ld.l1, 16 * 7)
            for s in range(LAST_D):
                pe_d_step(pe, s)
            pe_tail(pe)


def _layouts(a):
    def chunked(w):
        w = np.asarray(w)
        return np.ascontiguousarray(w.reshape(w.shape[0] // P, P, w.shape[1]).transpose(1, 0, 2))

    def column(v):
        return np.ascontiguousarray(np.asarray(v).reshape(-1, P).T)

    l0 = [np.asarray(a[f"L0_attn_{n}"]) for n in L0_MATS]
    wkv, bkv = np.asarray(a["L0_xattn_wkv"]), np.asarray(a["L0_xattn_bkv"])
    qw = np.stack([np.asarray(a["L0_xattn_wq"]), np.asarray(a["L0_xattn_wp"])])
    up = np.asarray(a["L0_ffn_up_w"]).transpose(0, 2, 1).reshape(EXPERTS, KC, P, HID).transpose(0, 2, 1, 3)
    down = np.asarray(a["L0_ffn_down_w"]).transpose(0, 2, 1)
    row = lambda n: np.asarray(a[n]).reshape(1, -1)
    r = np.arange(P)

    def by_place(w):
        return w.reshape(KV_HEADS, HEADS // KV_HEADS, HD, D).transpose(1, 0, 2, 3).reshape(D, D)

    out = {
        "x": np.asarray(a["x"]),
        "w0": chunked(np.concatenate(l0, axis=1)).reshape(P, KC, len(L0_MATS), D),
        "init": column(a["L0_attn_init_state"]),
        "qw": qw.reshape(2, KC, P, D).transpose(2, 0, 1, 3),
        "ctxT": chunked(np.asarray(a["ctx_2048"]).reshape(TOK, D).T),
        "wk0": chunked(wkv[:D].T), "wv0": chunked(wkv[D:].T),
        "bk0": column(bkv[:D]), "bq0": column(a["L0_xattn_bq"]),
        "bv": bkv[D:].reshape(1, D), "bp": row("L0_xattn_bp"),
        "wscale": row("L1_ffn_w_scale"), "fbias": row("L1_ffn_bias"), "rbias": row("L0_ffn_bias_corr"),
        "gate": chunked(np.asarray(a["L0_ffn_gate_w"]).T),
        "sup": chunked(np.asarray(a["L0_ffn_shared_up_w"]).T),
        "sdown": chunked(np.asarray(a["L0_ffn_shared_down_w"]).T),
        "we": np.concatenate([up.reshape(EXPERTS, P, D), down], axis=2),
        "wq1": chunked(by_place(np.asarray(a["L1_attn_wq"])).T), "wk1": chunked(np.asarray(a["L1_attn_wk"]).T),
        "wv1": chunked(np.asarray(a["L1_attn_wv"]).T), "wo1": chunked(by_place(np.asarray(a["L1_attn_wo"]).T)),
        "wf8": chunked(np.asarray(a["L1_ffn_weight"]).T).view(np.int32),
        "decay": column(a["L1_xattn_w"]), "bonus": column(a["L1_xattn_u"]),
        "ident": np.eye(P, dtype=np.float32), "ones": np.ones((P, P), np.float32),
        "before": (r[:, None] < r[None, :]).astype(np.float32),
        "head_rows": (r[:, None] // HD == np.arange(HEADS // KC)[None, :]).astype(np.float32),
        "half_pow": np.full((P, BATCH), -0.5, np.float32),
        "iota_e": np.tile(np.arange(EXPERTS, dtype=np.float32), (P, 1)),
        "lower_g": np.tile(np.tril(np.ones((EGROUPS, EGROUPS), np.float32), -1), (P, 1, 1)),
    }
    return {k: np.ascontiguousarray(v) for k, v in out.items()}


def kernel(**inputs):
    import concourse.bacc as bacc
    from concourse.bass_utils import run_bass_kernel_spmd

    arrays = _layouts(inputs)
    nc = bacc.Bacc("TRN2", target_bir_lowering=False, num_devices=1)
    t = {n: nc.dram_tensor(f"in_{n}", a.shape, mybir.dt.from_np(a.dtype), kind="ExternalInput").ap()
         for n, a in arrays.items()}
    t["out"] = nc.dram_tensor("out", (BATCH, SEQ, D), F32, kind="ExternalOutput").ap()
    build(nc, t)
    result = run_bass_kernel_spmd(nc, [{f"in_{n}": a for n, a in arrays.items()}], core_ids=[0])
    return result.results[0]["out"]
```
